# Optimizing a Trainium2 kernel written in Bass

```python
import numpy as np
import jax
import jax.numpy as jnp

def _softmax(x, axis=-1):
    return jax.nn.softmax(x, axis=axis)

def _gelu(x):
    return jax.nn.gelu(x, approximate=True)

def _silu(x):
    return jax.nn.silu(x)

def _sigmoid(x):
    return jax.nn.sigmoid(x)

def _layernorm(x, axis=-1, eps=1e-05):
    m = jnp.mean(x, axis=axis, keepdims=True)
    v = jnp.var(x, axis=axis, keepdims=True)
    return (x - m) / jnp.sqrt(v + eps)

def _scatter_add(tgt, idx, src, axis=0):
    return tgt.at[idx].add(src)

def _segment_sum(src, seg, n):
    return jax.ops.segment_sum(src, seg, n)
kernel_name = 'mk_adaln_d2_jaxref_r8_ba14d4'

def setup_inputs(seed: int=0):
    np.random.seed(seed)
    _w = jnp.asarray

    def _L0_attn_setup():
        import jax, jax.numpy as jnp
        import numpy as np
        B, T, C, H = (4, 256, 128, 8)
        D = C // H

        def _rope_tables(t, d, base=10000.0):
            inv = 1.0 / base ** (jnp.arange(0, d, 2, dtype=jnp.float32) / d)
            freqs = jnp.outer(jnp.arange(t, dtype=jnp.float32), inv)
            cos = jnp.concatenate([jnp.cos(freqs)] * 2, axis=-1)
            sin = jnp.concatenate([jnp.sin(freqs)] * 2, axis=-1)
            return (cos, sin)

        def _apply_rope(x, cos, sin):
            d2 = x.shape[-1] // 2
            x1, x2 = (x[..., :d2], x[..., d2:])
            rot = jnp.concatenate([-x2, x1], axis=-1)
            return x * cos + rot * sin
        key = jax.random.key(seed)
        ks = jax.random.split(key, 8)
        x = jax.random.normal(ks[0], (B, T, C), jnp.float32)
        w = lambda k: jax.random.normal(k, (C, C), jnp.float32) * 0.02
        signs = np.array([[1 if i >> b & 1 else -1 for b in range(3)] for i in range(8)], np.float32)
        head_dirs = jnp.asarray(signs / np.sqrt(3.0))
        return {'x': x, 'Wq': w(ks[1]), 'Wk': w(ks[2]), 'Wv': w(ks[3]), 'Wo': w(ks[4]), 'ln_g': jnp.ones((C,), jnp.float32), 'ln_b': jnp.zeros((C,), jnp.float32), 'head_scales': jax.random.normal(ks[5], (H,), jnp.float32) * 0.1, 'head_dirs': head_dirs}
    _L0_attn_in = _L0_attn_setup()

    def _L0_ffn_setup():
        import jax, jax.numpy as jnp
        import numpy as np
        D = 128
        I = 64
        E = 32
        K = 4
        T = 2 * 256
        C = 2 * T * K // E
        key = jax.random.key(seed)
        ks = jax.random.split(key, 9)
        bf = jnp.bfloat16
        std = 0.02
        x = jax.random.normal(ks[0], (2, 256, D), dtype=jnp.float32).astype(bf)
        gate_w = (std * jax.random.normal(ks[1], (E, D), dtype=jnp.float32)).astype(bf)
        bias = jnp.zeros((E,), jnp.float32)
        W1 = (std * jax.random.normal(ks[2], (E, D, I), dtype=jnp.float32)).astype(bf)
        W3 = (std * jax.random.normal(ks[3], (E, D, I), dtype=jnp.float32)).astype(bf)
        W2 = (std * jax.random.normal(ks[4], (E, I, D), dtype=jnp.float32)).astype(bf)
        sw1 = (std * jax.random.normal(ks[5], (I, D), dtype=jnp.float32)).astype(bf)
        sw3 = (std * jax.random.normal(ks[6], (I, D), dtype=jnp.float32)).astype(bf)
        sw2 = (std * jax.random.normal(ks[7], (D, I), dtype=jnp.float32)).astype(bf)
        return {'x': x, 'gate_w': gate_w, 'bias': bias, 'W1': W1, 'W3': W3, 'W2': W2, 'sw1': sw1, 'sw3': sw3, 'sw2': sw2}
    _L0_ffn_in = _L0_ffn_setup()
    _L0_c = _w((lambda *s: np.random.randn(*s).astype(np.float32) * 0.05)(32, 128))
    _L0_wmod = _w((lambda *s: np.random.randn(*s).astype(np.float32) * 0.05)(128, 6 * 128) * 128 ** (-0.5))

    def _L1_attn_setup():
        import jax, jax.numpy as jnp
        from jax import lax
        import numpy as np
        CHUNK = 64

        def short_conv(x, w):
            L = x.shape[1]
            K = w.shape[1]
            xp = jnp.pad(x, ((0, 0), (K - 1, 0), (0, 0)))
            return sum((xp[:, j:j + L, :] * w[:, j] for j in range(K)))

        def o2b_weighted_delta_rule(k, q, v, b):
            B, L, H, D = k.shape
            C = CHUNK
            Nc = L // C

            def to_chunks(t):
                return t.transpose(0, 2, 1, 3).reshape(B, H, Nc, C, D).transpose(2, 0, 1, 3, 4)
            Kc, Qc, Vc, Bc = map(to_chunks, (k, q, v, b))
            eyeC = jnp.eye(C, dtype=jnp.float32)
            W0 = jnp.zeros((B, H, D, D), jnp.float32)
            Cf = float(C)

            def step(carry, xs):
                W_t, W_avg = carry
                i, Ki, Qi, Vi, Bi = xs
                KiT = jnp.swapaxes(Ki, -1, -2)
                T = jnp.tril(Bi @ KiT, k=-1)
                inv = jnp.linalg.inv(eyeC + T)
                Ui = inv @ (Vi - Bi @ W_t)
                W_new = W_t + KiT @ Ui
                ts = (i * C).astype(jnp.float32)
                idx = jnp.arange(1, C + 1, dtype=jnp.float32) + ts
                cs = jnp.cumsum(idx)
                weighted_idx = idx + idx.sum() - cs
                w_i = (weighted_idx / ((1 + ts + Cf) * (ts + Cf) / 2))[:, None]
                coef1 = ts / (ts + Cf) * ((1 + ts) / (1 + ts + Cf))
                coef2 = Cf / (ts + Cf) * ((ts * 2 + 1 + Cf) / (1 + ts + Cf))
                W_avg_new = coef1 * W_avg + coef2 * W_t + KiT @ (Ui * w_i)
                tri0 = (1 + ts) * ts / 2
                a = (tri0 / (tri0 + cs))[:, None]
                c = 1.0 - a
                r = cs[:, None]
                j_idx = (cs - idx)[None, :]
                T_mat = jnp.where(r >= j_idx, (r - j_idx) / (tri0 + r), 0.0)
                O_i = Qi @ W_avg * a + Qi @ W_t * c + T_mat * (Qi @ KiT) @ Ui
                return ((W_new, W_avg_new), O_i)
            (_, _), O = lax.scan(step, (W0, W0), (jnp.arange(Nc), Kc, Qc, Vc, Bc))
            return O.transpose(1, 2, 0, 3, 4).reshape(B, H, L, D).transpose(0, 2, 1, 3)
        key = jax.random.key(seed)
        ks = jax.random.split(key, 9)
        B, L, Dm, H = (4, 256, 128, 16)
        Dh, K = (Dm // H, 4)
        s = 0.02
        return {'x': jax.random.normal(ks[0], (B, L, Dm), jnp.float32), 'Wk': s * jax.random.normal(ks[1], (Dm, Dm), jnp.float32), 'bk': jnp.zeros((Dm,), jnp.float32), 'Wq': s * jax.random.normal(ks[2], (Dm, Dm), jnp.float32), 'bq': jnp.zeros((Dm,), jnp.float32), 'Wv': s * jax.random.normal(ks[3], (Dm, Dm), jnp.float32), 'bv': jnp.zeros((Dm,), jnp.float32), 'Wbeta': s * jax.random.normal(ks[4], (H, Dm), jnp.float32), 'bbeta': jnp.zeros((H,), jnp.float32), 'conv_k': 0.1 * jax.random.normal(ks[5], (Dm, K), jnp.float32), 'conv_q': 0.1 * jax.random.normal(ks[6], (Dm, K), jnp.float32), 'conv_v': 0.1 * jax.random.normal(ks[7], (Dm, K), jnp.float32), 'rms_w': jnp.ones((Dh,), jnp.float32), 'Wout': s * jax.random.normal(ks[8], (Dm, Dm), jnp.float32), 'bout': jnp.zeros((Dm,), jnp.float32)}
    _L1_attn_in = _L1_attn_setup()

    def _L1_ffn_setup():
        import jax, jax.numpy as jnp
        import numpy as np
        EPS = 1e-06
        TOP_K = 2

        def rms_norm(x, scale, eps=EPS):
            xf = x.astype(jnp.float32)
            mean_sq = jnp.mean(xf * xf, axis=-1, keepdims=True)
            return (xf * (scale.astype(jnp.float32) * jax.lax.rsqrt(mean_sq + eps))).astype(x.dtype)
        key = jax.random.key(seed)
        k0, k1, k2, k3 = jax.random.split(key, 4)
        B, S, D, H, E = (2, 256, 128, 352, 8)
        x = jax.random.normal(k0, (B, S, D), dtype=jnp.float32)
        norm_scale = jnp.ones((D,), dtype=jnp.float32)
        w_router = jax.random.normal(k1, (E, D), dtype=jnp.float32) * 0.02
        w_up = jax.random.normal(k2, (E, 2 * H, D), dtype=jnp.float32) * 0.02
        w_down = jax.random.normal(k3, (E, D, H), dtype=jnp.float32) * 0.02
        return {'x': x, 'norm_scale': norm_scale, 'w_router': w_router, 'w_up': w_up, 'w_down': w_down}
    _L1_ffn_in = _L1_ffn_setup()
    _L1_c = _w((lambda *s: np.random.randn(*s).astype(np.float32) * 0.05)(32, 128))
    _L1_wmod = _w((lambda *s: np.random.randn(*s).astype(np.float32) * 0.05)(128, 6 * 128) * 128 ** (-0.5))
    _d = {'L0_attn_x': _L0_attn_in['x'], 'L0_attn_Wq': _L0_attn_in['Wq'], 'L0_attn_Wk': _L0_attn_in['Wk'], 'L0_attn_Wv': _L0_attn_in['Wv'], 'L0_attn_Wo': _L0_attn_in['Wo'], 'L0_attn_ln_g': _L0_attn_in['ln_g'], 'L0_attn_ln_b': _L0_attn_in['ln_b'], 'L0_attn_head_scales': _L0_attn_in['head_scales'], 'L0_attn_head_dirs': _L0_attn_in['head_dirs'], 'L0_ffn_gate_w': _L0_ffn_in['gate_w'], 'L0_ffn_bias': _L0_ffn_in['bias'], 'L0_ffn_W1': _L0_ffn_in['W1'], 'L0_ffn_W3': _L0_ffn_in['W3'], 'L0_ffn_W2': _L0_ffn_in['W2'], 'L0_ffn_sw1': _L0_ffn_in['sw1'], 'L0_ffn_sw3': _L0_ffn_in['sw3'], 'L0_ffn_sw2': _L0_ffn_in['sw2'], 'L0_c': _L0_c, 'L0_wmod': _L0_wmod, 'L1_attn_Wk': _L1_attn_in['Wk'], 'L1_attn_bk': _L1_attn_in['bk'], 'L1_attn_Wq': _L1_attn_in['Wq'], 'L1_attn_bq': _L1_attn_in['bq'], 'L1_attn_Wv': _L1_attn_in['Wv'], 'L1_attn_bv': _L1_attn_in['bv'], 'L1_attn_Wbeta': _L1_attn_in['Wbeta'], 'L1_attn_bbeta': _L1_attn_in['bbeta'], 'L1_attn_conv_k': _L1_attn_in['conv_k'], 'L1_attn_conv_q': _L1_attn_in['conv_q'], 'L1_attn_conv_v': _L1_attn_in['conv_v'], 'L1_attn_rms_w': _L1_attn_in['rms_w'], 'L1_attn_Wout': _L1_attn_in['Wout'], 'L1_attn_bout': _L1_attn_in['bout'], 'L1_ffn_norm_scale': _L1_ffn_in['norm_scale'], 'L1_ffn_w_router': _L1_ffn_in['w_router'], 'L1_ffn_w_up': _L1_ffn_in['w_up'], 'L1_ffn_w_down': _L1_ffn_in['w_down'], 'L1_c': _L1_c, 'L1_wmod': _L1_wmod}
    _x0 = _d['L0_attn_x']
    _d['L0_attn_x'] = jax.random.normal(jax.random.fold_in(jax.random.key(seed), 1), (32, 256, 128), dtype=_x0.dtype)
    del _x0
    return _d

def reference(L0_attn_x, L0_attn_Wq, L0_attn_Wk, L0_attn_Wv, L0_attn_Wo, L0_attn_ln_g, L0_attn_ln_b, L0_attn_head_scales, L0_attn_head_dirs, L0_ffn_gate_w, L0_ffn_bias, L0_ffn_W1, L0_ffn_W3, L0_ffn_W2, L0_ffn_sw1, L0_ffn_sw3, L0_ffn_sw2, L0_c, L0_wmod, L1_attn_Wk, L1_attn_bk, L1_attn_Wq, L1_attn_bq, L1_attn_Wv, L1_attn_bv, L1_attn_Wbeta, L1_attn_bbeta, L1_attn_conv_k, L1_attn_conv_q, L1_attn_conv_v, L1_attn_rms_w, L1_attn_Wout, L1_attn_bout, L1_ffn_norm_scale, L1_ffn_w_router, L1_ffn_w_up, L1_ffn_w_down, L1_c, L1_wmod):

    def _L0_attn_ref(x, Wq, Wk, Wv, Wo, ln_g, ln_b, head_scales, head_dirs):
        import jax, jax.numpy as jnp
        import numpy as np
        B, T, C, H = (4, 256, 128, 8)
        D = C // H

        def _rope_tables(t, d, base=10000.0):
            inv = 1.0 / base ** (jnp.arange(0, d, 2, dtype=jnp.float32) / d)
            freqs = jnp.outer(jnp.arange(t, dtype=jnp.float32), inv)
            cos = jnp.concatenate([jnp.cos(freqs)] * 2, axis=-1)
            sin = jnp.concatenate([jnp.sin(freqs)] * 2, axis=-1)
            return (cos, sin)

        def _apply_rope(x, cos, sin):
            d2 = x.shape[-1] // 2
            x1, x2 = (x[..., :d2], x[..., d2:])
            rot = jnp.concatenate([-x2, x1], axis=-1)
            return x * cos + rot * sin
        b, t, c = x.shape
        h = head_dirs.shape[0]
        d = c // h
        scale = 1.0 / jnp.sqrt(jnp.asarray(d, x.dtype))
        mu = jnp.mean(x, axis=-1, keepdims=True)
        var = jnp.mean((x - mu) ** 2, axis=-1, keepdims=True)
        xn = (x - mu) * jax.lax.rsqrt(var + 1e-05) * ln_g + ln_b
        q = (xn @ Wq.T).reshape(b, t, h, d).transpose(0, 2, 1, 3)
        k = (xn @ Wk.T).reshape(b, t, h, d).transpose(0, 2, 1, 3)
        v = (xn @ Wv.T).reshape(b, t, h, d).transpose(0, 2, 1, 3)
        cos, sin = _rope_tables(t, d)
        q = _apply_rope(q, cos, sin)
        k = _apply_rope(k, cos, sin)
        causal = jnp.tril(jnp.ones((t, t), bool))
        scores = jnp.einsum('bhqd,bhkd->bhqk', q, k) * scale
        scores = jnp.where(causal, scores, -jnp.inf)
        attn = jax.nn.softmax(scores, axis=-1)
        out = jnp.einsum('bhqk,bhkd->bhqd', attn, v)
        qp = jnp.einsum('bhtd,hd->bht', q[..., :3], head_dirs)
        kp = jnp.einsum('bhtd,hd->bht', k[..., :3], head_dirs)
        geo = qp[..., :, None] * kp[..., None, :]
        geo = jnp.where(causal, geo, -jnp.inf)
        geo_attn = jax.nn.softmax(geo, axis=-1)
        geo_out = jnp.einsum('bhqk,bhkd->bhqd', geo_attn, v)
        out = out + head_scales[None, :, None, None] * jax.lax.stop_gradient(geo_out - out)
        out = out.transpose(0, 2, 1, 3).reshape(b, t, c) @ Wo.T
        return x + out

    def _L0_ffn_ref(x, gate_w, bias, W1, W3, W2, sw1, sw3, sw2):
        import jax, jax.numpy as jnp
        import numpy as np
        D = 128
        I = 64
        E = 32
        K = 4
        T = 2 * 256
        C = 2 * T * K // E
        X = x.reshape(-1, D)
        logits = (X @ gate_w.T).astype(jnp.float32)
        scores = jax.nn.sigmoid(logits)
        _, idx = jax.lax.top_k(scores + bias[None, :], K)
        w = jnp.take_along_axis(scores, idx, axis=-1)
        w = w / jnp.clip(jnp.sum(w, axis=-1, keepdims=True), 1e-12, None)
        w = w.astype(x.dtype)
        eid = idx.reshape(-1)
        onehot = (eid[:, None] == jnp.arange(E)[None, :]).astype(jnp.int32)
        pos = jnp.take_along_axis(jnp.cumsum(onehot, axis=0) - 1, eid[:, None], axis=1)[:, 0]
        valid = pos < C
        posc = jnp.minimum(pos, C - 1)
        Xrep = jnp.repeat(X, K, axis=0)
        xe = jnp.zeros((E, C, D), x.dtype).at[eid, posc].add(jnp.where(valid[:, None], Xrep, jnp.zeros((), x.dtype)))
        h = jax.nn.silu(jnp.einsum('ecd,edi->eci', xe, W1)) * jnp.einsum('ecd,edi->eci', xe, W3)
        ye = jnp.einsum('eci,eid->ecd', h, W2)
        gflat = jnp.where(valid, w.reshape(-1), jnp.zeros((), x.dtype))
        yrows = ye[eid, posc] * gflat[:, None]
        out = yrows.reshape(-1, K, D).sum(axis=1)
        out = out + jax.nn.silu(X @ sw1.T) * (X @ sw3.T) @ sw2.T
        return out.reshape(x.shape)

    def _L1_attn_ref(x, Wk, bk, Wq, bq, Wv, bv, Wbeta, bbeta, conv_k, conv_q, conv_v, rms_w, Wout, bout):
        import jax, jax.numpy as jnp
        from jax import lax
        import numpy as np
        CHUNK = 64

        def short_conv(x, w):
            L = x.shape[1]
            K = w.shape[1]
            xp = jnp.pad(x, ((0, 0), (K - 1, 0), (0, 0)))
            return sum((xp[:, j:j + L, :] * w[:, j] for j in range(K)))

        def o2b_weighted_delta_rule(k, q, v, b):
            B, L, H, D = k.shape
            C = CHUNK
            Nc = L // C

            def to_chunks(t):
                return t.transpose(0, 2, 1, 3).reshape(B, H, Nc, C, D).transpose(2, 0, 1, 3, 4)
            Kc, Qc, Vc, Bc = map(to_chunks, (k, q, v, b))
            eyeC = jnp.eye(C, dtype=jnp.float32)
            W0 = jnp.zeros((B, H, D, D), jnp.float32)
            Cf = float(C)

            def step(carry, xs):
                W_t, W_avg = carry
                i, Ki, Qi, Vi, Bi = xs
                KiT = jnp.swapaxes(Ki, -1, -2)
                T = jnp.tril(Bi @ KiT, k=-1)
                inv = jnp.linalg.inv(eyeC + T)
                Ui = inv @ (Vi - Bi @ W_t)
                W_new = W_t + KiT @ Ui
                ts = (i * C).astype(jnp.float32)
                idx = jnp.arange(1, C + 1, dtype=jnp.float32) + ts
                cs = jnp.cumsum(idx)
                weighted_idx = idx + idx.sum() - cs
                w_i = (weighted_idx / ((1 + ts + Cf) * (ts + Cf) / 2))[:, None]
                coef1 = ts / (ts + Cf) * ((1 + ts) / (1 + ts + Cf))
                coef2 = Cf / (ts + Cf) * ((ts * 2 + 1 + Cf) / (1 + ts + Cf))
                W_avg_new = coef1 * W_avg + coef2 * W_t + KiT @ (Ui * w_i)
                tri0 = (1 + ts) * ts / 2
                a = (tri0 / (tri0 + cs))[:, None]
                c = 1.0 - a
                r = cs[:, None]
                j_idx = (cs - idx)[None, :]
                T_mat = jnp.where(r >= j_idx, (r - j_idx) / (tri0 + r), 0.0)
                O_i = Qi @ W_avg * a + Qi @ W_t * c + T_mat * (Qi @ KiT) @ Ui
                return ((W_new, W_avg_new), O_i)
            (_, _), O = lax.scan(step, (W0, W0), (jnp.arange(Nc), Kc, Qc, Vc, Bc))
            return O.transpose(1, 2, 0, 3, 4).reshape(B, H, L, D).transpose(0, 2, 1, 3)
        B, L, Dm = x.shape
        H = Wbeta.shape[0]
        Dh = Dm // H
        k = short_conv(x @ Wk.T + bk, conv_k)
        q = short_conv(x @ Wq.T + bq, conv_q)
        v = short_conv(x @ Wv.T + bv, conv_v)
        beta = jax.nn.sigmoid(x @ Wbeta.T + bbeta)
        k = k.reshape(B, L, H, Dh)
        q = q.reshape(B, L, H, Dh)
        v = jax.nn.silu(v.reshape(B, L, H, Dh))
        knorm = jnp.linalg.norm(k, axis=-1, keepdims=True)
        qnorm = jnp.linalg.norm(q, axis=-1, keepdims=True)
        k = k / (knorm + 1e-06)
        q = q / (qnorm + 1e-06)
        eta = beta
        b = eta[..., None] * k
        v = eta[..., None] * v
        o = o2b_weighted_delta_rule(k, q, v, b)
        o = o * jax.lax.rsqrt(jnp.mean(o * o, axis=-1, keepdims=True) + 1e-06) * rms_w
        o = o.reshape(B, L, Dm)
        return o @ Wout.T + bout

    def _L1_ffn_ref(x, norm_scale, w_router, w_up, w_down):
        import jax, jax.numpy as jnp
        import numpy as np
        EPS = 1e-06
        TOP_K = 2

        def rms_norm(x, scale, eps=EPS):
            xf = x.astype(jnp.float32)
            mean_sq = jnp.mean(xf * xf, axis=-1, keepdims=True)
            return (xf * (scale.astype(jnp.float32) * jax.lax.rsqrt(mean_sq + eps))).astype(x.dtype)
        skip = x
        xn = rms_norm(x, norm_scale)
        scores = jnp.einsum('bsd,ed->bse', xn, w_router)
        _, ids = jax.lax.top_k(scores, TOP_K)
        probs = jax.nn.softmax(scores, axis=-1)
        c = jnp.take_along_axis(probs, ids, axis=-1)
        h = jnp.einsum('bsd,ehd->bseh', xn, w_up)
        val, gate = jnp.split(h, 2, axis=-1)
        h = val * jax.nn.silu(gate)
        y = jnp.einsum('bseh,edh->bsed', h, w_down)
        yk = jnp.take_along_axis(y, ids[..., None], axis=2)
        out = jnp.sum(yk * c[..., None], axis=2)
        return out + skip
    x = L0_attn_x
    mod = (_silu(L0_c) @ L0_wmod).reshape(L0_c.shape[0], 6, 1, -1)
    sa, ca, ga, sb, cb, gb = (mod[:, 0], mod[:, 1], mod[:, 2], mod[:, 3], mod[:, 4], mod[:, 5])
    ga = (2 * (ga >= 0) - 1) * jnp.maximum(jnp.abs(ga), 0.25)
    gb = (2 * (gb >= 0) - 1) * jnp.maximum(jnp.abs(gb), 0.25)
    h = _layernorm(x, axis=-1) * (1 + ca) + sa
    x = x + ga * _L0_attn_ref(h, L0_attn_Wq, L0_attn_Wk, L0_attn_Wv, L0_attn_Wo, L0_attn_ln_g, L0_attn_ln_b, L0_attn_head_scales, L0_attn_head_dirs)
    h = _layernorm(x, axis=-1) * (1 + cb) + sb
    x = x + gb * _L0_ffn_ref(h, L0_ffn_gate_w, L0_ffn_bias, L0_ffn_W1, L0_ffn_W3, L0_ffn_W2, L0_ffn_sw1, L0_ffn_sw3, L0_ffn_sw2)
    mod = (_silu(L1_c) @ L1_wmod).reshape(L1_c.shape[0], 6, 1, -1)
    sa, ca, ga, sb, cb, gb = (mod[:, 0], mod[:, 1], mod[:, 2], mod[:, 3], mod[:, 4], mod[:, 5])
    ga = (2 * (ga >= 0) - 1) * jnp.maximum(jnp.abs(ga), 0.25)
    gb = (2 * (gb >= 0) - 1) * jnp.maximum(jnp.abs(gb), 0.25)
    h = _layernorm(x, axis=-1) * (1 + ca) + sa
    x = x + ga * _L1_attn_ref(h, L1_attn_Wk, L1_attn_bk, L1_attn_Wq, L1_attn_bq, L1_attn_Wv, L1_attn_bv, L1_attn_Wbeta, L1_attn_bbeta, L1_attn_conv_k, L1_attn_conv_q, L1_attn_conv_v, L1_attn_rms_w, L1_attn_Wout, L1_attn_bout)
    h = _layernorm(x, axis=-1) * (1 + cb) + sb
    x = x + gb * _L1_ffn_ref(h, L1_ffn_norm_scale, L1_ffn_w_router, L1_ffn_w_up, L1_ffn_w_down)
    return x

_drawn_inputs = setup_inputs


def setup_inputs(seed=0):
    import zlib

    import numpy as np

    out = dict(_drawn_inputs(seed))
    spreads = {'L0_attn_ln_g': (1.0, 0.6),
     'L0_attn_ln_b': (0.0, 0.8),
     'L0_ffn_bias': (0.0, 0.8),
     'L1_attn_bk': (0.0, 0.1),
     'L1_attn_bq': (0.0, 0.292),
     'L1_attn_bv': (0.0, 0.1),
     'L1_attn_bbeta': (0.0, 2.0),
     'L1_attn_rms_w': (1.0, 0.6),
     'L1_attn_bout': (0.0, 0.302),
     'L1_ffn_norm_scale': (1.0, 0.6)}
    factors = {'L0_attn_Wq': 8.0,
     'L0_attn_Wk': 8.0,
     'L0_attn_Wv': 8.0,
     'L0_attn_Wo': 8.0,
     'L0_attn_head_scales': 8.0,
     'L0_attn_head_dirs': 8.0,
     'L0_ffn_gate_w': 8.0,
     'L0_ffn_W1': 8.0,
     'L0_ffn_W3': 8.0,
     'L0_ffn_W2': 8.0,
     'L0_ffn_sw1': 8.0,
     'L0_ffn_sw3': 8.0,
     'L0_ffn_sw2': 8.0,
     'L1_attn_Wbeta': 8.0,
     'L1_ffn_w_router': 8.0,
     'L1_ffn_w_up': 8.0,
     'L1_ffn_w_down': 8.0}
    for name, (base, spread) in spreads.items():
        noise = np.random.default_rng([zlib.crc32(name.encode()), seed]).standard_normal(out[name].shape)
        drawn = base * np.exp(spread * noise) if base else spread * noise
        out[name] = jnp.asarray(drawn.astype(out[name].dtype))
    for name, factor in factors.items():
        out[name] = (out[name] * factor).astype(out[name].dtype)
    return out
```

```python
from contextlib import ExitStack

import numpy as np

import concourse.bass as bass
from concourse import mybir

F32 = mybir.dt.float32
BF16 = mybir.dt.bfloat16
U32 = mybir.dt.uint32
ALU = mybir.AluOpType
ACT = mybir.ActivationFunctionType
AX = mybir.AxisListType

B, T, D = 32, 256, 128
N = B * T
LN_EPS = 1e-5
RMS_EPS = 1e-6
CH = 512
NCH = N // CH
BPC = CH // T

H0, DH0 = 8, 16
GROUPS, PER = 2, 4
SLOT = 32
KB = T // SLOT
NEG = -1e30
SCALE0 = 1.0 / DH0 ** 0.5
GEO_D = 3
E0, I0, K0, CAP = 32, 64, 4, 2 * 512 * 4 // 32
H1, DH1, CONV = 16, 8, 4
E1, HID, K1 = 8, 352, 2
HC = [(0, 128), (128, 128), (256, 96)]


def constants():
    p = np.arange(128)
    quad, slot = p // SLOT, p % SLOT
    f = {}
    f["ident"] = np.eye(128)
    f["center"] = np.eye(128) - 1.0 / 128
    f["mean"] = np.full((128, 128), 1.0 / 128)
    half = DH0 // 2
    inv = (1.0 / np.float32(10000.0) ** (np.arange(0, DH0, 2, dtype=np.float32) / np.float32(DH0))).astype(np.float32)
    freqs = np.outer(np.arange(T, dtype=np.float32), inv).astype(np.float32).astype(np.float64)
    cos, sin = np.zeros((128, T)), np.zeros((128, T))
    for i in range(128):
        if slot[i] < DH0:
            cos[i] = np.cos(freqs[:, slot[i] % half])
            sin[i] = np.sin(freqs[:, slot[i] % half]) * (-1 if slot[i] < half else 1)
    f["cos"], f["sin"] = cos, sin
    f["sum_col"] = (slot == DH0)[:, None]
    f["max_any"] = ((slot >= DH0) & (slot < DH0 + KB))[:, None]
    f["max_rows"] = slot[:, None] == DH0 + np.arange(KB)[None, :]
    f["geo_kp"] = ((slot == 0) | (slot == 2))[:, None]
    f["geo_one"] = ((slot == 1) | (slot == 3))[:, None]
    f["geo_q"] = np.stack([slot == 2 * g for g in range(GROUPS)], 1)
    f["geo_m"] = np.stack([-1.0 * (slot == 2 * g + 1) for g in range(GROUPS)], 1)
    h = p // DH1
    f["same_head"] = h[:, None] == h[None, :]
    for d in range(DH1):
        f[f"pick{d}"] = (h[:, None] == h[None, :]) & (p % DH1 == d)[:, None]
    t = np.arange(1, T + 1, dtype=np.float64)
    f["step"] = np.broadcast_to(t, (128, T))
    at = SLOT * np.arange(KB)[None, :] + slot[:, None] + 1.0
    f["inv_weight_t"] = 1.0 / (at * (at + 1) / 2)
    f["before"] = p[:, None] < p[None, :]
    f["ones"] = np.ones((128, 128))
    f["iota"] = np.broadcast_to(p.astype(np.float64), (128, 128))
    f["row_no"] = p[:, None]
    f["tile_no"] = np.broadcast_to(np.arange(N // 128, dtype=np.float64), (128, N // 128))
    f["past"] = N + p[:, None]
    f = {k: np.ascontiguousarray(v, dtype=np.float32) for k, v in f.items()}
    b = {}
    b["ident_bf"] = np.eye(128)
    late = slot[:, None] < np.arange(2 * SLOT)[None, :]
    b["mask_max"] = np.where(late, NEG, 0.0)
    b["mask_key"] = np.where(slot[:, None] > np.arange(SLOT)[None, :], NEG, 0.0)
    b = {k: np.ascontiguousarray(v, dtype=np.float32) for k, v in b.items()}
    return f, b


def table_columns(tables):
    at, out = 0, {}
    for k, v in tables.items():
        out[k] = (at, at + v.shape[1])
        at += v.shape[1]
    return out, at


class Named(dict):

    def __getattr__(self, name):
        return self[name]


class Shared:
    pass


class Scope(ExitStack):

    def __init__(self, nc, name):
        super().__init__()
        self.nc, self.name, self.taken = nc, name, []

    def sb(self, name, shape, dt=F32):
        return self.enter_context(self.nc.sbuf_tensor(f"{self.name}_{name}", shape, dt))

    def ps(self, name, shape=(128, 512), dt=F32):
        return self.enter_context(self.nc.psum_tensor(f"{self.name}_{name}", list(shape), dt))

    def sems(self, names, tag=""):
        made = {n: self.nc.alloc_semaphore(f"{self.name}_{n}{tag}") for n in names.split()}
        self.taken += made.values()
        return Named(made)

    def __exit__(self, *exc):
        super().__exit__(*exc)
        if exc[0] is None:
            self.nc.clear_and_free_semaphores(self.taken)
            self.nc.all_engine_barrier()

    def block(self):
        return self.enter_context(self.nc.Block())


def setup_phase(nc, dram, g):
    with Scope(nc, "setup") as s:
        c_sb = s.sb("c", [128, 2, B])
        silu = s.sb("silu", [128, 2, B])
        wmod = s.sb("wmod", [128, 2, 6 * 128])
        absv = s.sb("absv", [128, 2, 2, B])
        sign = s.sb("sign", [128, 2, 2, B])
        tab_f = s.sb("tab_f", g.tab_bf.shape)
        ps = s.ps("mod", (128, 2, 6, B))
        k = s.sems("tables_in tab_bf weights_in silu_done mod_done mod_read raw_gates abs_done sign_done sign_scaled")
        block = s.block()

        @block.sync
        def _(sp):
            sp.dma_start(c_sb[:, 0, :], dram["c0"]).then_inc(k.weights_in, 16)
            sp.dma_start(c_sb[:, 1, :], dram["c1"]).then_inc(k.weights_in, 16)
            sp.dma_start(wmod[:, 0, :], dram["wmod0"]).then_inc(k.weights_in, 16)
            sp.dma_start(wmod[:, 1, :], dram["wmod1"]).then_inc(k.weights_in, 16)
            sp.dma_start(g.tab[:, :], dram["tables"]).then_inc(k.tables_in, 16)
            sp.dma_start(tab_f[:, :], dram["tables_bf"]).then_inc(k.tables_in, 16)
            sp.wait_ge(k.tables_in, 32)

        @block.scalar
        def _(act):
            act.wait_ge(k.weights_in, 64)
            nc.scalar.activation(silu[:, :, :], c_sb[:, :, :], ACT.Silu).then_inc(k.silu_done, 1)

        @block.tensor
        def _(pe):
            pe.wait_ge(k.silu_done, 1)
            for layer in range(2):
                for j in range(6):
                    last = nc.tensor.matmul(ps[:, layer, j, :], wmod[:, layer, 128 * j:128 * j + 128],
                                            silu[:, layer, :], start=True, stop=True)
            last.then_inc(k.mod_done, 1)

        @block.vector
        def _(dve):
            dve.wait_ge(k.tables_in, 32)
            nc.vector.tensor_copy(g.tab_bf[:, :], tab_f[:, :]).then_inc(k.tab_bf, 1)
            dve.wait_ge(k.mod_done, 1)
            nc.vector.tensor_copy(g.mod[:, :, :, :], ps[:, :, :, :]).then_inc(k.mod_read, 1)
            dve.wait_ge(k.mod_read, 1)
            for layer in range(2):
                for half in range(2):
                    nc.vector.tensor_scalar(g.mod[:, layer, 3 * half + 1, :], g.mod[:, layer, 3 * half + 1, :],
                                            1.0, None, ALU.add)
                    gate = g.mod[:, layer, 3 * half + 2, :]
                    nc.vector.scalar_tensor_tensor(absv[:, layer, half, :], gate, -1.0, gate, ALU.mult, ALU.max)\
                        .then_inc(k.abs_done, 1)
                    nc.vector.tensor_scalar(sign[:, layer, half, :], gate, 0.0, 2.0, ALU.is_ge, ALU.mult)\
                        .then_inc(k.sign_done, 1)
            dve.wait_ge(k.sign_done, 4)
            nc.vector.tensor_scalar(sign[:, :, :, :], sign[:, :, :, :], -1.0, None, ALU.add).then_inc(k.sign_scaled, 1)
            dve.wait_ge(k.sign_scaled, 1)
            dve.wait_ge(k.abs_done, 4)
            for layer in range(2):
                for half in range(2):
                    nc.vector.scalar_tensor_tensor(g.mod[:, layer, 3 * half + 2, :], absv[:, layer, half, :], 0.25,
                                                   sign[:, layer, half, :], ALU.max, ALU.mult)


RC = CH // SLOT


class Rstd:
    STEPS = 3
    MAGIC = float(0x5F3759DF)

    def __init__(self, s, name, count=RC, parts=True):
        if parts:
            self.turned = s.sb(f"{name}_turned", [128, count, SLOT])
            self.out = s.sb(f"{name}_out", [128, count * SLOT])
        self.v = s.sb(f"{name}_v", [128, count])
        self.y = s.sb(f"{name}_y", [128, count])
        self.t = s.sb(f"{name}_t", [128, count])
        self.count = count
        s.sems(f"{name}_turn {name}_v {name}_guess {name}_newton {name}_out")
        self.turn_done, self.v_done, self.guess_done, self.newton_done, self.out_done = s.taken[-5:]

    def run(self, nc, dve, psum, eps, it):
        nc.vector.transpose(self.turned[:, :, :].rearrange("p n i -> p (n i)"), psum).then_inc(self.turn_done, 1)
        dve.wait_ge(self.turn_done, it + 1)
        nc.vector.tensor_scalar(self.v[:, :], self.turned[:, :, 0], eps, None, ALU.add).then_inc(self.v_done, 1)
        dve.wait_ge(self.v_done, it + 1)
        self.root(nc, dve, it)
        nc.vector.transpose(self.out[:, :].rearrange("p (n i) -> p n i", i=SLOT),
                            self.y[:, :, None].to_broadcast([128, self.count, SLOT])).then_inc(self.out_done, 1)
        dve.wait_ge(self.out_done, it + 1)

    def root(self, nc, dve, it):
        nc.vector.tensor_scalar(self.y[:, :].bitcast(mybir.dt.int32), self.v[:, :].bitcast(mybir.dt.int32),
                                -0.5, self.MAGIC, ALU.mult, ALU.add).then_inc(self.guess_done, 1)
        dve.wait_ge(self.guess_done, it + 1)
        for n in range(self.STEPS):
            before = 3 * self.STEPS * it + 3 * n
            nc.vector.scalar_tensor_tensor(self.t[:, :], self.y[:, :], -0.5, self.y[:, :], ALU.mult, ALU.mult)\
                .then_inc(self.newton_done, 1)
            dve.wait_ge(self.newton_done, before + 1)
            nc.vector.tensor_tensor(self.t[:, :], self.t[:, :], self.v[:, :], ALU.mult).then_inc(self.newton_done, 1)
            dve.wait_ge(self.newton_done, before + 2)
            nc.vector.scalar_tensor_tensor(self.y[:, :], self.t[:, :], 1.5, self.y[:, :], ALU.add, ALU.mult)\
                .then_inc(self.newton_done, 1)
            dve.wait_ge(self.newton_done, before + 3)


def load_phase(nc, dram, g):
    with Scope(nc, "load") as s:
        rows = s.sb("rows", [128, 2, CH // 128, D])
        sq = s.sb("sq", [128, 2, CH])
        unit = s.sb("unit", [128, CH])
        unit2 = s.sb("unit2", [128, CH])
        ln = s.sb("ln", [128, 2])
        rstd = [Rstd(s, f"rstd{i}") for i in range(2)]
        turned = s.ps("turned")
        mid = [s.ps(f"mid{i}") for i in range(2)]
        var = [s.ps(f"var{i}") for i in range(2)]
        k = s.sems("rows_in0 rows_in1 ln_in turned x_copied centered0 centered1 squared0 squared1 var0 var1"
                   " unit modulated unit2 xn")
        block = s.block()
        x_rows = dram["x"].rearrange("b t c -> (b t) c")

        @block.sync
        def _(sp):
            sp.dma_start(ln[:, :], dram["ln"]).then_inc(k.ln_in, 16)
            with sp.Fori(0, NCH // 2) as i:
                for par, sem in ((0, k.rows_in0), (1, k.rows_in1)):
                    sp.wait_ge(k.turned, 2 * i + par - 1 if par else 2 * i)
                    sp.dma_start(rows[:, par], x_rows[bass.ds(i * (2 * CH) + par * CH, CH), :]
                                 .rearrange("(r p) c -> p r c", p=128)).then_inc(sem, 16)

        @block.tensor
        def _(pe):
            with pe.Fori(0, NCH // 2) as i:
                for par, sem in ((0, k.rows_in0), (1, k.rows_in1)):
                    it = 2 * i + par
                    cols = bass.ds(i * (2 * CH) + par * CH, CH)
                    pe.wait_ge(sem, 16 * (i + 1))
                    pe.wait_ge(k.x_copied, it)
                    for r in range(CH // 128):
                        last = nc.tensor.transpose(turned[:, 128 * r:128 * r + 128], rows[:, par, r, :], g.t("ident"))
                    last.then_inc(k.turned, 1)
                    pe.wait_ge(k.x_copied, it + 1)
                    pe.wait_ge(k.unit, it)
                    nc.tensor.matmul(mid[0][:, :], g.t("center"), g.xT[:, cols], start=True, stop=True)\
                        .then_inc(k.centered0, 1)
                    pe.wait_ge(k.squared0, it + 1)
                    nc.tensor.matmul(var[0][:, :], g.t("mean"), sq[:, 0, :], start=True, stop=True).then_inc(k.var0, 1)
                    pe.wait_ge(k.modulated, it + 1)
                    pe.wait_ge(k.unit2, it)
                    nc.tensor.matmul(mid[1][:, :], g.t("center"), g.hT[:, cols], start=True, stop=True)\
                        .then_inc(k.centered1, 1)
                    pe.wait_ge(k.squared1, it + 1)
                    nc.tensor.matmul(var[1][:, :], g.t("mean"), sq[:, 1, :], start=True, stop=True).then_inc(k.var1, 1)

        @block.scalar
        def _(act):
            act.wait_ge(k.ln_in, 16)
            with act.Fori(0, NCH) as it:
                act.wait_ge(k.turned, it + 1)
                nc.scalar.activation(g.xT[:, bass.ds(it * CH, CH)], turned[:, :], ACT.Copy).then_inc(k.x_copied, 1)
                act.wait_ge(k.centered0, it + 1)
                nc.scalar.activation(sq[:, 0, :], mid[0][:, :], ACT.Square).then_inc(k.squared0, 1)
                act.wait_ge(k.unit, it + 1)
                for j in range(BPC):
                    last = nc.scalar.activation(g.hT[:, bass.ds(it * CH + j * T, T)], unit[:, j * T:(j + 1) * T],
                                                ACT.Identity, scale=g.mod[:, 0, 1, bass.ds(it * BPC + j, 1)],
                                                bias=g.mod[:, 0, 0, bass.ds(it * BPC + j, 1)])
                last.then_inc(k.modulated, 1)
                act.wait_ge(k.centered1, it + 1)
                nc.scalar.activation(sq[:, 1, :], mid[1][:, :], ACT.Square).then_inc(k.squared1, 1)
                act.wait_ge(k.unit2, it + 1)
                nc.scalar.activation(g.xnT[:, bass.ds(it * CH, CH)], unit2[:, :], ACT.Identity,
                                     scale=ln[:, 0:1], bias=ln[:, 1:2]).then_inc(k.xn, 1)

        @block.vector
        def _(dve):
            with dve.Fori(0, NCH) as it:
                dve.wait_ge(k.var0, it + 1)
                rstd[0].run(nc, dve, var[0][:, :], LN_EPS, it)
                dve.wait_ge(k.modulated, it)
                nc.vector.tensor_tensor(unit[:, :], mid[0][:, :], rstd[0].out[:, :], ALU.mult).then_inc(k.unit, 1)
                dve.wait_ge(k.var1, it + 1)
                rstd[1].run(nc, dve, var[1][:, :], LN_EPS, it)
                dve.wait_ge(k.xn, it)
                nc.vector.tensor_tensor(unit2[:, :], mid[1][:, :], rstd[1].out[:, :], ALU.mult).then_inc(k.unit2, 1)


KEY_AT = {0: (0, 0), 1: (0, 256), 2: (1, 0), 3: (1, 192), 4: (1, 352), 5: (2, 0), 6: (2, 96), 7: (2, 160)}
KEY_COLS = [480, 480, 192]
KEY_OFF = [0, 480, 960]
KEY_ALL = sum(KEY_COLS)
MAX_AT = {6: (0, 0, 256), 7: (0, 256, 256), 4: (1, 0, 192), 5: (1, 192, 192),
          2: (2, 0, 128), 3: (2, 128, 128), 0: (2, 256, 64), 1: (2, 320, 64)}


def attention_phase(nc, dram, g):
    with Scope(nc, "attn") as s:
        w = s.sb("w", [128, 5, GROUPS, 128])
        wo = s.sb("wo", [128, GROUPS, 128])
        dirs = s.sb("dirs", [128, GROUPS, 128])
        hs = s.sb("hs", [128, GROUPS])
        share = s.sb("share", [128, 2, GROUPS])
        tq = s.sb("tq", [128, 2, GROUPS, T])
        tk = s.sb("tk", [128, 2, GROUPS, T])
        q = s.sb("q", [128, GROUPS, T])
        kk = s.sb("k", [128, GROUPS, T])
        q_diag = s.sb("q_diag", [128, GROUPS, KB, PER, SLOT])
        k_diag = s.sb("k_diag", [128, GROUPS, KB, PER, SLOT])
        v_diag = s.sb("v_diag", [128, GROUPS, KB, PER, SLOT])
        g_diag = s.sb("g_diag", [128, KB, PER, SLOT])
        q_less = s.sb("q_less", [128, GROUPS, T])
        v_slots = s.sb("v_slots", [128, GROUPS, T])
        qp = s.sb("qp", [128, T])
        kp = s.sb("kp", [128, T])
        run_max = s.sb("run_max", [128, T])
        run_min = s.sb("run_min", [128, T])
        geo_q = s.sb("geo_q", [128, GROUPS, T])
        mx = s.sb("mx", [128, GROUPS, SLOT])
        mxT = s.sb("mxT", [128, GROUPS, SLOT])
        p = s.sb("p", [128, 2, GROUPS, KEY_ALL])
        oT = s.sb("oT", [128, 2, GROUPS * KB, SLOT])
        coef = s.sb("coef", [128, 2, GROUPS * KB])
        ow = s.sb("ow", [128, 2, GROUPS * KB, DH0])
        aoT = s.sb("aoT", [128, GROUPS * KB, SLOT])
        ao = s.sb("ao", [128, GROUPS, T])
        res = s.sb("res", [128, T])
        bank = [s.ps(f"bank{i}") for i in range(8)]
        X, Y = bank[0:3], bank[3:6]
        k = s.sems("w_in cleared clear_ones share_ready"
                   " q_made qr_made k_made kr_made v_made qp_made kp_made max0_made max1_made"
                   " geo0_made geo1_made att0_made att1_made pvg_made pva_made out_made"
                   " v_read qp_read kp_read gq0 gq1 geo0_exp geo1_exp att0_exp att1_exp"
                   " tq1 tq2 tk1 tk2 v_turned ran_max ran_min max0_read max1_read geo_less geo0_q geo1_q"
                   " mx_turned mx_rows q_less_made oA_turned oG_turned recip coef weighted combined summed"
                   " q_ready k_ready q_diag_ready k_diag_ready g_diag_ready ga_made gb_made added x_done")
        block = s.block()
        tokens = lambda b: bass.ds(b * T, T)

        @block.sync
        def _(sp):
            sp.dma_start(w[:, :, :, :], dram["w_attn"]).then_inc(k.w_in, 16)
            sp.dma_start(wo[:, :, :], dram["wo"]).then_inc(k.w_in, 16)
            sp.dma_start(dirs[:, :, :], dram["dirs"]).then_inc(k.w_in, 16)
            sp.dma_start(hs[:, :], dram["hs"]).then_inc(k.w_in, 16)

        def scores(pe, out, diag, moving):
            for n in range(KB):
                at, c = KEY_AT[n]
                size = T - SLOT * n
                nc.tensor.matmul(out[at][:, c:c + size], diag[:, n], moving[:, SLOT * n:T], start=True, stop=False)
                last = nc.tensor.matmul(out[at][:, c:c + SLOT], g.t("ident_bf"), g.t("mask_key"),
                                        start=False, stop=True)
            return last

        def maxima(pe, out, diag, moving):
            for n in range(KB):
                at, c, size = MAX_AT[n]
                masked = SLOT if n % 2 else 2 * SLOT
                nc.tensor.matmul(out[at][:, c:c + size], diag[:, n], moving[:, 0:size], start=True, stop=False)
                last = nc.tensor.matmul(out[at][:, c + size - masked:c + size], g.t("ident_bf"),
                                        g.t("mask_max")[:, 0:masked], start=False, stop=True)
            return last

        def weigh(out, kind, gr):
            for n in range(KB):
                at, c = KEY_AT[n]
                size = T - SLOT * n
                last = nc.tensor.matmul(out[:, gr * T + SLOT * n:(gr + 1) * T], v_diag[:, gr, n],
                                        p[:, kind, gr, KEY_OFF[at] + c:KEY_OFF[at] + c + size],
                                        start=n == 0, stop=n == KB - 1)
            return last

        @block.tensor
        def _(pe):
            pe.wait_ge(k.w_in, 64)
            pe.wait_ge(k.cleared, 6)
            pe.wait_ge(k.clear_ones, 4)
            with pe.Fori(0, B) as b:
                xn = g.xnT[:, tokens(b)]

                def project(out, n, sem):
                    for gr in range(GROUPS):
                        last = nc.tensor.matmul(out[:, gr * T:(gr + 1) * T], w[:, n, gr, :], xn, start=True, stop=True)
                    last.then_inc(sem, 1)
                pe.wait_ge(k.added, b)
                project(X[0], 0, k.q_made)
                project(X[1], 1, k.qr_made)
                pe.wait_ge(k.att1_exp, b)
                project(Y[0], 2, k.k_made)
                project(Y[1], 3, k.kr_made)
                pe.wait_ge(k.oA_turned, b)
                project(bank[6], 4, k.v_made)
                pe.wait_ge(k.q_ready, b + 1)
                for gr in range(GROUPS):
                    last = nc.tensor.matmul(X[2][:, 0:T], dirs[:, gr, :], q[:, gr, :], start=gr == 0, stop=gr == 1)
                last.then_inc(k.qp_made, 1)
                pe.wait_ge(k.k_ready, b + 1)
                for gr in range(GROUPS):
                    last = nc.tensor.matmul(Y[2][:, 0:T], dirs[:, gr, :], kk[:, gr, :], start=gr == 0, stop=gr == 1)
                last.then_inc(k.kp_made, 1)
                pe.wait_ge(k.q_diag_ready, b + 1)
                pe.wait_ge(k.qp_read, b + 1)
                maxima(pe, X, q_diag[:, 0], kk[:, 0, :]).then_inc(k.max0_made, 1)
                pe.wait_ge(k.g_diag_ready, b + 1)
                maxima(pe, Y, q_diag[:, 1], kk[:, 1, :]).then_inc(k.max1_made, 1)
                pe.wait_ge(k.max0_read, b + 1)
                pe.wait_ge(k.g_diag_ready, b + 1)
                pe.wait_ge(k.geo0_q, b + 1)
                scores(pe, X, g_diag, geo_q[:, 0, :]).then_inc(k.geo0_made, 1)
                pe.wait_ge(k.max1_read, b + 1)
                pe.wait_ge(k.geo1_q, b + 1)
                scores(pe, Y, g_diag, geo_q[:, 1, :]).then_inc(k.geo1_made, 1)
                pe.wait_ge(k.k_diag_ready, b + 1)
                pe.wait_ge(k.q_less_made, b + 1)
                pe.wait_ge(k.geo0_exp, b + 1)
                scores(pe, X, k_diag[:, 0], q_less[:, 0, :]).then_inc(k.att0_made, 1)
                pe.wait_ge(k.v_turned, b + 1)
                pe.wait_ge(k.oG_turned, b)
                weigh(bank[7], 1, 0)
                pe.wait_ge(k.geo1_exp, b + 1)
                scores(pe, Y, k_diag[:, 1], q_less[:, 1, :]).then_inc(k.att1_made, 1)
                weigh(bank[7], 1, 1).then_inc(k.pvg_made, 1)
                pe.wait_ge(k.v_read, b + 1)
                pe.wait_ge(k.att0_exp, b + 1)
                weigh(bank[6], 0, 0)
                pe.wait_ge(k.att1_exp, b + 1)
                weigh(bank[6], 0, 1).then_inc(k.pva_made, 1)
                pe.wait_ge(k.summed, b + 1)
                for gr in range(GROUPS):
                    last = nc.tensor.matmul(X[2][:, 0:T], wo[:, gr, :], ao[:, gr, :], start=gr == 0, stop=gr == 1)
                last.then_inc(k.out_made, 1)

        def exps(act, made, out, kind, gr, sem):
            for i in range(3):
                last = nc.scalar.activation(p[:, kind, gr, KEY_OFF[i]:KEY_OFF[i] + KEY_COLS[i]], out[i][:, 0:KEY_COLS[i]],
                                            ACT.Exp, scale=1.0 if kind else SCALE0)
            last.then_inc(sem, 1)

        @block.scalar
        def _(act):
            with act.Fori(0, B) as b:
                act.wait_ge(k.v_made, b + 1)
                act.wait_ge(k.v_turned, b)
                nc.scalar.activation(v_slots[:, :, :], bank[6][:, :].rearrange("p (g t) -> p g t", g=GROUPS),
                                     ACT.Identity, bias=g.t("sum_col")).then_inc(k.v_read, 1)
                act.wait_ge(k.qp_made, b + 1)
                act.wait_ge(k.ga_made, b)
                act.wait_ge(k.gb_made, b)
                nc.scalar.activation(qp[:, :], X[2][:, 0:T], ACT.Copy)
                act.wait_ge(k.geo1_made, b)
                nc.scalar.activation(geo_q[:, 0, :], X[2][:, 0:T], ACT.Copy, scale=g.t("geo_q")[:, 0:1])\
                    .then_inc(k.gq0, 1)
                nc.scalar.activation(geo_q[:, 1, :], X[2][:, 0:T], ACT.Copy, scale=g.t("geo_q")[:, 1:2])\
                    .then_inc(k.qp_read, 1)
                act.wait_ge(k.kp_made, b + 1)
                act.wait_ge(k.ran_max, b)
                act.wait_ge(k.ran_min, b)
                nc.scalar.activation(kp[:, :], Y[2][:, 0:T], ACT.Copy).then_inc(k.kp_read, 1)
                for h in range(PER):
                    rows = slice(SLOT * h, SLOT * h + SLOT)
                    last = nc.scalar.activation(g_diag[rows, :, h, :],
                                                Y[2][rows, 0:T].rearrange("p (n i) -> p n i", i=SLOT), ACT.Identity,
                                                scale=g.t("geo_kp")[rows], bias=g.t("geo_one")[rows])
                last.then_inc(k.g_diag_ready, 1)
                act.wait_ge(k.k_ready, b + 1)
                act.wait_ge(k.att1_made, b)
                for h in range(PER):
                    part = slice(SLOT * h, SLOT * h + DH0)
                    last = nc.scalar.activation(k_diag[part, :, :, h, :].rearrange("p g n i -> p (g n) i"),
                                                kk[part, :, :].rearrange("p g (n i) -> p (g n) i", i=SLOT), ACT.Copy)
                last.then_inc(k.k_diag_ready, 1)
                act.wait_ge(k.geo0_made, b + 1)
                act.wait_ge(k.pvg_made, b)
                exps(act, k.geo0_made, X, 1, 0, k.geo0_exp)
                act.wait_ge(k.geo1_made, b + 1)
                exps(act, k.geo1_made, Y, 1, 1, k.geo1_exp)
                act.wait_ge(k.att0_made, b + 1)
                act.wait_ge(k.pva_made, b)
                exps(act, k.att0_made, X, 0, 0, k.att0_exp)
                act.wait_ge(k.att1_made, b + 1)
                exps(act, k.att1_made, Y, 0, 1, k.att1_exp)

        def both(ap):
            return ap[:, None, :].to_broadcast([128, GROUPS, T])

        def halves(ap):
            return ap[:, :].rearrange("p (g t) -> p g t", g=GROUPS)

        @block.vector
        def _(dve):
            nc.vector.memset(q_diag[:, :, :, :, :], 0.0).then_inc(k.cleared, 1)
            nc.vector.memset(k_diag[:, :, :, :, :], 0.0).then_inc(k.cleared, 1)
            nc.vector.memset(v_diag[:, :, :, :, :], 0.0).then_inc(k.cleared, 1)
            nc.vector.memset(g_diag[:, :, :, :], 0.0).then_inc(k.cleared, 1)
            nc.vector.memset(mx[:, :, :], 0.0).then_inc(k.cleared, 1)
            nc.vector.memset(aoT[:, :, :], 0.0).then_inc(k.cleared, 1)
            dve.wait_ge(k.cleared, 6)
            for h in range(PER):
                rows = slice(SLOT * h, SLOT * h + SLOT)
                for gr in range(GROUPS):
                    ones = nc.vector.tensor_scalar(k_diag[rows, gr, :, h, :], k_diag[rows, gr, :, h, :],
                                                   g.t("max_any")[rows], None, ALU.add)
                ones.then_inc(k.clear_ones, 1)
            dve.wait_ge(k.w_in, 64)
            nc.vector.tensor_copy(share[:, 1, :], hs[:, :]).then_inc(k.share_ready, 1)
            nc.vector.tensor_scalar(share[:, 0, :], hs[:, :], -1.0, 1.0, ALU.mult, ALU.add).then_inc(k.share_ready, 1)
            dve.wait_ge(k.share_ready, 2)
            with dve.Fori(0, B) as b:
                dve.wait_ge(k.q_ready, b)
                dve.wait_ge(k.q_made, b + 1)
                nc.vector.tensor_tensor(tq[:, 0], halves(X[0]), both(g.t("cos")), ALU.mult).then_inc(k.tq1, 1)
                dve.wait_ge(k.qr_made, b + 1)
                nc.vector.tensor_tensor(tq[:, 1], halves(X[1]), both(g.t("sin")), ALU.mult).then_inc(k.tq2, 1)
                dve.wait_ge(k.k_ready, b)
                dve.wait_ge(k.k_made, b + 1)
                nc.vector.tensor_tensor(tk[:, 0], halves(Y[0]), both(g.t("cos")), ALU.mult).then_inc(k.tk1, 1)
                dve.wait_ge(k.kr_made, b + 1)
                nc.vector.tensor_tensor(tk[:, 1], halves(Y[1]), both(g.t("sin")), ALU.mult).then_inc(k.tk2, 1)
                dve.wait_ge(k.v_read, b + 1)
                dve.wait_ge(k.pva_made, b)
                for h in range(PER):
                    rows = slice(SLOT * h, SLOT * h + SLOT)
                    last = nc.vector.transpose(v_diag[rows, :, :, h, :].rearrange("p g n d -> p (g n) d"),
                                               v_slots[rows, :, :].rearrange("p g (n d) -> p (g n) d", d=SLOT))
                last.then_inc(k.v_turned, 1)
                dve.wait_ge(k.q_ready, b + 1)
                dve.wait_ge(k.max1_made, b)
                for h in range(PER):
                    part = slice(SLOT * h, SLOT * h + DH0)
                    last = nc.vector.tensor_copy(q_diag[part, :, :, h, :].rearrange("p g n i -> p (g n) i"),
                                                 q[part, :, :].rearrange("p g (n i) -> p (g n) i", i=SLOT))
                last.then_inc(k.q_diag_ready, 1)
                dve.wait_ge(k.kp_read, b + 1)
                dve.wait_ge(k.ga_made, b)
                dve.wait_ge(k.gb_made, b)
                nc.vector.tensor_tensor_scan(run_max[:, :], kp[:, :], kp[:, :], -3e38, ALU.max, ALU.max)\
                    .then_inc(k.ran_max, 1)
                nc.vector.tensor_tensor_scan(run_min[:, :], kp[:, :], kp[:, :], 3e38, ALU.min, ALU.min)\
                    .then_inc(k.ran_min, 1)

                def read_max(out, gr, sem):
                    for at, c, count, size, n in ((0, 0, 2, 256, 6), (1, 0, 2, 192, 4), (2, 0, 2, 128, 2), (2, 256, 2, 64, 0)):
                        last = nc.vector.tensor_reduce(
                            mx[:, gr, DH0 + n:DH0 + n + count],
                            out[at][:, c:c + count * size].rearrange("p (n j) -> p n j", n=count), AX.X, ALU.max,
                            negate=True)
                    last.then_inc(sem, 1)
                dve.wait_ge(k.max0_made, b + 1)
                dve.wait_ge(k.mx_turned, b)
                read_max(X, 0, k.max0_read)
                dve.wait_ge(k.ga_made, b + 1)
                dve.wait_ge(k.gb_made, b + 1)
                nc.vector.tensor_tensor(run_max[:, :], run_max[:, :], run_min[:, :], ALU.max).then_inc(k.geo_less, 1)
                dve.wait_ge(k.geo_less, b + 1)
                dve.wait_ge(k.gq0, b + 1)
                nc.vector.scalar_tensor_tensor(geo_q[:, 0, :], run_max[:, :], g.t("geo_m")[:, 0:1], geo_q[:, 0, :],
                                               ALU.mult, ALU.add).then_inc(k.geo0_q, 1)
                dve.wait_ge(k.qp_read, b + 1)
                nc.vector.scalar_tensor_tensor(geo_q[:, 1, :], run_max[:, :], g.t("geo_m")[:, 1:2], geo_q[:, 1, :],
                                               ALU.mult, ALU.add).then_inc(k.geo1_q, 1)
                dve.wait_ge(k.max1_made, b + 1)
                read_max(Y, 1, k.max1_read)
                dve.wait_ge(k.max0_read, b + 1)
                dve.wait_ge(k.max1_read, b + 1)
                nc.vector.transpose(mxT[:, :, :].rearrange("p g i -> p (g i)"), mx[:, :, :].rearrange("p g i -> p (g i)"))\
                    .then_inc(k.mx_turned, 1)
                dve.wait_ge(k.mx_turned, b + 1)
                dve.wait_ge(k.att1_made, b)
                nc.vector.tensor_tensor(q_less[:, :, :].rearrange("p g (n i) -> p g n i", i=SLOT),
                                        mxT[:, :, None, :].to_broadcast([128, GROUPS, KB, SLOT]),
                                        g.t("max_rows")[:, None, :, None].to_broadcast([128, GROUPS, KB, SLOT]), ALU.mult)\
                    .then_inc(k.mx_rows, 1)
                dve.wait_ge(k.pvg_made, b + 1)
                nc.vector.transpose(oT[:, 1].rearrange("p n i -> p (n i)"), bank[7][:, :]).then_inc(k.oG_turned, 1)
                dve.wait_ge(k.pva_made, b + 1)
                nc.vector.transpose(oT[:, 0].rearrange("p n i -> p (n i)"), bank[6][:, :]).then_inc(k.oA_turned, 1)
                dve.wait_ge(k.oG_turned, b + 1)
                dve.wait_ge(k.oA_turned, b + 1)
                nc.vector.reciprocal(coef[:, :, :], oT[:, :, :, DH0]).then_inc(k.recip, 1)
                dve.wait_ge(k.recip, b + 1)
                by_group = coef[:, :, :].rearrange("p s (g n) -> p (s g) n", g=GROUPS)
                nc.vector.tensor_tensor(by_group, by_group, share[:, :, :].rearrange("p s g -> p (s g)")[:, :, None]
                                        .to_broadcast([128, 2 * GROUPS, KB]), ALU.mult).then_inc(k.coef, 1)
                dve.wait_ge(k.coef, b + 1)
                nc.vector.tensor_tensor(ow[:, :, :, :].rearrange("p s n d -> p (s n) d"),
                                        oT[:, :, :, 0:DH0].rearrange("p s n d -> p (s n) d"),
                                        coef[:, :, :].rearrange("p s n -> p (s n)")[:, :, None]
                                        .to_broadcast([128, 2 * GROUPS * KB, DH0]), ALU.mult).then_inc(k.weighted, 1)
                dve.wait_ge(k.weighted, b + 1)
                nc.vector.tensor_tensor(aoT[:, :, 0:DH0], ow[:, 0], ow[:, 1], ALU.add).then_inc(k.combined, 1)
                dve.wait_ge(k.combined, b + 1)
                nc.vector.transpose(ao[:, :, :].rearrange("p g t -> p (g t)"), aoT[:, :, :].rearrange("p n i -> p (n i)"))\
                    .then_inc(k.summed, 1)
                dve.wait_ge(k.out_made, b + 1)
                nc.vector.tensor_tensor(res[:, :], X[2][:, 0:T], g.hT[:, tokens(b)], ALU.add).then_inc(k.added, 1)
                dve.wait_ge(k.added, b + 1)
                nc.vector.scalar_tensor_tensor(g.xT[:, tokens(b)], res[:, :], g.mod[:, 0, 2, bass.ds(b, 1)],
                                               g.xT[:, tokens(b)], ALU.mult, ALU.add).then_inc(k.x_done, 1)

        @block.gpsimd
        def _(pool):
            with pool.Fori(0, B) as b:
                pool.wait_ge(k.tq1, b + 1)
                pool.wait_ge(k.tq2, b + 1)
                pool.wait_ge(k.q_diag_ready, b)
                pool.wait_ge(k.qp_made, b)
                pool.wait_ge(k.q_less_made, b)
                nc.gpsimd.tensor_tensor(q[:, :, :], tq[:, 0], tq[:, 1], ALU.add).then_inc(k.q_ready, 1)
                pool.wait_ge(k.tk1, b + 1)
                pool.wait_ge(k.tk2, b + 1)
                pool.wait_ge(k.max1_made, b)
                pool.wait_ge(k.k_diag_ready, b)
                nc.gpsimd.tensor_tensor(kk[:, :, :], tk[:, 0], tk[:, 1], ALU.add).then_inc(k.k_ready, 1)
                pool.wait_ge(k.qp_read, b + 1)
                pool.wait_ge(k.ran_max, b + 1)
                pool.wait_ge(k.geo1_q, b)
                nc.gpsimd.tensor_tensor(run_max[:, :], run_max[:, :], qp[:, :], ALU.mult).then_inc(k.ga_made, 1)
                pool.wait_ge(k.ran_min, b + 1)
                nc.gpsimd.tensor_tensor(run_min[:, :], run_min[:, :], qp[:, :], ALU.mult).then_inc(k.gb_made, 1)
                pool.wait_ge(k.mx_rows, b + 1)
                pool.wait_ge(k.q_ready, b + 1)
                nc.gpsimd.tensor_tensor(q_less[:, :, :], q_less[:, :, :], q[:, :, :], ALU.add).then_inc(k.q_less_made, 1)


class Chain:

    def __init__(self, eng, sem, per, it):
        self.eng, self.sem, self.per, self.it, self.n = eng, sem, per, it, 0

    def __call__(self, ins, wait=True):
        ins.then_inc(self.sem, 1)
        self.n += 1
        assert self.n <= self.per
        if wait:
            self.eng.wait_ge(self.sem, self.per * self.it + self.n)


TILES = CH // 128
ROW = D + E0


def route_phase(nc, dram, g):
    CHOICES = TILES * K0
    with Scope(nc, "route") as s:
        gate_w = s.sb("gate_w", [128, E0], BF16)
        gate_wf = s.sb("gate_wf", [128, E0])
        bias = s.sb("bias", [128, E0])
        sw_bf = s.sb("sw_bf", [128, 2, I0], BF16)
        sw = s.sb("sw", [128, 2, I0])
        sw2_bf = s.sb("sw2_bf", [I0, D], BF16)
        sw2 = s.sb("sw2", [I0, D])
        iota = s.sb("iota", [128, CAP], BF16)
        before = s.sb("before", [128, 128], BF16)
        ones = s.sb("ones", [128, 128], BF16)
        zero = s.sb("zero", [128, 13 * D])
        zero_bf = s.sb("zero_bf", [128, 128], BF16)
        sq = s.sb("sq", [128, CH])
        unit = s.sb("unit", [128, CH])
        h2 = s.sb("h2", [128, CH])
        rows = s.sb("rows", [128, TILES, ROW])
        score = s.sb("score", [128, TILES, E0])
        biased = s.sb("biased", [128, TILES, E0])
        top = s.sb("top", [128, TILES, 8])
        top_at = s.sb("top_at", [128, TILES, 8], U32)
        chosen = s.sb("chosen", [128, TILES, K0])
        by_expert = s.sb("by_expert", [128, CHOICES, 3, E0], BF16)
        mask = s.sb("mask", [128, TILES, E0], BF16)
        gates = s.sb("gates", [128, TILES, E0])
        total = s.sb("total", [128, TILES])
        seen = s.sb("seen", [128, 2])
        place = s.sb("place", [128, TILES, E0])
        base = s.sb("base", [128, E0])
        own = s.sb("own", [128, CHOICES, E0])
        slot = s.sb("slot", [128, CHOICES])
        by_slot = s.sb("by_slot", [128, CHOICES, CAP], BF16)
        sig1 = s.sb("sig1", [I0, CH])
        hid = s.sb("hid", [I0, CH])
        held = s.sb("held", [128, 3, E0])
        free = s.sb("free", [128, E0])
        rstd = Rstd(s, "rstd")
        mid, var, up1, up3, turned, small, slots_ps, shared = (s.ps(n) for n in
            ("mid", "var", "up1", "up3", "turned", "small", "slots_ps", "shared"))
        k = s.sems("w_in zeroed consts cleared rows_out zero_out centered squared var unit modulated logits up1 up3"
                   " turned score sig1 rows_read mask counted route hid_part hid shared_made x_half x_done slots_done"
                   " slots_added held tail idx")
        block = s.block()
        STEPS = 2 * TILES + 12 + CHOICES + 2

        @block.sync
        def _(sp):
            sp.dma_start(gate_w[:, :], dram["gate_w"]).then_inc(k.w_in, 16)
            sp.dma_start(bias[:, :], dram["gate_bias"].to_broadcast([128, E0])).then_inc(k.w_in, 16)
            sp.dma_start(sw_bf[:, :, :], dram["sw13"]).then_inc(k.w_in, 16)
            sp.dma_start(sw2_bf[:, :], dram["sw2"]).then_inc(k.w_in, 16)
            sp.wait_ge(k.zeroed, 1)
            acc = g.acc.rearrange("(p r) c -> p (r c)", p=128)
            for i in range(5):
                sp.dma_start(acc[:, i * 13 * D:(i + 1) * 13 * D], zero[:, :]).then_inc(k.zero_out, 16)
            sp.dma_start(g.rows[N:N + CAP, :], zero[:, 0:ROW]).then_inc(k.zero_out, 16)
            with sp.Fori(0, NCH) as it:
                sp.wait_ge(k.rows_read, it + 1)
                sp.wait_ge(k.route, STEPS * it + 2 * TILES + 9)
                sp.dma_start(g.rows[bass.ds(it * CH, CH), :].rearrange("(r p) c -> p r c", p=128), rows[:, :, :])\
                    .then_inc(k.rows_out, 16)
            sp.wait_ge(k.rows_out, 16 * NCH)
            sp.wait_ge(k.zero_out, 16 * 6)

        @block.tensor
        def _(pe):
            pe.wait_ge(k.consts, 5)
            nc.tensor.matmul(slots_ps[:, 0:3 * E0], zero_bf[:, :], zero_bf[:, 0:3 * E0], start=True, stop=False)
            with pe.Fori(0, NCH) as it:
                cols = bass.ds(it * CH, CH)
                pe.wait_ge(k.unit, it)
                nc.tensor.matmul(mid[:, :], g.t("center"), g.xT[:, cols], start=True, stop=True).then_inc(k.centered, 1)
                pe.wait_ge(k.squared, it + 1)
                nc.tensor.matmul(var[:, :], g.t("mean"), sq[:, :], start=True, stop=True).then_inc(k.var, 1)
                pe.wait_ge(k.modulated, it + 1)
                pe.wait_ge(k.counted, 2 * it)
                for j in range(TILES):
                    last = nc.tensor.matmul(small[:, j * E0:(j + 1) * E0], h2[:, 128 * j:128 * j + 128], gate_wf[:, :],
                                            start=True, stop=True)
                last.then_inc(k.logits, 1)
                pe.wait_ge(k.hid, it)
                nc.tensor.matmul(up1[0:I0, :], sw[:, 0, :], h2[:, :], start=True, stop=True).then_inc(k.up1, 1)
                nc.tensor.matmul(up3[0:I0, :], sw[:, 1, :], h2[:, :], start=True, stop=True).then_inc(k.up3, 1)
                for j in range(TILES):
                    last = nc.tensor.transpose(turned[:, 128 * j:128 * j + 128], h2[:, 128 * j:128 * j + 128], g.t("ident"))
                last.then_inc(k.turned, 1)
                pe.wait_ge(k.route, STEPS * it + 2 * TILES + 4)
                for j in range(TILES + 1):
                    out = small[:, 128 + j * E0:128 + (j + 1) * E0]
                    for i in range(min(j, TILES)):
                        last = nc.tensor.matmul(out, ones[:, :], mask[:, i, :], start=i == 0, stop=i == TILES - 1)
                    if j < TILES:
                        last = nc.tensor.matmul(out, before[:, :], mask[:, j, :], start=j == 0, stop=True)
                last.then_inc(k.mask, 1)
                pe.wait_ge(k.hid, it + 1)
                pe.wait_ge(k.x_done, it)
                nc.tensor.matmul(shared[:, :], sw2[:, :], hid[:, :], start=True, stop=True).then_inc(k.shared_made, 1)
                pe.wait_ge(k.route, STEPS * (it + 1))
                for c in range(CHOICES):
                    last = nc.tensor.matmul(slots_ps[:, 0:3 * E0], by_slot[:, c, :],
                                            by_expert[:, c, :, :].rearrange("p v e -> p (v e)"), start=False, stop=False)
                last.then_inc(k.slots_added, 1)
            nc.tensor.matmul(slots_ps[:, 0:3 * E0], zero_bf[:, :], zero_bf[:, 0:3 * E0], start=False, stop=True)\
                .then_inc(k.slots_done, 1)

        @block.scalar
        def _(act):
            with act.Fori(0, NCH) as it:
                act.wait_ge(k.centered, it + 1)
                nc.scalar.activation(sq[:, :], mid[:, :], ACT.Square).then_inc(k.squared, 1)
                act.wait_ge(k.unit, it + 1)
                act.wait_ge(k.turned, it)
                for j in range(BPC):
                    last = nc.scalar.activation(h2[:, j * T:(j + 1) * T], unit[:, j * T:(j + 1) * T], ACT.Identity,
                                                scale=g.mod[:, 0, 4, bass.ds(it * BPC + j, 1)],
                                                bias=g.mod[:, 0, 3, bass.ds(it * BPC + j, 1)])
                last.then_inc(k.modulated, 1)
                act.wait_ge(k.logits, it + 1)
                act.wait_ge(k.route, STEPS * it)
                nc.scalar.activation(score[:, :, :].rearrange("p j e -> p (j e)"), small[:, 0:TILES * E0], ACT.Sigmoid)\
                    .then_inc(k.score, 1)
                act.wait_ge(k.up1, it + 1)
                act.wait_ge(k.hid_part, it)
                nc.scalar.activation(sig1[:, :], up1[0:I0, :], ACT.Sigmoid).then_inc(k.sig1, 1)
                act.wait_ge(k.turned, it + 1)
                act.wait_ge(k.rows_out, 16 * it)
                nc.scalar.activation(rows[:, :, 0:D], turned[:, :].rearrange("p (j c) -> p j c", c=D), ACT.Copy)\
                    .then_inc(k.rows_read, 1)

        @block.vector
        def _(dve):
            nc.vector.memset(zero[:, :], 0.0).then_inc(k.zeroed, 1)
            nc.vector.memset(base[:, :], 0.0).then_inc(k.cleared, 1)
            nc.vector.memset(zero_bf[:, :], 0.0).then_inc(k.consts, 1)
            nc.vector.tensor_copy(before[:, :], g.t("before")).then_inc(k.consts, 1)
            nc.vector.tensor_copy(ones[:, :], g.t("ones")).then_inc(k.consts, 1)
            nc.vector.tensor_copy(iota[:, :], g.t("iota")).then_inc(k.cleared, 1)
            dve.wait_ge(k.w_in, 64)
            nc.vector.tensor_copy(gate_wf[:, :], gate_w[:, :]).then_inc(k.consts, 1)
            nc.vector.tensor_copy(sw[:, :, :], sw_bf[:, :, :])
            nc.vector.tensor_copy(sw2[:, :], sw2_bf[:, :]).then_inc(k.consts, 1)
            dve.wait_ge(k.cleared, 2)

            def per_tile(ap):
                return ap[:, None, :].to_broadcast([128, TILES, E0])
            with dve.Fori(0, NCH) as it:
                dve.wait_ge(k.var, it + 1)
                rstd.run(nc, dve, var[:, :], LN_EPS, it)
                dve.wait_ge(k.modulated, it)
                nc.vector.tensor_tensor(unit[:, :], mid[:, :], rstd.out[:, :], ALU.mult).then_inc(k.unit, 1)
                dve.wait_ge(k.score, it + 1)
                then = Chain(dve, k.route, STEPS, it)
                then(nc.vector.tensor_tensor(biased[:, :, :], score[:, :, :], per_tile(bias), ALU.add))
                nc.vector.tensor_copy(seen[:, 0:1], biased[:, 0, 0:1])
                for j in range(TILES):
                    then(nc.vector.max(top[:, j, :], biased[:, j, :]), wait=j == TILES - 1)
                nc.vector.tensor_copy(seen[:, 1:2], top[:, 0, 0:1])
                for j in range(TILES):
                    then(nc.vector.max_index(top_at[:, j, :], top[:, j, :], biased[:, j, :]), wait=j == TILES - 1)
                then(nc.vector.tensor_copy(chosen[:, :, :], top_at[:, :, 0:K0]))
                dve.wait_ge(k.slots_added, it)
                onehot = by_expert[:, :, 0, :]
                then(nc.vector.tensor_tensor(onehot, g.t("iota")[:, None, 0:E0].to_broadcast([128, CHOICES, E0]),
                                             chosen[:, :, :].rearrange("p j c -> p (j c)")[:, :, None]
                                             .to_broadcast([128, CHOICES, E0]), ALU.is_equal))
                with nc.allow_low_precision(reason="sums of one-hot rows are 0 or 1"):
                    then(nc.vector.tensor_reduce(mask[:, :, :], onehot.rearrange("p (j c) e -> p j e c", c=K0),
                                                 AX.X, ALU.add))
                then(nc.vector.tensor_tensor(gates[:, :, :], mask[:, :, :], score[:, :, :], ALU.mult))
                then(nc.vector.tensor_reduce(total[:, :], gates[:, :, :], AX.X, ALU.add))
                then(nc.vector.tensor_scalar(total[:, :], total[:, :], 1e-12, None, ALU.max))
                then(nc.vector.reciprocal(total[:, :], total[:, :]))
                dve.wait_ge(k.rows_out, 16 * it)
                then(nc.vector.tensor_tensor(rows[:, :, D:ROW], gates[:, :, :],
                                             total[:, :, None].to_broadcast([128, TILES, E0]), ALU.mult))
                dve.wait_ge(k.mask, it + 1)
                then(nc.vector.tensor_tensor(place[:, :, :], small[:, 128:128 + TILES * E0]
                                             .rearrange("p (j e) -> p j e", e=E0), per_tile(base), ALU.add))
                nc.vector.tensor_tensor(base[:, :], base[:, :], small[:, 128 + TILES * E0:128 + (TILES + 1) * E0], ALU.add)\
                    .then_inc(k.counted, 2)
                dve.wait_ge(k.counted, 2 * (it + 1))
                then(nc.vector.tensor_tensor(own[:, :, :].rearrange("p (j c) e -> p j c e", c=K0),
                                             onehot.rearrange("p (j c) e -> p j c e", c=K0),
                                             place[:, :, None, :].to_broadcast([128, TILES, K0, E0]), ALU.mult))
                then(nc.vector.tensor_reduce(slot[:, :], own[:, :, :], AX.X, ALU.add))
                for c in range(CHOICES):
                    then(nc.vector.tensor_scalar(by_slot[:, c, :], iota[:, :], slot[:, c:c + 1], None, ALU.is_equal), wait=False)
                then(nc.vector.tensor_scalar(by_expert[:, :, 1, :], onehot, g.t("row_no"), None, ALU.mult))
                then(nc.vector.tensor_tensor(by_expert[:, :, 2, :].rearrange("p (j c) e -> p j c e", c=K0),
                                             onehot.rearrange("p (j c) e -> p j c e", c=K0),
                                             g.t("tile_no")[:, bass.ds(it * TILES, TILES)][:, :, None, None]
                                             .to_broadcast([128, TILES, K0, E0]), ALU.mult))
                dve.wait_ge(k.sig1, it + 1)
                dve.wait_ge(k.shared_made, it)
                nc.vector.tensor_tensor(sig1[:, :], sig1[:, :], up1[0:I0, :], ALU.mult).then_inc(k.hid_part, 1)
                dve.wait_ge(k.hid_part, it + 1)
                dve.wait_ge(k.up3, it + 1)
                nc.vector.tensor_tensor(hid[:, :], sig1[:, :], up3[0:I0, :], ALU.mult).then_inc(k.hid, 1)
                dve.wait_ge(k.shared_made, it + 1)
                for j in range(BPC):
                    x = g.xT[:, bass.ds(it * CH + j * T, T)]
                    last = nc.vector.scalar_tensor_tensor(x, shared[:, j * T:(j + 1) * T],
                                                          g.mod[:, 0, 5, bass.ds(it * BPC + j, 1)], x, ALU.mult, ALU.add)
                last.then_inc(k.x_done, 1)
            dve.wait_ge(k.slots_done, 1)
            nc.vector.tensor_copy(held[:, :, :].rearrange("p v e -> p (v e)"), slots_ps[:, 0:3 * E0]).then_inc(k.held, 1)
            dve.wait_ge(k.held, 1)
            nc.vector.tensor_scalar(free[:, :], held[:, 0, :], -1.0, 1.0, ALU.mult, ALU.add).then_inc(k.tail, 1)
            nc.vector.scalar_tensor_tensor(held[:, 1, :], held[:, 2, :], 128.0, held[:, 1, :], ALU.mult, ALU.add)\
                .then_inc(k.tail, 1)
            dve.wait_ge(k.tail, 2)
            nc.vector.scalar_tensor_tensor(held[:, 1, :], free[:, :], g.t("past"), held[:, 1, :], ALU.mult, ALU.add)\
                .then_inc(k.tail, 1)
            dve.wait_ge(k.tail, 3)
            nc.vector.tensor_copy(g.slot_token[:, :], held[:, 1, :])


def experts_phase(nc, dram, g):
    PAR = 2
    with Scope(nc, "exp") as s:
        w13_bf = s.sb("w13_bf", [128, E0, 2 * I0], BF16)
        w2_bf = s.sb("w2_bf", [I0, E0, D], BF16)
        w13 = s.sb("w13", [128, E0, 2 * I0])
        w2 = s.sb("w2", [I0, E0, D])
        rows = s.sb("rows", [128, E0 * ROW])
        y = s.sb("y", [128, E0 * D])
        xg = s.sb("xg", [128, PAR, D])
        xgT = s.sb("xgT", [128, PAR, 128])
        sig = s.sb("sig", [128, PAR, I0])
        hid = s.sb("hid", [128, PAR, 128])
        hidT = s.sb("hidT", [I0, PAR, 128])
        ps = [[s.ps(f"{n}{par}") for n in ("x", "up", "h", "down")] for par in range(PAR)]
        w = s.sems("w_in padded w13 w2 gathered added")
        k = [s.sems("staged turned x_copied up sig part hid h_turned h_copied down y", par) for par in range(PAR)]
        block = s.block()

        @block.sync
        def _(sp):
            sp.dma_start(w13_bf[:, :, :], dram["w13"]).then_inc(w.w_in, 16)
            sp.dma_start(w2_bf[:, :, :], dram["w2"]).then_inc(w.w_in, 16)

        @block.gpsimd
        def _(pool):
            for e in range(E0):
                nc.gpsimd.indirect_dma_start(rows[:, e * ROW:(e + 1) * ROW], None, g.rows,
                                             bass.IndirectOffsetOnAxis(g.slot_token[:, e:e + 1], 0)).then_inc(w.gathered, 16)
            for e in range(E0):
                pool.wait_ge(k[e % PAR].y, e // PAR + 1)
                if e:
                    pool.wait_ge(w.added, 16 * e)
                nc.gpsimd.indirect_dma_start(g.acc, bass.IndirectOffsetOnAxis(g.slot_token[:, e:e + 1], 0),
                                             y[:, e * D:(e + 1) * D], None, compute_op=ALU.add).then_inc(w.added, 16)
            pool.wait_ge(w.added, 16 * E0)

        @block.tensor
        def _(pe):
            pe.wait_ge(w.w13, 1)
            pe.wait_ge(w.w2, 1)
            with pe.Fori(0, E0 // PAR) as i:
                for par in range(PAR):
                    pe.wait_ge(k[par].staged, i + 1)
                    nc.tensor.transpose(ps[par][0][:, 0:128], xg[:, par, :], g.t("ident")).then_inc(k[par].turned, 1)
                for par in range(PAR):
                    pe.wait_ge(k[par].x_copied, i + 1)
                    nc.tensor.matmul(ps[par][1][:, 0:2 * I0], xgT[:, par, :], w13[:, bass.ds(i * PAR + par, 1), :]
                                     .rearrange("p e i -> p (e i)"), start=True, stop=True).then_inc(k[par].up, 1)
                for par in range(PAR):
                    pe.wait_ge(k[par].hid, i + 1)
                    nc.tensor.transpose(ps[par][2][:, 0:128], hid[:, par, :], g.t("ident")).then_inc(k[par].h_turned, 1)
                for par in range(PAR):
                    pe.wait_ge(k[par].h_copied, i + 1)
                    nc.tensor.matmul(ps[par][3][:, 0:D], hidT[:, par, :], w2[:, bass.ds(i * PAR + par, 1), :]
                                     .rearrange("p e i -> p (e i)"), start=True, stop=True).then_inc(k[par].down, 1)

        @block.scalar
        def _(act):
            act.wait_ge(w.w_in, 32)
            nc.scalar.activation(w2[:, :, :], w2_bf[:, :, :], ACT.Copy).then_inc(w.w2, 1)
            with act.Fori(0, E0 // PAR) as i:
                for par in range(PAR):
                    act.wait_ge(k[par].turned, i + 1)
                    nc.scalar.activation(xgT[:, par, :], ps[par][0][:, 0:128], ACT.Copy).then_inc(k[par].x_copied, 1)
                for par in range(PAR):
                    act.wait_ge(k[par].up, i + 1)
                    nc.scalar.activation(sig[:, par, :], ps[par][1][:, 0:I0], ACT.Sigmoid).then_inc(k[par].sig, 1)
                for par in range(PAR):
                    act.wait_ge(k[par].h_turned, i + 1)
                    nc.scalar.activation(hidT[:, par, :], ps[par][2][0:I0, 0:128], ACT.Copy).then_inc(k[par].h_copied, 1)

        @block.vector
        def _(dve):
            dve.wait_ge(w.w_in, 32)
            nc.vector.tensor_copy(w13[:, :, :], w13_bf[:, :, :]).then_inc(w.w13, 1)
            nc.vector.memset(hid[:, :, :], 0.0).then_inc(w.padded, 1)
            dve.wait_ge(w.padded, 1)
            dve.wait_ge(w.gathered, 16 * E0)
            with dve.Fori(0, E0 // PAR) as i:
                for par in range(PAR):
                    dve.wait_ge(k[par].turned, i)
                    nc.vector.tensor_copy(xg[:, par, :], rows[:, bass.ds(i * (PAR * ROW) + par * ROW, D)])\
                        .then_inc(k[par].staged, 1)
                for par in range(PAR):
                    dve.wait_ge(k[par].sig, i + 1)
                    nc.vector.tensor_tensor(sig[:, par, :], sig[:, par, :], ps[par][1][:, 0:I0], ALU.mult)\
                        .then_inc(k[par].part, 1)
                for par in range(PAR):
                    dve.wait_ge(k[par].part, i + 1)
                    nc.vector.tensor_tensor(hid[:, par, 0:I0], sig[:, par, :], ps[par][1][:, I0:2 * I0], ALU.mult)\
                        .then_inc(k[par].hid, 1)
                for par in range(PAR):
                    dve.wait_ge(k[par].down, i + 1)
                    nc.vector.tensor_scalar(y[:, bass.ds(i * (PAR * D) + par * D, D)], ps[par][3][:, 0:D],
                                            rows[:, bass.ds(i * (PAR * (ROW + 1)) + par * (ROW + 1) + D, 1)], None,
                                            ALU.mult).then_inc(k[par].y, 1)


GT = 8


def project_phase(nc, dram, g):
    LEAD = CONV - 1
    HEADS_IN_BLOCK = SLOT // DH1
    with Scope(nc, "proj") as s:
        w = s.sb("w", [128, 3, 128])
        wb = s.sb("wb", [128, H1])
        wb_wide = s.sb("wb_wide", [128, H1, DH1])
        bias = s.sb("bias", [128, 4])
        taps = s.sb("taps", [128, 3, CONV])
        last_bias = s.sb("last_bias", [128, 3])
        rows = s.sb("rows", [128, TILES, D])
        sq = s.sb("sq", [128, CH])
        unit = s.sb("unit", [128, CH])
        h3 = s.sb("h3", [128, CH])
        pad = s.sb("pad", [128, 3, BPC, LEAD + T])
        conv = s.sb("conv", [128, 3, CH])
        sq2 = s.sb("sq2", [128, 2, CH])
        sig = s.sb("sig", [128, CH])
        rate = s.sb("rate", [128, CH])
        len_t = s.sb("len_t", [128, 2, RC, SLOT])
        ss = s.sb("ss", [128, 2, RC, HEADS_IN_BLOCK])
        inv = s.sb("inv", [128, 2, RC, HEADS_IN_BLOCK])
        rstd = Rstd(s, "rstd")
        root = Rstd(s, "root", 2 * RC * HEADS_IN_BLOCK, parts=False)
        mid, var, turned = s.ps("mid"), s.ps("var"), s.ps("turned")
        made = [s.ps(f"made{i}") for i in range(4)]
        sums = s.ps("sums")
        k = s.sems("w_in wide rows_in turned x_added x_out centered squared var unit modulated made0 made1 made2 made3"
                   " padded0 padded1 padded2 sq2_0 sq2_1 sum0 sum1 len0 len1 sig rate conv root inv v_part v_done k_done"
                   " q_done b_done zeroed spread")
        block = s.block()
        acc = g.acc[0:N, :]
        CONVS = 3 * LEAD

        @block.sync
        def _(sp):
            for dst, name in ((w[:, :, :], "w1_qkv"), (wb[:, :], "w_beta"), (bias[:, :], "b1"), (taps[:, :, :], "taps")):
                sp.dma_start(dst, dram[name]).then_inc(k.w_in, 16)
            with sp.Fori(0, NCH) as it:
                cols = bass.ds(it * CH, CH)
                sp.wait_ge(k.turned, it)
                sp.dma_start(rows[:, :, :], acc[cols, :].rearrange("(r p) c -> p r c", p=128)).then_inc(k.rows_in, 16)
                sp.wait_ge(k.x_added, it + 1)
                sp.dma_start(g.x_kept[:, cols], g.xT[:, cols]).then_inc(k.x_out, 16)
            sp.wait_ge(k.x_out, 16 * NCH)

        @block.tensor
        def _(pe):
            pe.wait_ge(k.wide, 2)
            with pe.Fori(0, NCH) as it:
                cols = bass.ds(it * CH, CH)
                pe.wait_ge(k.rows_in, 16 * (it + 1))
                pe.wait_ge(k.x_added, it)
                for r in range(TILES):
                    last = nc.tensor.transpose(turned[:, 128 * r:128 * r + 128], rows[:, r, :], g.t("ident"))
                last.then_inc(k.turned, 1)
                pe.wait_ge(k.x_added, it + 1)
                pe.wait_ge(k.unit, it)
                nc.tensor.matmul(mid[:, :], g.t("center"), g.xT[:, cols], start=True, stop=True).then_inc(k.centered, 1)
                pe.wait_ge(k.squared, it + 1)
                nc.tensor.matmul(var[:, :], g.t("mean"), sq[:, :], start=True, stop=True).then_inc(k.var, 1)
                pe.wait_ge(k.modulated, it + 1)
                for i, (sem, free) in enumerate(((k.made0, k.conv), (k.made1, k.conv), (k.made2, k.conv))):
                    pe.wait_ge(free, CONVS * it)
                    nc.tensor.matmul(made[i][:, :], w[:, i, :], h3[:, :], start=True, stop=True).then_inc(sem, 1)
                pe.wait_ge(k.rate, it)
                nc.tensor.matmul(made[3][:, :], wb_wide[:, :, :].rearrange("p h d -> p (h d)"), h3[:, :],
                                 start=True, stop=True).then_inc(k.made3, 1)
                pe.wait_ge(k.sq2_0, it + 1)
                nc.tensor.matmul(sums[:, :], g.t("same_head"), sq2[:, 0, :], start=True, stop=True).then_inc(k.sum0, 1)
                pe.wait_ge(k.sq2_1, it + 1)
                pe.wait_ge(k.len0, it + 1)
                nc.tensor.matmul(sums[:, :], g.t("same_head"), sq2[:, 1, :], start=True, stop=True).then_inc(k.sum1, 1)

        @block.scalar
        def _(act):
            act.wait_ge(k.wide, 2)
            act.wait_ge(k.zeroed, 1)
            with act.Fori(0, NCH) as it:
                act.wait_ge(k.centered, it + 1)
                nc.scalar.activation(sq[:, :], mid[:, :], ACT.Square).then_inc(k.squared, 1)
                act.wait_ge(k.unit, it + 1)
                act.wait_ge(k.made3, it)
                for j in range(BPC):
                    last = nc.scalar.activation(h3[:, j * T:(j + 1) * T], unit[:, j * T:(j + 1) * T], ACT.Identity,
                                                scale=g.mod[:, 1, 1, bass.ds(it * BPC + j, 1)],
                                                bias=g.mod[:, 1, 0, bass.ds(it * BPC + j, 1)])
                last.then_inc(k.modulated, 1)
                act.wait_ge(k.conv, CONVS * it)
                act.wait_ge(k.v_done, it)
                act.wait_ge(k.k_done, it)
                act.wait_ge(k.q_done, it)
                for i, (sem, done) in enumerate(((k.made0, k.padded0), (k.made1, k.padded1), (k.made2, k.padded2))):
                    act.wait_ge(sem, it + 1)
                    nc.scalar.activation(pad[:, i, :, LEAD:LEAD + T], made[i][:, :].rearrange("p (b t) -> p b t", t=T),
                                         ACT.Identity, bias=bias[:, i:i + 1])
                    nc.scalar.activation(conv[:, i, :], made[i][:, :], ACT.Identity, scale=taps[:, i, LEAD:CONV],
                                         bias=last_bias[:, i:i + 1]).then_inc(done, 1)
                act.wait_ge(k.made3, it + 1)
                act.wait_ge(k.b_done, it)
                nc.scalar.activation(rate[:, :], made[3][:, :], ACT.Sigmoid, bias=bias[:, 3:4]).then_inc(k.rate, 1)
                for i, sem in ((0, k.sq2_0), (1, k.sq2_1)):
                    act.wait_ge(k.conv, CONVS * it + LEAD * (i + 1))
                    nc.scalar.activation(sq2[:, i, :], conv[:, i, :], ACT.Square).then_inc(sem, 1)
                act.wait_ge(k.conv, CONVS * (it + 1))
                act.wait_ge(k.v_done, it)
                nc.scalar.activation(sig[:, :], conv[:, 2, :], ACT.Sigmoid).then_inc(k.sig, 1)

        @block.vector
        def _(dve):
            nc.vector.memset(pad[:, :, :, 0:LEAD], 0.0).then_inc(k.zeroed, 1)
            dve.wait_ge(k.w_in, 64)
            nc.vector.tensor_copy(wb_wide[:, :, :], wb[:, :, None].to_broadcast([128, H1, DH1])).then_inc(k.wide, 1)
            nc.vector.tensor_tensor(last_bias[:, :], bias[:, 0:3], taps[:, :, LEAD], ALU.mult).then_inc(k.wide, 1)
            with dve.Fori(0, NCH) as it:
                cols = bass.ds(it * CH, CH)
                dve.wait_ge(k.turned, it + 1)
                for j in range(BPC):
                    x = g.xT[:, bass.ds(it * CH + j * T, T)]
                    last = nc.vector.scalar_tensor_tensor(x, turned[:, j * T:(j + 1) * T],
                                                          g.mod[:, 0, 5, bass.ds(it * BPC + j, 1)], x, ALU.mult, ALU.add)
                last.then_inc(k.x_added, 1)
                dve.wait_ge(k.var, it + 1)
                rstd.run(nc, dve, var[:, :], LN_EPS, it)
                dve.wait_ge(k.modulated, it)
                nc.vector.tensor_tensor(unit[:, :], mid[:, :], rstd.out[:, :], ALU.mult).then_inc(k.unit, 1)
                then = Chain(dve, k.conv, CONVS, it)
                for i, sem in ((0, k.padded0), (1, k.padded1), (2, k.padded2)):
                    dve.wait_ge(sem, it + 1)
                    out = conv[:, i, :].rearrange("p (b t) -> p b t", t=T)
                    for tap in range(LEAD):
                        then(nc.vector.scalar_tensor_tensor(out, pad[:, i, :, tap:tap + T], taps[:, i, tap:tap + 1], out,
                                                            ALU.mult, ALU.add))
                dve.wait_ge(k.sum0, it + 1)
                nc.vector.transpose(len_t[:, 0].rearrange("p n i -> p (n i)"), sums[:, :]).then_inc(k.len0, 1)
                dve.wait_ge(k.sum1, it + 1)
                nc.vector.transpose(len_t[:, 1].rearrange("p n i -> p (n i)"), sums[:, :]).then_inc(k.len1, 1)
                dve.wait_ge(k.len0, it + 1)
                dve.wait_ge(k.len1, it + 1)
                STEPS = 5
                then = Chain(dve, k.inv, STEPS, it)
                own = len_t[:, :, :, :].rearrange("p s n (h d) -> p (s n h) d", d=DH1)[:, :, 0]
                flat = lambda a: a[:, :, :, :].rearrange("p s n h -> p (s n h)")
                then(nc.vector.tensor_scalar(root.v[:, :], own, 1e-30, None, ALU.max))
                root.root(nc, dve, it)
                then(nc.vector.tensor_tensor(flat(inv), own, root.y[:, :], ALU.mult))
                then(nc.vector.tensor_scalar(flat(inv), flat(inv), 1e-6, None, ALU.add))
                then(nc.vector.reciprocal(flat(inv), flat(inv)))
                wt = g.t("inv_weight_t")
                then(nc.vector.tensor_tensor(inv[:, 1].rearrange("p (b n) h -> p b n h", b=BPC),
                                             inv[:, 1].rearrange("p (b n) h -> p b n h", b=BPC),
                                             wt[:, None, :, None].to_broadcast([128, BPC, KB, HEADS_IN_BLOCK]), ALU.mult))
                dve.wait_ge(k.x_out, 16 * (it + 1))
                for i, sem in ((0, k.k_done), (1, k.q_done)):
                    nc.vector.tensor_copy(len_t[:, i].rearrange("p n (h d) -> p (n h) d", d=DH1),
                                          inv[:, i].rearrange("p n h -> p (n h)")[:, :, None]
                                          .to_broadcast([128, RC * HEADS_IN_BLOCK, DH1])).then_inc(k.spread, 1)
                    dve.wait_ge(k.spread, 4 * it + 2 * i + 1)
                    nc.vector.transpose(sq2[:, i, :], len_t[:, i].rearrange("p n i -> p (n i)")).then_inc(k.spread, 1)
                    dve.wait_ge(k.spread, 4 * it + 2 * i + 2)
                    nc.vector.tensor_tensor((g.kT, g.qT)[i][:, cols], conv[:, i, :], sq2[:, i, :], ALU.mult).then_inc(sem, 1)

        @block.gpsimd
        def _(pool):
            with pool.Fori(0, NCH) as it:
                cols = bass.ds(it * CH, CH)
                pool.wait_ge(k.sig, it + 1)
                nc.gpsimd.tensor_tensor(sig[:, :], sig[:, :], conv[:, 2, :], ALU.mult).then_inc(k.v_part, 1)
                pool.wait_ge(k.v_part, it + 1)
                pool.wait_ge(k.rate, it + 1)
                nc.gpsimd.tensor_tensor(g.vT[:, cols], sig[:, :], rate[:, :], ALU.mult).then_inc(k.v_done, 1)
                pool.wait_ge(k.k_done, it + 1)
                nc.gpsimd.tensor_tensor(g.bT[:, cols], g.kT[:, cols], rate[:, :], ALU.mult).then_inc(k.b_done, 1)


def delta_phase(nc, dram, g):
    COLS = B * DH1
    HALF = DH1 // 2
    with Scope(nc, "delta") as s:
        wide = s.sb("wide", [128, 2, 3, GT, COLS])
        W = s.sb("W", [128, COLS])
        A = s.sb("A", [128, COLS])
        sW = s.sb("sW", [128, 2, COLS])
        m1 = s.sb("m1", [128, COLS])
        m2 = s.sb("m2", [128, COLS])
        m3 = s.sb("m3", [128, 2, GT // 2, COLS])
        pred = s.sb("pred", [128, B])
        seen = s.sb("seen", [128, 1])
        u = s.sb("u", [128, B])
        ps = [[s.ps(f"ps{a}{i}") for i in range(HALF)] for a in range(2)]
        k = s.sems("zeroed picked0 picked1 evac0 evac1 read0 read1 pred u m2 W scaled A m3_0 m3_1 out0 out1 step")
        picked, evac, m3_done, out_done = ((k.picked0, k.picked1), (k.evac0, k.evac1), (k.m3_0, k.m3_1), (k.out0, k.out1))
        block = s.block()
        BODY = 2 * GT
        BODIES = T // BODY
        QUART = GT // 2
        src = (g.bT, g.kT, g.qT)

        def by_batch(x, first, count):
            return x[:, :].rearrange("p (b t) -> p b t", t=T)[:, :, bass.ds(first, count)]

        @block.tensor
        def _(pe):
            def pick(first, n):
                moving = by_batch(src[n % 3], first, GT)
                for d in range(DH1):
                    last = nc.tensor.matmul(ps[n % 2][d // 2][:, (d % 2) * COLS:(d % 2 + 1) * COLS],
                                            g.t(f"pick{d}"), moving, start=True, stop=True)
                last.then_inc(picked[n % 2], 1)
            for n in range(3):
                if n == 2:
                    pe.wait_ge(evac[0], 1)
                pick(0, n)
            def ahead(i, n):
                pe.wait_ge(evac[n % 2], 3 * i + (n - 2) // 2 + 1)
                pick(i * BODY + GT * (n // 3), n)
            with pe.Fori(0, BODIES - 1) as i:
                for n in range(3, 9):
                    ahead(i, n)
            for n in range(3, 6):
                ahead(BODIES - 1, n)

        @block.scalar
        def _(act):
            def spread(i, n, h, dd):
                to = wide[:, (n // 3) % 2, n % 3].rearrange("p t (b d) -> p d b t", d=DH1)
                return nc.scalar.activation(to[:, 2 * h + dd], ps[n % 2][h][:, dd * COLS:(dd + 1) * COLS]
                                            .rearrange("p (b t) -> p b t", t=GT), ACT.Copy)

            def body(i, halves_ahead):
                for half in range(2):
                    if half in halves_ahead:
                        act.wait_ge(k.m2, BODY * i + GT * half)
                        for par in range(2):
                            act.wait_ge(m3_done[par], GT * i + GT // 2 * half)
                    for t in range(GT):
                        if half in halves_ahead:
                            for piece in range(3 * t, 3 * t + 3):
                                n = 3 + 3 * half + piece // DH1
                                if piece % DH1 == 0:
                                    act.wait_ge(picked[n % 2], 3 * i + n // 2 + 1)
                                ins = spread(i, n, piece % DH1 // 2, piece % 2)
                                if piece % DH1 == DH1 - 1:
                                    ins.then_inc(evac[n % 2], 1)
                        step = BODY * i + GT * half + t
                        act.wait_ge(k.W, step + 1)
                        act.wait_ge(k.A, BODY * i + max(GT * half + t - 1, 0))
                        nc.scalar.activation(sW[:, t % 2, :], W[:, :], ACT.Copy,
                                             scale=g.t("step")[:, bass.ds(step, 1)]).then_inc(k.scaled, 1)
            for n in range(3):
                act.wait_ge(picked[n % 2], n // 2 + 1)
                for piece in range(DH1):
                    last = spread(0, n, piece // 2, piece % 2)
                last.then_inc(evac[n % 2], 1)
            with act.Fori(0, BODIES - 1) as i:
                body(i, (0, 1))
            body(BODIES - 1, (0,))

        @block.vector
        def _(dve):
            nc.vector.memset(W[:, :], 0.0).then_inc(k.zeroed, 1)
            nc.vector.memset(A[:, :], 0.0).then_inc(k.zeroed, 1)
            dve.wait_ge(k.zeroed, 2)
            pairs = lambda ap: ap.rearrange("p (b d) -> p b d", d=DH1)

            def outputs(i, quarter):
                nc.vector.tensor_reduce(by_batch(g.vT, i * BODY + QUART * quarter, QUART).rearrange("p b t -> p t b"),
                                        m3[:, quarter % 2, :, :].rearrange("p t (b d) -> p t b d", d=DH1), AX.X, ALU.add)\
                    .then_inc(out_done[quarter % 2], 1)

            def products(i, quarter):
                dve.wait_ge(m3_done[quarter % 2], GT * i + QUART * (quarter // 2 + 1))
            with dve.Fori(0, BODIES) as i:
                for half in range(2):
                    for a in range(2):
                        dve.wait_ge(evac[a], 3 * i + (3 if half else 2 - a))
                    for t in range(GT):
                        step = BODY * i + GT * half + t
                        quarter = (GT * half + t) // QUART
                        sums = t % QUART == QUART - 1 and quarter > 0
                        if sums:
                            products(i, quarter - 1)
                        nc.vector.tensor_tensor(m1[:, :], W[:, :], wide[:, half, 0, t, :], ALU.mult).then_inc(k.step, 1)
                        if sums:
                            outputs(i, quarter - 1)
                        dve.wait_ge(k.step, step + 1)
                        nc.vector.tensor_reduce(pred[:, :], pairs(m1[:, :]), AX.X, ALU.add).then_inc(k.pred, 1)
                        dve.wait_ge(k.pred, step + 1)
                        v = by_batch(g.vT, step, 1)[:, :, 0]
                        nc.vector.tensor_tensor(u[:, :], v, pred[:, :], ALU.subtract).then_inc(k.u, 1)
                        dve.wait_ge(k.u, step + 1)
                        nc.vector.tensor_tensor(pairs(m2[:, :]), pairs(wide[:, half, 1, t, :]),
                                                u[:, :, None].to_broadcast([128, B, DH1]), ALU.mult).then_inc(k.m2, 1)
                        dve.wait_ge(k.m2, step + 1)
                        dve.wait_ge(k.scaled, step)
                        nc.vector.tensor_tensor(W[:, :], W[:, :], m2[:, :], ALU.add).then_inc(k.W, 1)
                        dve.wait_ge(k.W, step + 1)
                products(i, 3)
                nc.vector.tensor_copy(seen[:, :], m3[:, 1, 0, 0:1])
                outputs(i, 3)

        @block.gpsimd
        def _(pool):
            pool.wait_ge(k.zeroed, 2)
            with pool.Fori(0, BODIES) as i:
                for t in range(BODY):
                    step = BODY * i + t
                    par, place = t // QUART % 2, t % QUART
                    if place == 0:
                        pool.wait_ge(out_done[par], 2 * i + t // GT)
                    pool.wait_ge(k.scaled, step + 1)
                    if place:
                        pool.wait_ge(m3_done[par], GT * i + QUART * (t // GT) + place)
                    else:
                        pool.wait_ge(m3_done[1 - par], GT * i + QUART * ((t + QUART) // GT))
                    nc.gpsimd.tensor_tensor(A[:, :], A[:, :], sW[:, t % 2, :], ALU.add).then_inc(k.A, 1)
                    pool.wait_ge(k.A, step + 1)
                    nc.gpsimd.tensor_tensor(m3[:, par, place, :], A[:, :], wide[:, t // GT, 2, t % GT, :], ALU.mult)\
                        .then_inc(m3_done[par], 1)


def mix_phase(nc, dram, g):
    HEADS_IN_BLOCK = SLOT // DH1
    with Scope(nc, "mix") as s:
        w_out = s.sb("w_out", [128, D])
        router = s.sb("router", [128, E1])
        per_channel = s.sb("per_channel", [128, 3])
        sq = s.sb("sq", [128, 3, CH])
        ms = s.sb("ms", [128, RC, SLOT])
        scale = s.sb("scale", [128, CH])
        on = s.sb("on", [128, CH])
        mixed = s.sb("mixed", [128, CH])
        unit = s.sb("unit", [128, CH])
        h4 = s.sb("h4", [128, CH])
        xn = s.sb("xn", [128, CH])
        score = s.sb("score", [128, TILES, E1])
        top = s.sb("top", [128, TILES, 8])
        top_at = s.sb("top_at", [128, TILES, 8], U32)
        chosen = s.sb("chosen", [128, TILES, K1])
        onehot = s.sb("onehot", [128, TILES, E1, K1])
        mask = s.sb("mask", [128, TILES, E1])
        less = s.sb("less", [128, TILES, E1])
        ex = s.sb("ex", [128, TILES, E1])
        total = s.sb("total", [128, TILES])
        seen = s.sb("seen", [128, 2])
        gates = s.sb("gates", [128, TILES, E1])
        head_root = Rstd(s, "head", RC * HEADS_IN_BLOCK, parts=False)
        rstd = [Rstd(s, f"rstd{i}") for i in range(2)]
        heads, out_ps, mid, var, rms, logits, turned = (s.ps(n) for n in
            ("heads", "out_ps", "mid", "var", "rms", "logits", "turned"))
        k = s.sems("w_in w_ready x_in sq0 heads head_read head_steps on out_made mixed x_added centered squared var unit"
                   " modulated sq2 rms xn logits score route exp gates turned gates_out skipped xn_copied")
        block = s.block()
        STEPS = 14

        @block.sync
        def _(sp):
            for dst, name in ((w_out[:, :], "w1_out"), (router[:, :], "router"), (per_channel[:, :], "cols1")):
                sp.dma_start(dst, dram[name]).then_inc(k.w_in, 16)
            sp.dma_start(g.keptT[:, :], g.x_kept).then_inc(k.x_in, 16)

        @block.tensor
        def _(pe):
            pe.wait_ge(k.w_ready, 1)
            pe.wait_ge(k.x_in, 16)
            with pe.Fori(0, NCH) as it:
                cols = bass.ds(it * CH, CH)
                pe.wait_ge(k.sq0, it + 1)
                pe.wait_ge(k.head_read, it)
                nc.tensor.matmul(heads[:, :], g.t("same_head"), sq[:, 0, :], start=True, stop=True).then_inc(k.heads, 1)
                pe.wait_ge(k.on, it + 1)
                pe.wait_ge(k.mixed, it)
                nc.tensor.matmul(out_ps[:, :], w_out[:, :], on[:, :], start=True, stop=True).then_inc(k.out_made, 1)
                pe.wait_ge(k.x_added, it + 1)
                pe.wait_ge(k.unit, it)
                nc.tensor.matmul(mid[:, :], g.t("center"), g.keptT[:, cols], start=True, stop=True).then_inc(k.centered, 1)
                pe.wait_ge(k.squared, it + 1)
                nc.tensor.matmul(var[:, :], g.t("mean"), sq[:, 1, :], start=True, stop=True).then_inc(k.var, 1)
                pe.wait_ge(k.sq2, it + 1)
                nc.tensor.matmul(rms[:, :], g.t("mean"), sq[:, 2, :], start=True, stop=True).then_inc(k.rms, 1)
                pe.wait_ge(k.xn, it + 1)
                pe.wait_ge(k.score, it)
                for j in range(TILES):
                    last = nc.tensor.matmul(logits[:, j * E1:(j + 1) * E1], xn[:, 128 * j:128 * j + 128], router[:, :],
                                            start=True, stop=True)
                last.then_inc(k.logits, 1)
                pe.wait_ge(k.gates, it + 1)
                pe.wait_ge(k.gates_out, it)
                for j in range(TILES):
                    last = nc.tensor.transpose(turned[0:E1, 128 * j:128 * j + 128], gates[:, j, :], g.t("ident"))
                last.then_inc(k.turned, 1)

        @block.scalar
        def _(act):
            act.wait_ge(k.w_in, 48)
            with act.Fori(0, NCH) as it:
                cols = bass.ds(it * CH, CH)
                nc.scalar.activation(sq[:, 0, :], g.vT[:, cols], ACT.Square).then_inc(k.sq0, 1)
                act.wait_ge(k.out_made, it + 1)
                nc.scalar.activation(mixed[:, :], out_ps[:, :], ACT.Identity, bias=per_channel[:, 1:2]).then_inc(k.mixed, 1)
                act.wait_ge(k.centered, it + 1)
                nc.scalar.activation(sq[:, 1, :], mid[:, :], ACT.Square).then_inc(k.squared, 1)
                act.wait_ge(k.unit, it + 1)
                act.wait_ge(k.skipped, it)
                for j in range(BPC):
                    last = nc.scalar.activation(h4[:, j * T:(j + 1) * T], unit[:, j * T:(j + 1) * T], ACT.Identity,
                                                scale=g.mod[:, 1, 4, bass.ds(it * BPC + j, 1)],
                                                bias=g.mod[:, 1, 3, bass.ds(it * BPC + j, 1)])
                last.then_inc(k.modulated, 1)
                act.wait_ge(k.modulated, it + 1)
                nc.scalar.activation(sq[:, 2, :], h4[:, :], ACT.Square).then_inc(k.sq2, 1)
                act.wait_ge(k.xn, it + 1)
                nc.scalar.activation(g.normT[:, cols], xn[:, :], ACT.Copy).then_inc(k.xn_copied, 1)
                act.wait_ge(k.logits, it + 1)
                nc.scalar.activation(score[:, :, :].rearrange("p j e -> p (j e)"), logits[:, 0:TILES * E1], ACT.Copy)\
                    .then_inc(k.score, 1)
                act.wait_ge(k.route, STEPS * it + 2 * TILES)
                nc.scalar.activation(ex[:, :, :], less[:, :, :], ACT.Exp).then_inc(k.exp, 1)
                act.wait_ge(k.turned, it + 1)
                nc.scalar.activation(g.gatesT[:, cols], turned[0:E1, :], ACT.Copy).then_inc(k.gates_out, 1)

        @block.vector
        def _(dve):
            dve.wait_ge(k.w_in, 48)
            nc.vector.tensor_scalar(w_out[:, :], w_out[:, :], per_channel[:, 0:1], None, ALU.mult).then_inc(k.w_ready, 1)
            dve.wait_ge(k.x_in, 16)
            with dve.Fori(0, NCH) as it:
                cols = bass.ds(it * CH, CH)
                dve.wait_ge(k.heads, it + 1)
                nc.vector.transpose(ms[:, :, :].rearrange("p n i -> p (n i)"), heads[:, :]).then_inc(k.head_read, 1)
                dve.wait_ge(k.head_read, it + 1)
                then = Chain(dve, k.head_steps, 3, it)
                by_head = ms[:, :, :].rearrange("p n (h d) -> p (n h) d", d=DH1)
                then(nc.vector.tensor_scalar(head_root.v[:, :], by_head[:, :, 0], 1.0 / DH1, RMS_EPS, ALU.mult, ALU.add))
                head_root.root(nc, dve, it)
                then(nc.vector.tensor_copy(by_head, head_root.y[:, :, None].to_broadcast([128, RC * HEADS_IN_BLOCK, DH1])))
                then(nc.vector.transpose(scale[:, :], ms[:, :, :].rearrange("p n i -> p (n i)")))
                nc.vector.tensor_tensor(on[:, :], g.vT[:, cols], scale[:, :], ALU.mult).then_inc(k.on, 1)
                dve.wait_ge(k.mixed, it + 1)
                for j in range(BPC):
                    x = g.keptT[:, bass.ds(it * CH + j * T, T)]
                    last = nc.vector.scalar_tensor_tensor(x, mixed[:, j * T:(j + 1) * T],
                                                          g.mod[:, 1, 2, bass.ds(it * BPC + j, 1)], x, ALU.mult, ALU.add)
                last.then_inc(k.x_added, 1)
                dve.wait_ge(k.var, it + 1)
                rstd[0].run(nc, dve, var[:, :], LN_EPS, it)
                dve.wait_ge(k.modulated, it)
                nc.vector.tensor_tensor(unit[:, :], mid[:, :], rstd[0].out[:, :], ALU.mult).then_inc(k.unit, 1)
                dve.wait_ge(k.rms, it + 1)
                rstd[1].run(nc, dve, rms[:, :], RMS_EPS, it)
                dve.wait_ge(k.xn_copied, it)
                dve.wait_ge(k.logits, it)
                nc.vector.scalar_tensor_tensor(xn[:, :], h4[:, :], per_channel[:, 2:3], rstd[1].out[:, :],
                                               ALU.mult, ALU.mult).then_inc(k.xn, 1)
                dve.wait_ge(k.centered, it + 1)
                for j in range(BPC):
                    x = g.keptT[:, bass.ds(it * CH + j * T, T)]
                    last = nc.vector.scalar_tensor_tensor(x, h4[:, j * T:(j + 1) * T],
                                                          g.mod[:, 1, 5, bass.ds(it * BPC + j, 1)], x, ALU.mult, ALU.add)
                last.then_inc(k.skipped, 1)
                dve.wait_ge(k.score, it + 1)
                nc.vector.tensor_copy(seen[:, 0:1], score[:, 0, 0:1])
                then = Chain(dve, k.route, STEPS, it)
                for j in range(TILES):
                    then(nc.vector.max(top[:, j, :], score[:, j, :]), wait=j == TILES - 1)
                nc.vector.tensor_copy(seen[:, 1:2], top[:, 0, 0:1])
                for j in range(TILES - 1):
                    then(nc.vector.max_index(top_at[:, j, :], top[:, j, :], score[:, j, :]), wait=False)
                j = TILES - 1
                nc.vector.max_index(top_at[:, j, :], top[:, j, :], score[:, j, :])
                then(nc.vector.tensor_tensor(less[:, :, :], score[:, :, :], top[:, :, 0:1].to_broadcast([128, TILES, E1]),
                                             ALU.subtract))
                then(nc.vector.tensor_copy(chosen[:, :, :], top_at[:, :, 0:K1]))
                then(nc.vector.tensor_tensor(onehot[:, :, :, :], g.t("iota")[:, None, 0:E1, None]
                                             .to_broadcast([128, TILES, E1, K1]),
                                             chosen[:, :, None, :].to_broadcast([128, TILES, E1, K1]), ALU.is_equal))
                then(nc.vector.tensor_reduce(mask[:, :, :], onehot[:, :, :, :], AX.X, ALU.add))
                dve.wait_ge(k.exp, it + 1)
                then(nc.vector.tensor_tensor(mask[:, :, :], mask[:, :, :], ex[:, :, :], ALU.mult))
                then(nc.vector.tensor_reduce(total[:, :], ex[:, :, :], AX.X, ALU.add))
                then(nc.vector.reciprocal(total[:, :], total[:, :]))
                nc.vector.tensor_tensor(gates[:, :, :], mask[:, :, :], total[:, :, None].to_broadcast([128, TILES, E1]),
                                        ALU.mult).then_inc(k.gates, 1)


def ffn_phase(nc, dram, g, out):
    P = len(HC)
    with Scope(nc, "ffn") as s:
        w_up = s.sb("w_up", [128, E1, 2 * HID])
        w_down = s.sb("w_down", [128, E1, P, D])
        xs = s.sb("xs", [128, 2, CH])
        sg = s.sb("sg", [128, P, CH])
        hid = s.sb("hid", [128, 2, P, CH])
        y = s.sb("y", [128, CH])
        rows = s.sb("rows", [128, TILES, D])
        gates_ps = s.ps("gates")
        acc = s.ps("acc")
        val = [s.ps(f"val{p}") for p in range(P)]
        gate = [s.ps(f"gate{p}") for p in range(P)]
        k = s.sems("w_in spread xs val0 val1 val2 gate0 gate1 gate2 sg0 sg1 sg2 hid0 hid1 hid2 down acc y turned rows out")
        val_made, gate_made = (k.val0, k.val1, k.val2), (k.gate0, k.gate1, k.gate2)
        sg_made, hid_made = (k.sg0, k.sg1, k.sg2), (k.hid0, k.hid1, k.hid2)
        block = s.block()
        out_rows = out.rearrange("b t c -> (b t) c")

        @block.sync
        def _(sp):
            sp.dma_start(w_up[:, :, :], dram["w_up"]).then_inc(k.w_in, 16)
            sp.dma_start(w_down[:, :, :, :], dram["w_down"]).then_inc(k.w_in, 16)
            with sp.Fori(0, NCH) as it:
                sp.wait_ge(k.rows, it + 1)
                sp.dma_start(out_rows[bass.ds(it * CH, CH), :].rearrange("(r p) c -> p r c", p=128), rows[:, :, :])\
                    .then_inc(k.out, 16)
            sp.wait_ge(k.out, 16 * NCH)

        @block.tensor
        def _(pe):
            pe.wait_ge(k.w_in, 32)
            with pe.Fori(0, NCH) as it:
                cols = bass.ds(it * CH, CH)

                def spread(e):
                    nc.tensor.matmul(gates_ps[:, :], g.t("ident")[0:E1, e:e + 1].to_broadcast([E1, 128]),
                                     g.gatesT[:, cols], start=True, stop=True).then_inc(k.spread, 1)

                def down(e):
                    if e == 0:
                        pe.wait_ge(k.y, it)
                    for p, (at, size) in enumerate(HC):
                        pe.wait_ge(hid_made[p], E1 * it + e + 1)
                        last = nc.tensor.matmul(acc[:, :], w_down[0:size, e, p, :], hid[0:size, e % 2, p, :],
                                                start=e == 0 and p == 0, stop=e == E1 - 1 and p == P - 1)
                    last.then_inc(k.down, 1)
                for e in range(E1):
                    for p, (at, size) in enumerate(HC):
                        pe.wait_ge(sg_made[p], E1 * it + e)
                        if e == 0 and p == 1:
                            pe.wait_ge(k.rows, it)
                        nc.tensor.matmul(gate[p][0:size, :], w_up[:, e, HID + at:HID + at + size], g.normT[:, cols],
                                         start=True, stop=True).then_inc(gate_made[p], 1)
                        if e == 0 and p == 1:
                            spread(0)
                    if e:
                        down(e - 1)
                    pe.wait_ge(k.xs, E1 * it + e + 1)
                    for p, (at, size) in enumerate(HC):
                        pe.wait_ge(hid_made[p], E1 * it + e)
                        nc.tensor.matmul(val[p][0:size, :], w_up[:, e, at:at + size], xs[:, e % 2, :],
                                         start=True, stop=True).then_inc(val_made[p], 1)
                    if e < E1 - 1:
                        spread(e + 1)
                down(E1 - 1)
                pe.wait_ge(k.y, it + 1)
                for r in range(TILES):
                    last = nc.tensor.transpose(gates_ps[:, 128 * r:128 * r + 128], y[:, 128 * r:128 * r + 128], g.t("ident"))
                last.then_inc(k.turned, 1)

        @block.scalar
        def _(act):
            with act.Fori(0, NCH) as it:
                for e in range(E1):
                    for p, (at, size) in enumerate(HC):
                        act.wait_ge(gate_made[p], E1 * it + e + 1)
                        act.wait_ge(hid_made[p], E1 * it + e)
                        nc.scalar.activation(sg[0:size, p, :], gate[p][0:size, :], ACT.Silu).then_inc(sg_made[p], 1)
                act.wait_ge(k.turned, it + 1)
                act.wait_ge(k.out, 16 * it)
                nc.scalar.activation(rows[:, :, :], gates_ps[:, :].rearrange("p (r c) -> p r c", c=D), ACT.Copy)\
                    .then_inc(k.rows, 1)

        @block.vector
        def _(dve):
            with dve.Fori(0, NCH) as it:
                cols = bass.ds(it * CH, CH)
                for e in range(E1):
                    dve.wait_ge(val_made[P - 1], E1 * it + max(e - 1, 0))
                    dve.wait_ge(k.spread, E1 * it + e + 1)
                    nc.vector.tensor_tensor(xs[:, e % 2, :], g.normT[:, cols], gates_ps[:, :], ALU.mult).then_inc(k.xs, 1)
                    dve.wait_ge(k.down, E1 * it + max(e - 1, 0))
                    for p, (at, size) in enumerate(HC):
                        dve.wait_ge(val_made[p], E1 * it + e + 1)
                        dve.wait_ge(sg_made[p], E1 * it + e + 1)
                        nc.vector.tensor_tensor(hid[0:size, e % 2, p, :], sg[0:size, p, :], val[p][0:size, :], ALU.mult)\
                            .then_inc(hid_made[p], 1)
                dve.wait_ge(k.down, E1 * (it + 1))
                dve.wait_ge(k.turned, it)
                for j in range(BPC):
                    last = nc.vector.scalar_tensor_tensor(y[:, j * T:(j + 1) * T], acc[:, j * T:(j + 1) * T],
                                                          g.mod[:, 1, 5, bass.ds(it * BPC + j, 1)],
                                                          g.keptT[:, bass.ds(it * CH + j * T, T)], ALU.mult, ALU.add)
                last.then_inc(k.y, 1)


def launch_arrays(inputs):
    a = {k: np.asarray(v) for k, v in inputs.items()}
    out = {}
    f, bf = constants()
    out["tables"] = np.concatenate(list(f.values()), 1)
    out["tables_bf"] = np.concatenate(list(bf.values()), 1)
    out["x"] = a["L0_attn_x"]
    for layer in range(2):
        out[f"c{layer}"] = a[f"L{layer}_c"].T
        out[f"wmod{layer}"] = a[f"L{layer}_wmod"]
    out["ln"] = np.stack([a["L0_attn_ln_g"], a["L0_attn_ln_b"]], 1)

    def slots(w):
        z = np.zeros((H0, SLOT) + w.shape[1:], w.dtype)
        z[:, :DH0] = w.reshape((H0, DH0) + w.shape[1:])
        return z.reshape((GROUPS, PER * SLOT) + w.shape[1:])
    half = DH0 // 2
    turn = np.concatenate([np.arange(half, DH0), np.arange(half)])
    turned = lambda w: w.reshape(H0, DH0, D)[:, turn].reshape(D, D)
    wq, wk, wv = (a[f"L0_attn_W{n}"] for n in "qkv")
    out["w_attn"] = np.stack([slots(w).transpose(2, 0, 1) for w in (wq, turned(wq), wk, turned(wk), wv)], 1)
    out["wo"] = slots(a["L0_attn_Wo"].T).transpose(1, 0, 2)
    dirs = np.zeros((GROUPS, PER, SLOT, PER, SLOT), np.float32)
    for gr in range(GROUPS):
        for h in range(PER):
            for r in range(2):
                dirs[gr, h, :GEO_D, h, 2 * gr + r] = a["L0_attn_head_dirs"][gr * PER + h]
    out["dirs"] = dirs.reshape(GROUPS, 128, 128).transpose(1, 0, 2)
    out["hs"] = np.repeat(a["L0_attn_head_scales"].reshape(GROUPS, PER), SLOT, 1).T
    out["gate_w"] = a["L0_ffn_gate_w"].T
    out["gate_bias"] = a["L0_ffn_bias"][None, :]
    out["sw13"] = np.stack([a["L0_ffn_sw1"].T, a["L0_ffn_sw3"].T], 1)
    out["sw2"] = a["L0_ffn_sw2"].T
    out["w13"] = np.concatenate([a["L0_ffn_W1"], a["L0_ffn_W3"]], 2).transpose(1, 0, 2)
    out["w2"] = a["L0_ffn_W2"].transpose(1, 0, 2)
    out["w1_qkv"] = np.stack([a[f"L1_attn_W{n}"].T for n in "kqv"], 1)
    out["w_beta"] = a["L1_attn_Wbeta"].T
    out["b1"] = np.stack([a[f"L1_attn_b{n}"] for n in "kqv"] + [np.repeat(a["L1_attn_bbeta"], DH1)], 1)
    out["taps"] = np.stack([a[f"L1_attn_conv_{n}"] for n in "kqv"], 1)
    out["w1_out"] = a["L1_attn_Wout"].T
    out["cols1"] = np.stack([np.tile(a["L1_attn_rms_w"], H1), a["L1_attn_bout"], a["L1_ffn_norm_scale"]], 1)
    out["router"] = a["L1_ffn_w_router"].T
    out["w_up"] = a["L1_ffn_w_up"].transpose(2, 0, 1)
    down = np.zeros((E1, len(HC) * 128, D), np.float32)
    down[:, :HID] = a["L1_ffn_w_down"].transpose(0, 2, 1)
    out["w_down"] = down.reshape(E1, len(HC), 128, D).transpose(2, 0, 1, 3)
    return {k: np.ascontiguousarray(v) for k, v in out.items()}


def build(nc, dram, out):
    f, bf = constants()
    cols, nf = table_columns(f)
    cols_bf, nb = table_columns(bf)
    with ExitStack() as ctx:
        g = Shared()
        g.tab = ctx.enter_context(nc.sbuf_tensor("tables_sb", [128, nf], F32))
        g.tab_bf = ctx.enter_context(nc.sbuf_tensor("tables_bf_sb", [128, nb], BF16))

        def t(name):
            if name in cols:
                return g.tab[:, cols[name][0]:cols[name][1]]
            return g.tab_bf[:, cols_bf[name][0]:cols_bf[name][1]]
        g.t = t
        g.mod = ctx.enter_context(nc.sbuf_tensor("mod", [128, 2, 6, B], F32))
        g.xT = ctx.enter_context(nc.sbuf_tensor("xT", [128, N], F32))
        g.hT = ctx.enter_context(nc.sbuf_tensor("hT", [128, N], F32))
        g.xnT = ctx.enter_context(nc.sbuf_tensor("xnT", [128, N], F32))
        g.slot_token = ctx.enter_context(nc.sbuf_tensor("slot_token", [128, E0], U32))
        g.rows = nc.dram_tensor("rows", (N + CAP, ROW), F32, kind="Internal").ap()
        g.acc = nc.dram_tensor("acc", (N + CAP, D), F32, kind="Internal").ap()
        g.x_kept = nc.dram_tensor("x_kept", (128, N), F32, kind="Internal").ap()
        setup_phase(nc, dram, g)
        load_phase(nc, dram, g)
        attention_phase(nc, dram, g)
        route_phase(nc, dram, g)
        experts_phase(nc, dram, g)
        g.kT, g.qT, g.vT = g.xT, g.hT, g.xnT
        rates = ctx.enter_context(ExitStack())
        g.bT = rates.enter_context(nc.sbuf_tensor("bT", [128, N], F32))
        project_phase(nc, dram, g)
        delta_phase(nc, dram, g)
        rates.close()
        g.keptT, g.normT = g.xT, g.hT
        g.gatesT = ctx.enter_context(nc.sbuf_tensor("gatesT", [E1, N], F32))
        mix_phase(nc, dram, g)
        ffn_phase(nc, dram, g, out)


def kernel(**inputs):
    import concourse.bacc as bacc
    from concourse.bass_utils import run_bass_kernel_spmd

    nc = bacc.Bacc("TRN2", target_bir_lowering=False, num_devices=1)
    arrays = {f"in_{name}": a for name, a in launch_arrays(inputs).items()}
    dram = {name[3:]: nc.dram_tensor(name, a.shape, mybir.dt.from_np(a.dtype), kind="ExternalInput").ap()
            for name, a in arrays.items()}
    out = nc.dram_tensor("out", (B, T, D), F32, kind="ExternalOutput").ap()
    build(nc, dram, out)
    return run_bass_kernel_spmd(nc, [arrays], core_ids=[0]).results[0]["out"]
```

```python
from contextlib import ExitStack

import numpy as np

import concourse.bass as bass
from concourse import mybir

F32 = mybir.dt.float32
BF16 = mybir.dt.bfloat16
U32 = mybir.dt.uint32
ALU = mybir.AluOpType
ACT = mybir.ActivationFunctionType
AX = mybir.AxisListType

B, T, D = 32, 256, 128
N = B * T
LN_EPS = 1e-5
RMS_EPS = 1e-6
CH = 512
NCH = N // CH
BPC = CH // T

H0, DH0 = 8, 16
GROUPS, PER = 2, 4
SLOT = 32
KB = T // SLOT
NEG = -1e30
SCALE0 = 1.0 / DH0 ** 0.5
GEO_D = 3
E0, I0, K0, CAP = 32, 64, 4, 2 * 512 * 4 // 32
H1, DH1, CONV = 16, 8, 4
E1, HID, K1 = 8, 352, 2
HC = [(0, 128), (128, 128), (256, 96)]


def constants():
    p = np.arange(128)
    quad, slot = p // SLOT, p % SLOT
    f = {}
    f["ident"] = np.eye(128)
    f["center"] = np.eye(128) - 1.0 / 128
    f["mean"] = np.full((128, 128), 1.0 / 128)
    half = DH0 // 2
    inv = (1.0 / np.float32(10000.0) ** (np.arange(0, DH0, 2, dtype=np.float32) / np.float32(DH0))).astype(np.float32)
    freqs = np.outer(np.arange(T, dtype=np.float32), inv).astype(np.float32).astype(np.float64)
    cos, sin = np.zeros((128, T)), np.zeros((128, T))
    for i in range(128):
        if slot[i] < DH0:
            cos[i] = np.cos(freqs[:, slot[i] % half])
            sin[i] = np.sin(freqs[:, slot[i] % half]) * (-1 if slot[i] < half else 1)
    f["cos"], f["sin"] = cos, sin
    f["own_head"] = quad[:, None] == np.arange(PER)[None, :]
    f["own_head_scaled"] = SCALE0 * f["own_head"]
    f["mask_own"] = np.where(slot[:, None] < np.arange(SLOT)[None, :], NEG, 0.0)
    h = p // DH1
    f["same_head"] = h[:, None] == h[None, :]
    for d in range(DH1):
        f[f"pick{d}"] = (h[:, None] == h[None, :]) & (p % DH1 == d)[:, None]
    t = np.arange(1, T + 1, dtype=np.float64)
    f["step"] = np.broadcast_to(t, (128, T))
    at = SLOT * np.arange(KB)[None, :] + slot[:, None] + 1.0
    f["inv_weight_t"] = 1.0 / (at * (at + 1) / 2)
    f["before"] = p[:, None] < p[None, :]
    f["ones"] = np.ones((128, 128))
    f["iota"] = np.broadcast_to(p.astype(np.float64), (128, 128))
    f["row_no"] = p[:, None]
    f["tile_no"] = np.broadcast_to(np.arange(N // 128, dtype=np.float64), (128, N // 128))
    f["past"] = N + p[:, None]
    f = {k: np.ascontiguousarray(v, dtype=np.float32) for k, v in f.items()}
    b = {}
    b["ident_bf"] = np.eye(128)
    late = slot[:, None] < np.arange(2 * SLOT)[None, :]
    b["mask_max"] = np.where(late, NEG, 0.0)
    b = {k: np.ascontiguousarray(v, dtype=np.float32) for k, v in b.items()}
    return f, b


def table_columns(tables):
    at, out = 0, {}
    for k, v in tables.items():
        out[k] = (at, at + v.shape[1])
        at += v.shape[1]
    return out, at


class Named(dict):

    def __getattr__(self, name):
        return self[name]


class Shared:
    pass


class Scope(ExitStack):

    def __init__(self, nc, name):
        super().__init__()
        self.nc, self.name, self.taken = nc, name, []

    def sb(self, name, shape, dt=F32):
        return self.enter_context(self.nc.sbuf_tensor(f"{self.name}_{name}", shape, dt))

    def ps(self, name, shape=(128, 512), dt=F32):
        return self.enter_context(self.nc.psum_tensor(f"{self.name}_{name}", list(shape), dt))

    def sems(self, names, tag=""):
        made = {n: self.nc.alloc_semaphore(f"{self.name}_{n}{tag}") for n in names.split()}
        self.taken += made.values()
        return Named(made)

    def __exit__(self, *exc):
        super().__exit__(*exc)
        if exc[0] is None:
            self.nc.clear_and_free_semaphores(self.taken)
            self.nc.all_engine_barrier()

    def block(self):
        return self.enter_context(self.nc.Block())


def setup_phase(nc, dram, g):
    with Scope(nc, "setup") as s:
        c_sb = s.sb("c", [128, 2, B])
        silu = s.sb("silu", [128, 2, B])
        wmod = s.sb("wmod", [128, 2, 6 * 128])
        absv = s.sb("absv", [128, 2, 2, B])
        sign = s.sb("sign", [128, 2, 2, B])
        tab_f = s.sb("tab_f", g.tab_bf.shape)
        ps = s.ps("mod", (128, 2, 6, B))
        k = s.sems("tables_in tab_bf weights_in silu_done mod_done mod_read raw_gates abs_done sign_done sign_scaled")
        block = s.block()

        @block.sync
        def _(sp):
            sp.dma_start(c_sb[:, 0, :], dram["c0"]).then_inc(k.weights_in, 16)
            sp.dma_start(c_sb[:, 1, :], dram["c1"]).then_inc(k.weights_in, 16)
            sp.dma_start(wmod[:, 0, :], dram["wmod0"]).then_inc(k.weights_in, 16)
            sp.dma_start(wmod[:, 1, :], dram["wmod1"]).then_inc(k.weights_in, 16)
            sp.dma_start(g.tab[:, :], dram["tables"]).then_inc(k.tables_in, 16)
            sp.dma_start(tab_f[:, :], dram["tables_bf"]).then_inc(k.tables_in, 16)
            sp.wait_ge(k.tables_in, 32)

        @block.scalar
        def _(act):
            act.wait_ge(k.weights_in, 64)
            nc.scalar.activation(silu[:, :, :], c_sb[:, :, :], ACT.Silu).then_inc(k.silu_done, 1)

        @block.tensor
        def _(pe):
            pe.wait_ge(k.silu_done, 1)
            for layer in range(2):
                for j in range(6):
                    last = nc.tensor.matmul(ps[:, layer, j, :], wmod[:, layer, 128 * j:128 * j + 128],
                                            silu[:, layer, :], start=True, stop=True)
            last.then_inc(k.mod_done, 1)

        @block.vector
        def _(dve):
            dve.wait_ge(k.tables_in, 32)
            nc.vector.tensor_copy(g.tab_bf[:, :], tab_f[:, :]).then_inc(k.tab_bf, 1)
            dve.wait_ge(k.mod_done, 1)
            nc.vector.tensor_copy(g.mod[:, :, :, :], ps[:, :, :, :]).then_inc(k.mod_read, 1)
            dve.wait_ge(k.mod_read, 1)
            for layer in range(2):
                for half in range(2):
                    nc.vector.tensor_scalar(g.mod[:, layer, 3 * half + 1, :], g.mod[:, layer, 3 * half + 1, :],
                                            1.0, None, ALU.add)
                    gate = g.mod[:, layer, 3 * half + 2, :]
                    nc.vector.scalar_tensor_tensor(absv[:, layer, half, :], gate, -1.0, gate, ALU.mult, ALU.max)\
                        .then_inc(k.abs_done, 1)
                    nc.vector.tensor_scalar(sign[:, layer, half, :], gate, 0.0, 2.0, ALU.is_ge, ALU.mult)\
                        .then_inc(k.sign_done, 1)
            dve.wait_ge(k.sign_done, 4)
            nc.vector.tensor_scalar(sign[:, :, :, :], sign[:, :, :, :], -1.0, None, ALU.add).then_inc(k.sign_scaled, 1)
            dve.wait_ge(k.sign_scaled, 1)
            dve.wait_ge(k.abs_done, 4)
            for layer in range(2):
                for half in range(2):
                    nc.vector.scalar_tensor_tensor(g.mod[:, layer, 3 * half + 2, :], absv[:, layer, half, :], 0.25,
                                                   sign[:, layer, half, :], ALU.max, ALU.mult)


RC = CH // SLOT


class Rstd:
    STEPS = 3
    MAGIC = float(0x5F3759DF)

    def __init__(self, s, name, count=RC, parts=True, room=None):
        if room is not None:
            self.turned, self.out = room[0].rearrange("p (n i) -> p n i", i=SLOT), room[1]
        elif parts:
            self.turned = s.sb(f"{name}_turned", [128, count, SLOT])
            self.out = s.sb(f"{name}_out", [128, count * SLOT])
        self.v = s.sb(f"{name}_v", [128, count])
        self.y = s.sb(f"{name}_y", [128, count])
        self.t = s.sb(f"{name}_t", [128, count])
        self.count = count
        s.sems(f"{name}_turn {name}_v {name}_guess {name}_newton {name}_out")
        self.turn_done, self.v_done, self.guess_done, self.newton_done, self.out_done = s.taken[-5:]

    def run(self, nc, dve, psum, eps, it):
        run_roots(nc, dve, [self], [psum], eps, it)

    def root(self, nc, dve, it):
        newton_roots(nc, dve, [self], it)


def run_roots(nc, dve, group, psums, eps, it, made=None):
    for n, (r, psum) in enumerate(zip(group, psums)):
        if made:
            dve.wait_ge(made[n], it + 1)
        nc.vector.transpose(r.turned[:, :, :].rearrange("p n i -> p (n i)"), psum).then_inc(r.turn_done, 1)
    for r in group:
        dve.wait_ge(r.turn_done, it + 1)
        nc.vector.tensor_scalar(r.v[:, :], r.turned[:, :, 0], eps, None, ALU.add).then_inc(r.v_done, 1)
    for r in group:
        dve.wait_ge(r.v_done, it + 1)
    newton_roots(nc, dve, group, it)
    for r in group:
        nc.vector.transpose(r.out[:, :].rearrange("p (n i) -> p n i", i=SLOT),
                            r.y[:, :, None].to_broadcast([128, r.count, SLOT])).then_inc(r.out_done, 1)
    for r in group:
        dve.wait_ge(r.out_done, it + 1)


def newton_roots(nc, dve, group, it):
    for r in group:
        nc.vector.tensor_scalar(r.y[:, :].bitcast(mybir.dt.int32), r.v[:, :].bitcast(mybir.dt.int32),
                                -0.5, Rstd.MAGIC, ALU.mult, ALU.add).then_inc(r.guess_done, 1)
    for n in range(Rstd.STEPS):
        before = 3 * Rstd.STEPS * it + 3 * n
        for r in group:
            if n == 0:
                dve.wait_ge(r.guess_done, it + 1)
            else:
                dve.wait_ge(r.newton_done, before)
            nc.vector.scalar_tensor_tensor(r.t[:, :], r.y[:, :], -0.5, r.y[:, :], ALU.mult, ALU.mult)\
                .then_inc(r.newton_done, 1)
        for r in group:
            dve.wait_ge(r.newton_done, before + 1)
            nc.vector.tensor_tensor(r.t[:, :], r.t[:, :], r.v[:, :], ALU.mult).then_inc(r.newton_done, 1)
        for r in group:
            dve.wait_ge(r.newton_done, before + 2)
            nc.vector.scalar_tensor_tensor(r.y[:, :], r.t[:, :], 1.5, r.y[:, :], ALU.add, ALU.mult)\
                .then_inc(r.newton_done, 1)
    for r in group:
        dve.wait_ge(r.newton_done, 3 * Rstd.STEPS * (it + 1))


PAR = 2


def load_phase(nc, dram, g):
    with Scope(nc, "load") as s:
        rows = s.sb("rows", [128, PAR, CH // 128, D])
        sq = s.sb("sq", [128, PAR, 2, CH])
        unit = s.sb("unit", [128, PAR, CH])
        h = s.sb("h", [128, PAR, CH])
        unit2 = s.sb("unit2", [128, PAR, CH])
        ln = s.sb("ln", [128, 2])
        rstd = [[Rstd(s, f"rstd{i}{par}") for i in range(2)] for par in range(PAR)]
        mid = [[s.ps(f"mid{i}{par}") for i in range(2)] for par in range(PAR)]
        var = [[s.ps(f"var{i}{par}") for i in range(2)] for par in range(PAR)]
        turned = [var[par][0] for par in range(PAR)]
        ln_in = s.sems("ln_in").ln_in
        k = [s.sems("rows_in turned x_copied centered0 centered1 squared0 squared1 var0 var1"
                    " unit modulated passed unit2 xn", par) for par in range(PAR)]
        block = s.block()
        x_rows = dram["x"].rearrange("b t c -> (b t) c")
        cols = lambda i, par: bass.ds(i * (PAR * CH) + par * CH, CH)

        @block.sync
        def _(sp):
            sp.dma_start(ln[:, :], dram["ln"]).then_inc(ln_in, 16)
            with sp.Fori(0, NCH // PAR) as i:
                for par in range(PAR):
                    sp.wait_ge(k[par].turned, i)
                    sp.dma_start(rows[:, par], x_rows[cols(i, par), :].rearrange("(r p) c -> p r c", p=128))\
                        .then_inc(k[par].rows_in, 16)

        @block.tensor
        def _(pe):
            def turn(i):
                for par in range(PAR):
                    pe.wait_ge(k[par].rows_in, 16 * (i + 1))
                    pe.wait_ge(k[par].unit, i)
                    for r in range(CH // 128):
                        last = nc.tensor.transpose(turned[par][:, 128 * r:128 * r + 128], rows[:, par, r, :], g.t("ident"))
                    last.then_inc(k[par].turned, 1)

            def center0(i):
                for par in range(PAR):
                    pe.wait_ge(k[par].x_copied, i + 1)
                    nc.tensor.matmul(mid[par][0][:, :], g.t("center"), g.xT[:, cols(i, par)], start=True, stop=True)\
                        .then_inc(k[par].centered0, 1)

            def var0(i):
                for par in range(PAR):
                    pe.wait_ge(k[par].squared0, i + 1)
                    nc.tensor.matmul(var[par][0][:, :], g.t("mean"), sq[:, par, 0, :], start=True, stop=True)\
                        .then_inc(k[par].var0, 1)

            def center1(i):
                for par in range(PAR):
                    pe.wait_ge(k[par].modulated, i + 1)
                    pe.wait_ge(k[par].unit2, i)
                    nc.tensor.matmul(mid[par][1][:, :], g.t("center"), h[:, par, :], start=True, stop=True)\
                        .then_inc(k[par].centered1, 1)

            def var1(i):
                for par in range(PAR):
                    pe.wait_ge(k[par].squared1, i + 1)
                    nc.tensor.matmul(var[par][1][:, :], g.t("mean"), sq[:, par, 1, :], start=True, stop=True)\
                        .then_inc(k[par].var1, 1)
            turn(0)
            center0(0)
            var0(0)
            with pe.Fori(0, NCH // PAR - 1) as i:
                turn(i + 1)
                center1(i)
                center0(i + 1)
                var1(i)
                var0(i + 1)
            center1(NCH // PAR - 1)
            var1(NCH // PAR - 1)

        @block.scalar
        def _(act):
            act.wait_ge(ln_in, 16)

            def copy_x(i):
                for par in range(PAR):
                    act.wait_ge(k[par].turned, i + 1)
                    nc.scalar.activation(g.xT[:, cols(i, par)], turned[par][:, :], ACT.Copy).then_inc(k[par].x_copied, 1)

            def square0(i):
                for par in range(PAR):
                    act.wait_ge(k[par].centered0, i + 1)
                    nc.scalar.activation(sq[:, par, 0, :], mid[par][0][:, :], ACT.Square).then_inc(k[par].squared0, 1)

            def modulate(i):
                for par in range(PAR):
                    act.wait_ge(k[par].unit, i + 1)
                    act.wait_ge(k[par].centered1, i)
                    act.wait_ge(k[par].passed, i)
                    for j in range(BPC):
                        b = i * (PAR * BPC) + par * BPC + j
                        last = nc.scalar.activation(h[:, par, j * T:(j + 1) * T], unit[:, par, j * T:(j + 1) * T],
                                                    ACT.Identity, scale=g.mod[:, 0, 1, bass.ds(b, 1)],
                                                    bias=g.mod[:, 0, 0, bass.ds(b, 1)])
                    last.then_inc(k[par].modulated, 1)

            def square1(i):
                for par in range(PAR):
                    act.wait_ge(k[par].centered1, i + 1)
                    nc.scalar.activation(sq[:, par, 1, :], mid[par][1][:, :], ACT.Square).then_inc(k[par].squared1, 1)

            def affine(i):
                for par in range(PAR):
                    act.wait_ge(k[par].unit2, i + 1)
                    nc.scalar.activation(g.xnT[:, cols(i, par)], unit2[:, par, :], ACT.Identity,
                                         scale=ln[:, 0:1], bias=ln[:, 1:2]).then_inc(k[par].xn, 1)
            copy_x(0)
            square0(0)
            modulate(0)
            with act.Fori(0, NCH // PAR - 1) as i:
                copy_x(i + 1)
                square1(i)
                square0(i + 1)
                affine(i)
                modulate(i + 1)
            square1(NCH // PAR - 1)
            affine(NCH // PAR - 1)

        @block.vector
        def _(dve):
            def norm0(i):
                run_roots(nc, dve, [rstd[par][0] for par in range(PAR)], [var[par][0][:, :] for par in range(PAR)], LN_EPS, i,
                          [k[par].var0 for par in range(PAR)])
                for par in range(PAR):
                    dve.wait_ge(k[par].modulated, i)
                    nc.vector.tensor_tensor(unit[:, par, :], mid[par][0][:, :], rstd[par][0].out[:, :], ALU.mult)\
                        .then_inc(k[par].unit, 1)

            def norm1(i):
                run_roots(nc, dve, [rstd[par][1] for par in range(PAR)], [var[par][1][:, :] for par in range(PAR)], LN_EPS, i,
                          [k[par].var1 for par in range(PAR)])
                for par in range(PAR):
                    dve.wait_ge(k[par].xn, i)
                    nc.vector.tensor_tensor(unit2[:, par, :], mid[par][1][:, :], rstd[par][1].out[:, :], ALU.mult)\
                        .then_inc(k[par].unit2, 1)
            def pass_on(i):
                for par in range(PAR):
                    dve.wait_ge(k[par].centered0, i + 1)
                    dve.wait_ge(k[par].modulated, i + 1)
                    for j in range(BPC):
                        b = i * (PAR * BPC) + par * BPC + j
                        x = g.xT[:, bass.ds(b * T, T)]
                        last = nc.vector.scalar_tensor_tensor(x, h[:, par, j * T:(j + 1) * T], g.mod[:, 0, 2, bass.ds(b, 1)], x,
                                                              ALU.mult, ALU.add)
                    last.then_inc(k[par].passed, 1)
            norm0(0)
            with dve.Fori(0, NCH // PAR - 1) as i:
                norm1(i)
                pass_on(i)
                norm0(i + 1)
            pass_on(NCH // PAR - 1)
            norm1(NCH // PAR - 1)


KEYS_AT = {6: (0, 0, 256), 7: (0, 256, 256), 4: (1, 0, 192), 5: (1, 192, 192), 0: (1, 384, 64), 1: (1, 448, 64),
           2: (2, 0, 128), 3: (2, 128, 128)}
BANKS = 3
ROW_OFF = [SLOT * n * (n + 1) // 2 for n in range(KB + 1)]
EARLY_OFF = [SLOT * n * (n - 1) // 2 for n in range(KB + 1)]


def attention_phase(nc, dram, g):
    with Scope(nc, "attn") as s:
        w = s.sb("w", [128, 5, GROUPS, 128])
        wo = s.sb("wo", [128, GROUPS, 128])
        dirs = s.sb("dirs", [128, 2, GROUPS, 128])
        hs = s.sb("hs", [128, GROUPS])
        share = s.sb("share", [128, 2, GROUPS])
        tq = s.sb("tq", [128, 2, GROUPS, T])
        tk = s.sb("tk", [128, 2, GROUPS, T])
        q = s.sb("q", [128, 2, GROUPS, T])
        kk = s.sb("k", [128, 2, GROUPS, T])
        q_diag = s.sb("q_diag", [128, GROUPS, KB, PER, SLOT])
        v_rows = s.sb("v_rows", [128, GROUPS * KB, SLOT])
        v_diag = s.sb("v_diag", [128, GROUPS * KB, PER, SLOT])
        geo_rows = s.sb("geo_rows", [128, 2, T])
        less_qp = s.sb("less_qp", [128, T])
        run_max = s.sb("run_max", [128, T])
        run_min = s.sb("run_min", [128, T])
        geo_cols = s.sb("geo_cols", [128, 2, 2, KB, SLOT])
        kp_wide = s.sb("kp_wide", [128, 2, GROUPS, KB, SLOT])
        geo_own = s.sb("geo_own", [128, 2, GROUPS, KB, SLOT])
        mx = s.sb("mx", [128, GROUPS, KB])
        p_att = s.sb("p_att", [128, GROUPS, ROW_OFF[KB]])
        p_geo = s.sb("p_geo", [128, GROUPS, EARLY_OFF[KB]])
        p_own = s.sb("p_own", [128, GROUPS, KB, SLOT])
        PITCH = T + SLOT
        turned = s.sb("turned", [128, 2, GROUPS, KB * PITCH])
        oT = s.sb("oT", [128, 2, GROUPS * KB, SLOT])
        coef = s.sb("coef", [128, 2, GROUPS * KB])
        ow = s.sb("ow", [128, 2, GROUPS * KB, DH0])
        aoT = s.sb("aoT", [128, GROUPS * KB, SLOT])
        ao = s.sb("ao", [128, GROUPS, T])
        score = [s.ps(f"score{i}") for i in range(BANKS)]
        F = [s.ps(f"front{i}") for i in range(3)]
        O = [s.ps(f"out{i}") for i in range(2)]
        k = s.sems("w_in cleared ones share_ready q_made qr_made k_made kr_made v_made q_row k_row kp_made"
                   " tq1 tq2 tk1 tk2 q_ready k_ready v_turned v_diag rows_copied less_qp kp_copied ran_max ran_min"
                   " ga_made gb_made less_max geo_cols geo_own turned_g turned_a recip coef weighted combined summed"
                   " out_made x_done")
        by_bank = [s.sems("scored max_read att_exp", n) for n in range(BANKS)]
        by_group = [s.sems("q_diag geo_exp att_turned geo_turned att_weighed geo_weighed", gr) for gr in range(GROUPS)]
        block = s.block()
        tokens = lambda b: bass.ds(b * T, T)
        halves = lambda ap: ap[:, :].rearrange("p (g t) -> p g t", g=GROUPS)

        def steps(eng, front, step):
            front(0, 0)
            step(0, 0, front)
            with eng.Fori(0, B // 2 - 1) as i:
                step(2 * i + 1, 1, front)
                step(2 * i + 2, 0, front)
            step(B - 1, 1, None)

        @block.sync
        def _(sp):
            sp.dma_start(w[:, :, :, :], dram["w_attn"]).then_inc(k.w_in, 16)
            sp.dma_start(wo[:, :, :], dram["wo"]).then_inc(k.w_in, 16)
            sp.dma_start(dirs[:, :, :, :], dram["dirs"]).then_inc(k.w_in, 16)
            sp.dma_start(hs[:, :], dram["hs"]).then_inc(k.w_in, 16)

        @block.tensor
        def _(pe):
            pe.wait_ge(k.w_in, 64)
            pe.wait_ge(k.cleared, 3)
            pe.wait_ge(k.ones, PER)

            def project(out, n, b, sem):
                for gr in range(GROUPS):
                    last = nc.tensor.matmul(out[:, gr * T:(gr + 1) * T], w[:, n, gr, :], g.xnT[:, tokens(b)],
                                            start=True, stop=True)
                last.then_inc(sem, 1)

            def front_qk(b):
                pe.wait_ge(k.kp_copied, b)
                project(F[0], 0, b, k.q_made)
                pe.wait_ge(k.v_turned, b)
                project(F[1], 1, b, k.qr_made)
                pe.wait_ge(k.less_qp, b)
                if not isinstance(b, int) or b > 0:
                    pe.wait_ge(k.x_done, b - 1)
                project(F[2], 2, b, k.k_made)

            def front_v(b):
                pe.wait_ge(k.tq1, b + 1)
                project(F[0], 3, b, k.kr_made)
                pe.wait_ge(k.tq2, b + 1)
                project(F[1], 4, b, k.v_made)

            def front_geo(b, par):
                pe.wait_ge(k.tk1, b + 1)
                pe.wait_ge(k.q_ready, b + 1)
                for gr in range(GROUPS):
                    last = nc.tensor.matmul(F[2][:, 0:T], dirs[:, 0, gr, :], q[:, par, gr, :], start=gr == 0, stop=gr == 1)
                last.then_inc(k.q_row, 1)
                pe.wait_ge(k.k_ready, b + 1)
                for gr in range(GROUPS):
                    last = nc.tensor.matmul(F[2][:, T:2 * T], dirs[:, 0, gr, :], kk[:, par, gr, :],
                                            start=gr == 0, stop=gr == 1)
                last.then_inc(k.k_row, 1)
                pe.wait_ge(k.tk2, b + 1)
                for gr in range(GROUPS):
                    last = nc.tensor.matmul(F[0][:, gr * T:(gr + 1) * T], dirs[:, 1, gr, :], kk[:, par, gr, :],
                                            start=True, stop=True)
                last.then_inc(k.kp_made, 1)

            def scores(b, par, gr):
                pe.wait_ge(by_group[gr].q_diag, b + 1)
                pe.wait_ge(k.k_ready, b + 1)
                for bank in range(BANKS):
                    pe.wait_ge(by_bank[bank].att_exp, GROUPS * b + gr)
                    for n, (at, c, size) in KEYS_AT.items():
                        if at == bank:
                            masked = SLOT if n % 2 else 2 * SLOT
                            nc.tensor.matmul(score[at][:, c:c + size], q_diag[:, gr, n], kk[:, par, gr, 0:size],
                                             start=True, stop=False)
                            last = nc.tensor.matmul(score[at][:, c + size - masked:c + size], g.t("ident_bf"),
                                                    g.t("mask_max")[:, 0:masked], start=False, stop=True)
                    last.then_inc(by_bank[bank].scored, 1)

            def weigh(b, kind, gr):
                pe.wait_ge(k.v_diag, b + 1)
                pe.wait_ge((k.turned_a, k.turned_g)[kind], b)
                pe.wait_ge((by_group[gr].att_turned, by_group[gr].geo_turned)[kind], b + 1)
                for n in range(KB):
                    last = nc.tensor.matmul(O[kind][:, gr * T + SLOT * n:(gr + 1) * T], v_diag[:, gr * KB + n],
                                            turned[:, kind, gr, n * T + SLOT * n:(n + 1) * T],
                                            start=n == 0, stop=n == KB - 1)
                last.then_inc((by_group[gr].att_weighed, by_group[gr].geo_weighed)[kind], 1)

            def front(b, par):
                front_qk(b)
                front_v(b)
                front_geo(b, par)

            def mix(b):
                pe.wait_ge(k.less_qp, b + 2 if not isinstance(b, int) or b < B - 1 else B)
                pe.wait_ge(k.summed, b + 1)
                for gr in range(GROUPS):
                    last = nc.tensor.matmul(F[2][:, 0:T], wo[:, gr, :], ao[:, gr, :], start=gr == 0, stop=gr == 1)
                last.then_inc(k.out_made, 1)

            def step(b, par, ahead):
                scores(b, par, 0)
                if not isinstance(b, int) or b > 0:
                    mix(b - 1)
                if ahead:
                    front_qk(b + 1)
                scores(b, par, 1)
                if ahead:
                    front_v(b + 1)
                weigh(b, 0, 0)
                weigh(b, 1, 0)
                if ahead:
                    front_geo(b + 1, 1 - par)
                weigh(b, 0, 1)
                weigh(b, 1, 1)
                if not ahead:
                    mix(b)
            steps(pe, front, step)

        @block.scalar
        def _(act):
            act.wait_ge(k.cleared, 3)

            def geo_exps(b, par, gr):
                act.wait_ge(k.geo_cols, b + 1)
                act.wait_ge(k.kp_copied, b + 1)
                act.wait_ge(by_group[gr].geo_turned, b)
                for n in range(1, KB):
                    nc.scalar.activation(p_geo[:, gr, EARLY_OFF[n]:EARLY_OFF[n + 1]],
                                         kp_wide[:, par, gr, 0:n, :].rearrange("p n i -> p (n i)"), ACT.Exp,
                                         scale=geo_cols[:, par, 0, n, gr:gr + 1], bias=geo_cols[:, par, 1, n, gr:gr + 1])
                act.wait_ge(k.geo_own, 3 * (b + 1))
                nc.scalar.activation(p_own[:, gr], geo_own[:, par, gr], ACT.Exp).then_inc(by_group[gr].geo_exp, 1)

            def att_exps(b, gr):
                act.wait_ge(by_group[gr].att_turned, b)
                for bank in range(BANKS):
                    act.wait_ge(by_bank[bank].max_read, GROUPS * b + gr + 1)
                    for n, (at, c, size) in KEYS_AT.items():
                        if at == bank:
                            last = nc.scalar.activation(p_att[:, gr, ROW_OFF[n]:ROW_OFF[n + 1]],
                                                        score[at][:, c:c + SLOT * (n + 1)], ACT.Exp, bias=mx[:, gr, n:n + 1])
                    last.then_inc(by_bank[bank].att_exp, 1)

            def front(b, par):
                act.wait_ge(k.q_row, b + 1)
                act.wait_ge(k.k_row, b + 1)
                act.wait_ge(k.geo_cols, b)
                nc.scalar.activation(geo_rows[:, :, :].rearrange("p s t -> p (s t)"), F[2][:, :], ACT.Copy)\
                    .then_inc(k.rows_copied, 1)
                act.wait_ge(k.ga_made, b)
                act.wait_ge(k.gb_made, b)
                nc.scalar.activation(less_qp[:, :], F[2][:, 0:T], ACT.Copy, scale=-1.0).then_inc(k.less_qp, 1)
                act.wait_ge(k.kp_made, b + 1)
                nc.scalar.activation(kp_wide[:, par].rearrange("p g n i -> p (g n i)"), F[0][:, :], ACT.Copy)\
                    .then_inc(k.kp_copied, 1)

            def step(b, par, ahead):
                att_exps(b, 0)
                geo_exps(b, par, 0)
                att_exps(b, 1)
                geo_exps(b, par, 1)
                if ahead:
                    ahead(b + 1, 1 - par)
            steps(act, front, step)

        @block.vector
        def _(dve):
            nc.vector.memset(v_diag[:, :, :, :], 0.0).then_inc(k.cleared, 1)
            nc.vector.memset(aoT[:, :, :], 0.0).then_inc(k.cleared, 1)
            nc.vector.memset(mx[:, :, :], 0.0).then_inc(k.cleared, 1)
            dve.wait_ge(k.cleared, 3)
            for h in range(PER):
                nc.vector.memset(v_diag[SLOT * h:SLOT * h + SLOT, :, h, DH0:DH0 + 1], 1.0).then_inc(k.ones, 1)
            dve.wait_ge(k.w_in, 64)
            nc.vector.tensor_copy(share[:, 1, :], hs[:, :]).then_inc(k.share_ready, 1)
            nc.vector.tensor_scalar(share[:, 0, :], hs[:, :], -1.0, 1.0, ALU.mult, ALU.add).then_inc(k.share_ready, 1)
            dve.wait_ge(k.share_ready, 2)

            def both(ap):
                return ap[:, None, :].to_broadcast([128, GROUPS, T])

            def front_q(b):
                dve.wait_ge(k.q_ready, b)
                dve.wait_ge(k.q_made, b + 1)
                nc.vector.tensor_tensor(tq[:, 0], halves(F[0]), both(g.t("cos")), ALU.mult).then_inc(k.tq1, 1)
                dve.wait_ge(k.qr_made, b + 1)
                nc.vector.tensor_tensor(tq[:, 1], halves(F[1]), both(g.t("sin")), ALU.mult).then_inc(k.tq2, 1)

            def front_k(b):
                dve.wait_ge(k.k_ready, b)
                dve.wait_ge(k.k_made, b + 1)
                nc.vector.tensor_tensor(tk[:, 0], halves(F[2]), both(g.t("cos")), ALU.mult).then_inc(k.tk1, 1)
                dve.wait_ge(k.kr_made, b + 1)
                nc.vector.tensor_tensor(tk[:, 1], halves(F[0]), both(g.t("sin")), ALU.mult).then_inc(k.tk2, 1)

            def front_v(b):
                dve.wait_ge(k.v_made, b + 1)
                dve.wait_ge(k.v_diag, b)
                nc.vector.transpose(v_rows[:, :, :].rearrange("p n d -> p (n d)"), F[1][:, :]).then_inc(k.v_turned, 1)

            def front_extremes(b):
                dve.wait_ge(k.rows_copied, b + 1)
                dve.wait_ge(k.less_max, b)
                kp = geo_rows[:, 1, :]
                nc.vector.tensor_tensor_scan(run_max[:, :], kp, kp, -3e38, ALU.max, ALU.max).then_inc(k.ran_max, 1)
                nc.vector.tensor_tensor_scan(run_min[:, :], kp, kp, 3e38, ALU.min, ALU.min).then_inc(k.ran_min, 1)

            def front_cols(b, par):
                dve.wait_ge(k.ran_min, b + 1)
                dve.wait_ge(k.ga_made, b + 1)
                dve.wait_ge(k.gb_made, b + 1)
                nc.vector.tensor_tensor(geo_rows[:, 1, :], run_max[:, :], run_min[:, :], ALU.min).then_inc(k.less_max, 1)
                if not isinstance(b, int) or b > 1:
                    dve.wait_ge(by_group[1].geo_exp, b - 1)
                dve.wait_ge(k.less_max, b + 1)
                nc.vector.transpose(geo_cols[:, par].rearrange("p s n i -> p (s n i)"),
                                    geo_rows[:, :, :].rearrange("p s t -> p (s t)")).then_inc(k.geo_cols, 1)

            def read_max(b, gr):
                for bank in range(BANKS):
                    dve.wait_ge(by_bank[bank].scored, GROUPS * b + gr + 1)
                    for at, c, size, n in ((0, 0, 256, 6), (1, 0, 192, 4), (1, 384, 64, 0), (2, 0, 128, 2)):
                        if at == bank:
                            last = nc.vector.tensor_reduce(mx[:, gr, n:n + 2], score[at][:, c:c + 2 * size]
                                                           .rearrange("p (n j) -> p n j", n=2), AX.X, ALU.max, negate=True)
                    last.then_inc(by_bank[bank].max_read, 1)

            def by_key(kind, gr):
                return turned[:, kind, gr, 0:KB * T].rearrange("p (j q) -> p j q", q=T)

            def turn_att(b, gr):
                for bank in range(BANKS):
                    dve.wait_ge(by_bank[bank].att_exp, GROUPS * b + gr + 1)
                dve.wait_ge(by_group[gr].att_weighed, b)
                for n in range(KB):
                    last = nc.vector.transpose(by_key(0, gr)[:, 0:n + 1, SLOT * n:SLOT * n + SLOT],
                                               p_att[:, gr, ROW_OFF[n]:ROW_OFF[n + 1]].rearrange("p (j i) -> p j i", i=SLOT))
                last.then_inc(by_group[gr].att_turned, 1)

            def turn_geo(b, gr):
                dve.wait_ge(by_group[gr].geo_exp, b + 1)
                dve.wait_ge(by_group[gr].geo_weighed, b)
                for n in range(1, KB):
                    nc.vector.transpose(by_key(1, gr)[:, 0:n, SLOT * n:SLOT * n + SLOT],
                                        p_geo[:, gr, EARLY_OFF[n]:EARLY_OFF[n + 1]].rearrange("p (j i) -> p j i", i=SLOT))
                nc.vector.transpose(turned[:, 1, gr, :].rearrange("p (n i) -> p n i", i=PITCH)[:, :, 0:SLOT], p_own[:, gr])\
                    .then_inc(by_group[gr].geo_turned, 1)

            def outputs(b):
                for gr in range(GROUPS):
                    dve.wait_ge(by_group[gr].att_weighed, b + 1)
                nc.vector.transpose(oT[:, 0].rearrange("p n i -> p (n i)"), O[0][:, :]).then_inc(k.turned_a, 1)
                for gr in range(GROUPS):
                    dve.wait_ge(by_group[gr].geo_weighed, b + 1)
                nc.vector.transpose(oT[:, 1].rearrange("p n i -> p (n i)"), O[1][:, :]).then_inc(k.turned_g, 1)
                dve.wait_ge(k.turned_g, b + 1)
                dve.wait_ge(k.turned_a, b + 1)
                nc.vector.reciprocal(coef[:, :, :], oT[:, :, :, DH0]).then_inc(k.recip, 1)
                dve.wait_ge(k.recip, b + 1)
                grouped = coef[:, :, :].rearrange("p s (g n) -> p (s g) n", g=GROUPS)
                nc.vector.tensor_tensor(grouped, grouped, share[:, :, :].rearrange("p s g -> p (s g)")[:, :, None]
                                        .to_broadcast([128, 2 * GROUPS, KB]), ALU.mult).then_inc(k.coef, 1)
                dve.wait_ge(k.coef, b + 1)
                nc.vector.tensor_tensor(ow[:, :, :, :].rearrange("p s n d -> p (s n) d"),
                                        oT[:, :, :, 0:DH0].rearrange("p s n d -> p (s n) d"),
                                        coef[:, :, :].rearrange("p s n -> p (s n)")[:, :, None]
                                        .to_broadcast([128, 2 * GROUPS * KB, DH0]), ALU.mult).then_inc(k.weighted, 1)
                dve.wait_ge(k.weighted, b + 1)
                nc.vector.tensor_tensor(aoT[:, :, 0:DH0], ow[:, 0], ow[:, 1], ALU.add).then_inc(k.combined, 1)
                dve.wait_ge(k.combined, b + 1)
                nc.vector.transpose(ao[:, :, :].rearrange("p g t -> p (g t)"), aoT[:, :, :].rearrange("p n i -> p (n i)"))\
                    .then_inc(k.summed, 1)

            def add(b):
                dve.wait_ge(k.out_made, b + 1)
                x = g.xT[:, tokens(b)]
                nc.vector.scalar_tensor_tensor(x, F[2][:, 0:T], g.mod[:, 0, 2, bass.ds(b, 1)], x, ALU.mult, ALU.add)\
                    .then_inc(k.x_done, 1)

            def front(b, par):
                front_q(b)
                front_k(b)
                front_v(b)
                front_extremes(b)
                front_cols(b, par)

            def step(b, par, ahead):
                read_max(b, 0)
                if not isinstance(b, int) or b > 0:
                    add(b - 1)
                if ahead:
                    front_q(b + 1)
                turn_att(b, 0)
                read_max(b, 1)
                if ahead:
                    front_k(b + 1)
                turn_geo(b, 0)
                if ahead:
                    front_v(b + 1)
                turn_att(b, 1)
                if ahead:
                    front_extremes(b + 1)
                turn_geo(b, 1)
                if ahead:
                    front_cols(b + 1, 1 - par)
                outputs(b)
                if not ahead:
                    add(b)
            steps(dve, front, step)

        @block.gpsimd
        def _(pool):
            def diagonal(out, rows, mask, count, size):
                return nc.gpsimd.tensor_tensor(out, rows[:, :, None, :].to_broadcast([128, count, PER, size]),
                                               mask[:, None, :, None].to_broadcast([128, count, PER, size]), ALU.mult)

            def front(b, par):
                later = not isinstance(b, int) or b > 0
                pool.wait_ge(k.tq1, b + 1)
                pool.wait_ge(k.tq2, b + 1)
                if later:
                    pool.wait_ge(k.q_row, b - 1)
                    pool.wait_ge(by_group[1].q_diag, b - 1)
                nc.gpsimd.tensor_tensor(q[:, par], tq[:, 0], tq[:, 1], ALU.add).then_inc(k.q_ready, 1)
                pool.wait_ge(k.tk1, b + 1)
                pool.wait_ge(k.tk2, b + 1)
                if later:
                    for bank in range(BANKS):
                        pool.wait_ge(by_bank[bank].scored, GROUPS * (b - 1))
                    pool.wait_ge(k.kp_made, b - 1)
                nc.gpsimd.tensor_tensor(kk[:, par], tk[:, 0], tk[:, 1], ALU.add).then_inc(k.k_ready, 1)
                for gr in range(GROUPS):
                    pool.wait_ge(k.q_ready, b + 1)
                    if later:
                        for bank in range(BANKS):
                            pool.wait_ge(by_bank[bank].scored, GROUPS * b + gr - 1)
                    diagonal(q_diag[:, gr], q[:, par, gr].rearrange("p (n i) -> p n i", i=SLOT), g.t("own_head_scaled"),
                             KB, SLOT).then_inc(by_group[gr].q_diag, 1)
                pool.wait_ge(k.less_qp, b + 1)
                pool.wait_ge(k.ran_max, b + 1)
                nc.gpsimd.tensor_tensor(run_max[:, :], run_max[:, :], less_qp[:, :], ALU.mult).then_inc(k.ga_made, 1)
                pool.wait_ge(k.ran_min, b + 1)
                nc.gpsimd.tensor_tensor(run_min[:, :], run_min[:, :], less_qp[:, :], ALU.mult).then_inc(k.gb_made, 1)
                shape = [128, GROUPS, KB, SLOT]
                by_query = [geo_cols[:, par, n, :, 0:GROUPS].rearrange("p n g -> p g n")[:, :, :, None].to_broadcast(shape)
                            for n in range(2)]
                pool.wait_ge(k.geo_cols, b + 1)
                pool.wait_ge(k.kp_copied, b + 1)
                nc.gpsimd.tensor_tensor(geo_own[:, par], kp_wide[:, par], by_query[0], ALU.mult).then_inc(k.geo_own, 1)
                pool.wait_ge(k.geo_own, 3 * b + 1)
                nc.gpsimd.tensor_tensor(geo_own[:, par], geo_own[:, par], by_query[1], ALU.add).then_inc(k.geo_own, 1)
                pool.wait_ge(k.geo_own, 3 * b + 2)
                nc.gpsimd.tensor_tensor(geo_own[:, par], geo_own[:, par], g.t("mask_own")[:, None, None, :].to_broadcast(shape),
                                        ALU.add).then_inc(k.geo_own, 1)
                pool.wait_ge(k.v_turned, b + 1)
                for kind in ("att_weighed", "geo_weighed"):
                    pool.wait_ge(by_group[1][kind], b)
                diagonal(v_diag[:, :, :, 0:DH0], v_rows[:, :, 0:DH0], g.t("own_head"), GROUPS * KB, DH0).then_inc(k.v_diag, 1)

            def step(b, par, ahead):
                if ahead:
                    ahead(b + 1, 1 - par)
            pool.wait_ge(k.ones, PER)
            steps(pool, front, step)


class Chain:

    def __init__(self, eng, sem, per, it):
        self.eng, self.sem, self.per, self.it, self.n = eng, sem, per, it, 0

    def __call__(self, ins, wait=True):
        ins.then_inc(self.sem, 1)
        self.n += 1
        assert self.n <= self.per
        if wait:
            self.done()

    def done(self):
        self.eng.wait_ge(self.sem, self.per * self.it + self.n)


TILES = CH // 128
ROW = D + E0


def route_phase(nc, dram, g):
    CHOICES = TILES * K0
    with Scope(nc, "route") as s:
        gate_w = s.sb("gate_w", [128, E0], BF16)
        gate_wf = s.sb("gate_wf", [128, E0])
        bias = s.sb("bias", [128, E0])
        sw_bf = s.sb("sw_bf", [128, 2, I0], BF16)
        sw = s.sb("sw", [128, 2, I0])
        sw2_bf = s.sb("sw2_bf", [I0, D], BF16)
        sw2 = s.sb("sw2", [I0, D])
        iota = s.sb("iota", [128, CAP], BF16)
        before = s.sb("before", [128, 128], BF16)
        ones = s.sb("ones", [128, 128], BF16)
        zero = s.sb("zero", [128, 13 * D])
        zero_bf = s.sb("zero_bf", [128, 128], BF16)
        sq = s.sb("sq", [128, PAR, CH])
        unit = s.sb("unit", [128, PAR, CH])
        h2 = s.sb("h2", [128, PAR, CH])
        rows = s.sb("rows", [128, PAR, TILES, ROW])
        score = s.sb("score", [128, PAR, TILES, E0])
        biased = s.sb("biased", [128, PAR, TILES, E0])
        top = s.sb("top", [128, PAR, TILES, 8])
        top_at = s.sb("top_at", [128, PAR, TILES, 8], U32)
        chosen = s.sb("chosen", [128, PAR, TILES, K0])
        onehot = s.sb("onehot", [128, PAR, CHOICES, E0], BF16)
        by_expert = s.sb("by_expert", [128, PAR, 3, CHOICES, E0], BF16)
        mask = s.sb("mask", [128, PAR, TILES, E0], BF16)
        gates = s.sb("gates", [128, PAR, TILES, E0])
        total = s.sb("total", [128, PAR, TILES])
        seen = s.sb("seen", [128, PAR, 1])
        place = s.sb("place", [128, PAR, TILES, E0])
        base = s.sb("base", [128, PAR, E0])
        own = s.sb("own", [128, PAR, CHOICES, E0])
        slot = s.sb("slot", [128, PAR, CHOICES])
        by_slot = s.sb("by_slot", [128, PAR, CHOICES, CAP], BF16)
        sig1 = s.sb("sig1", [I0, PAR, CH])
        hid = s.sb("hid", [I0, PAR, CH])
        held = s.sb("held", [128, 3, E0])
        free = s.sb("free", [128, E0])
        rstd = [Rstd(s, f"rstd{par}") for par in range(PAR)]
        slots_ps, turned = s.ps("slots_ps"), s.ps("turned")
        bank = [[s.ps(f"bank{n}{par}") for n in range(3)] for par in range(PAR)]
        mid, up1, shared, var, up3, small = ([bank[par][n] for par in range(PAR)] for n in (0, 0, 0, 1, 1, 2))
        c = s.sems("w_in zeroed consts cleared zero_out rows_read counted slots_done held tail")
        k = [s.sems("rows_out centered squared var unit modulated logits up1 up3 turned score sig1 mask counted"
                    " route spread hid_part hid shared_made x_done slots_added", par) for par in range(PAR)]
        block = s.block()
        STEPS = 2 * TILES + 11 + CHOICES
        cols = lambda i, par: bass.ds(i * (PAR * CH) + par * CH, CH)
        both = range(PAR)

        @block.sync
        def _(sp):
            sp.dma_start(gate_w[:, :], dram["gate_w"]).then_inc(c.w_in, 16)
            sp.dma_start(bias[:, :], dram["gate_bias"].to_broadcast([128, E0])).then_inc(c.w_in, 16)
            sp.dma_start(sw_bf[:, :, :], dram["sw13"]).then_inc(c.w_in, 16)
            sp.dma_start(sw2_bf[:, :], dram["sw2"]).then_inc(c.w_in, 16)
            sp.wait_ge(c.zeroed, 1)
            acc = g.acc.rearrange("(p r) c -> p (r c)", p=128)
            for i in range(5):
                sp.dma_start(acc[:, i * 13 * D:(i + 1) * 13 * D], zero[:, :]).then_inc(c.zero_out, 16)
            sp.dma_start(g.rows[N:N + CAP, :], zero[:, 0:ROW]).then_inc(c.zero_out, 16)
            with sp.Fori(0, NCH // PAR) as i:
                for par in both:
                    sp.wait_ge(c.rows_read, PAR * i + par + 1)
                    sp.wait_ge(k[par].route, STEPS * i + 2 * TILES + 9)
                    sp.dma_start(g.rows[cols(i, par), :].rearrange("(r p) c -> p r c", p=128), rows[:, par])\
                        .then_inc(k[par].rows_out, 16)
            for par in both:
                sp.wait_ge(k[par].rows_out, 16 * (NCH // PAR))
            sp.wait_ge(c.zero_out, 16 * 6)

        @block.tensor
        def _(pe):
            pe.wait_ge(c.consts, 5)
            nc.tensor.matmul(slots_ps[:, 0:3 * E0], zero_bf[:, :], zero_bf[:, 0:3 * E0], start=True, stop=False)
            with pe.Fori(0, NCH // PAR) as i:
                for par in both:
                    pe.wait_ge(k[par].x_done, i)
                    nc.tensor.matmul(mid[par][:, :], g.t("center"), g.xT[:, cols(i, par)], start=True, stop=True)\
                        .then_inc(k[par].centered, 1)
                for par in both:
                    pe.wait_ge(k[par].squared, i + 1)
                    nc.tensor.matmul(var[par][:, :], g.t("mean"), sq[:, par, :], start=True, stop=True)\
                        .then_inc(k[par].var, 1)
                for par in both:
                    pe.wait_ge(k[par].modulated, i + 1)
                    pe.wait_ge(k[par].counted, i)
                    for j in range(TILES):
                        last = nc.tensor.matmul(small[par][:, j * E0:(j + 1) * E0], h2[:, par, 128 * j:128 * j + 128],
                                                gate_wf[:, :], start=True, stop=True)
                    last.then_inc(k[par].logits, 1)
                for par in both:
                    nc.tensor.matmul(up1[par][0:I0, :], sw[:, 0, :], h2[:, par, :], start=True, stop=True)\
                        .then_inc(k[par].up1, 1)
                    nc.tensor.matmul(up3[par][0:I0, :], sw[:, 1, :], h2[:, par, :], start=True, stop=True)\
                        .then_inc(k[par].up3, 1)
                for par in both:
                    pe.wait_ge(c.rows_read, PAR * i + par)
                    for j in range(TILES):
                        last = nc.tensor.transpose(turned[:, 128 * j:128 * j + 128], h2[:, par, 128 * j:128 * j + 128],
                                                   g.t("ident"))
                    last.then_inc(k[par].turned, 1)
                for par in both:
                    pe.wait_ge(k[par].route, STEPS * i + 2 * TILES + 4)
                    for j in range(TILES + 1):
                        out = small[par][:, 128 + j * E0:128 + (j + 1) * E0]
                        for n in range(min(j, TILES)):
                            last = nc.tensor.matmul(out, ones[:, :], mask[:, par, n, :], start=n == 0, stop=n == TILES - 1)
                        if j < TILES:
                            last = nc.tensor.matmul(out, before[:, :], mask[:, par, j, :], start=j == 0, stop=True)
                    last.then_inc(k[par].mask, 1)
                for par in both:
                    pe.wait_ge(k[par].hid, i + 1)
                    nc.tensor.matmul(shared[par][:, :], sw2[:, :], hid[:, par, :], start=True, stop=True)\
                        .then_inc(k[par].shared_made, 1)
                for par in both:
                    pe.wait_ge(k[par].route, STEPS * (i + 1))
                    pe.wait_ge(k[par].spread, 3 * (i + 1))
                    for n in range(CHOICES):
                        last = nc.tensor.matmul(slots_ps[:, 0:3 * E0], by_slot[:, par, n, :], by_expert[:, par, :, n, :],
                                                start=False, stop=False)
                    last.then_inc(k[par].slots_added, 1)
            nc.tensor.matmul(slots_ps[:, 0:3 * E0], zero_bf[:, :], zero_bf[:, 0:3 * E0], start=False, stop=True)\
                .then_inc(c.slots_done, 1)

        @block.scalar
        def _(act):
            with act.Fori(0, NCH // PAR) as i:
                for par in both:
                    act.wait_ge(k[par].centered, i + 1)
                    nc.scalar.activation(sq[:, par, :], mid[par][:, :], ACT.Square).then_inc(k[par].squared, 1)
                for par in both:
                    act.wait_ge(k[par].unit, i + 1)
                    act.wait_ge(k[par].turned, i)
                    for j in range(BPC):
                        b = i * (PAR * BPC) + par * BPC + j
                        last = nc.scalar.activation(h2[:, par, j * T:(j + 1) * T], unit[:, par, j * T:(j + 1) * T],
                                                    ACT.Identity, scale=g.mod[:, 0, 4, bass.ds(b, 1)],
                                                    bias=g.mod[:, 0, 3, bass.ds(b, 1)])
                    last.then_inc(k[par].modulated, 1)
                for par in both:
                    act.wait_ge(k[par].logits, i + 1)
                    act.wait_ge(k[par].route, STEPS * i)
                    nc.scalar.activation(score[:, par].rearrange("p j e -> p (j e)"), small[par][:, 0:TILES * E0],
                                         ACT.Sigmoid).then_inc(k[par].score, 1)
                for par in both:
                    act.wait_ge(k[par].up1, i + 1)
                    act.wait_ge(k[par].hid, i)
                    nc.scalar.activation(sig1[:, par, :], up1[par][0:I0, :], ACT.Sigmoid).then_inc(k[par].sig1, 1)
                for par in both:
                    act.wait_ge(k[par].turned, i + 1)
                    act.wait_ge(k[par].rows_out, 16 * i)
                    nc.scalar.activation(rows[:, par, :, 0:D], turned[:, :].rearrange("p (j c) -> p j c", c=D), ACT.Copy)\
                        .then_inc(c.rows_read, 1)

        @block.vector
        def _(dve):
            nc.vector.memset(zero[:, :], 0.0).then_inc(c.zeroed, 1)
            nc.vector.memset(base[:, 0, :], 0.0).then_inc(c.cleared, 1)
            nc.vector.memset(zero_bf[:, :], 0.0).then_inc(c.consts, 1)
            nc.vector.tensor_copy(before[:, :], g.t("before")).then_inc(c.consts, 1)
            nc.vector.tensor_copy(ones[:, :], g.t("ones")).then_inc(c.consts, 1)
            nc.vector.tensor_copy(iota[:, :], g.t("iota")).then_inc(c.cleared, 1)
            dve.wait_ge(c.w_in, 64)
            nc.vector.tensor_copy(gate_wf[:, :], gate_w[:, :]).then_inc(c.consts, 1)
            nc.vector.tensor_copy(sw[:, :, :], sw_bf[:, :, :])
            nc.vector.tensor_copy(sw2[:, :], sw2_bf[:, :]).then_inc(c.consts, 1)
            dve.wait_ge(c.cleared, 2)

            def per_tile(ap):
                return ap[:, None, :].to_broadcast([128, TILES, E0])

            def by_choice(ap):
                return ap.rearrange("p (j c) e -> p j c e", c=K0)
            with dve.Fori(0, NCH // PAR) as i:
                run_roots(nc, dve, rstd, [var[par][:, :] for par in both], LN_EPS, i, [k[par].var for par in both])
                for par in both:
                    nc.vector.tensor_tensor(unit[:, par, :], mid[par][:, :], rstd[par].out[:, :], ALU.mult)\
                        .then_inc(k[par].unit, 1)
                then = [Chain(dve, k[par].route, STEPS, i) for par in both]
                for par in both:
                    dve.wait_ge(k[par].score, i + 1)
                    then[par](nc.vector.tensor_tensor(biased[:, par], score[:, par], per_tile(bias), ALU.add), wait=False)
                for par in both:
                    then[par].done()
                    nc.vector.tensor_copy(seen[:, par, 0:1], biased[:, par, 0, 0:1])
                    for j in range(TILES):
                        then[par](nc.vector.max(top[:, par, j, :], biased[:, par, j, :]), wait=False)
                for par in both:
                    then[par].done()
                    nc.vector.tensor_copy(seen[:, par, 0:1], top[:, par, 0, 0:1])
                    for j in range(TILES):
                        then[par](nc.vector.max_index(top_at[:, par, j, :], top[:, par, j, :], biased[:, par, j, :]), wait=False)
                for par in both:
                    then[par].done()
                    then[par](nc.vector.tensor_copy(chosen[:, par], top_at[:, par, :, 0:K0]), wait=False)
                for par in both:
                    dve.wait_ge(k[par].spread, 3 * i)
                    then[par].done()
                    then[par](nc.vector.tensor_tensor(onehot[:, par], g.t("iota")[:, None, 0:E0]
                                                      .to_broadcast([128, CHOICES, E0]),
                                                      chosen[:, par].rearrange("p j c -> p (j c)")[:, :, None]
                                                      .to_broadcast([128, CHOICES, E0]), ALU.is_equal), wait=False)
                for par in both:
                    then[par].done()
                    with nc.allow_low_precision(reason="sums of one-hot rows are 0 or 1"):
                        then[par](nc.vector.tensor_reduce(mask[:, par], onehot[:, par].rearrange("p (j c) e -> p j e c", c=K0),
                                                          AX.X, ALU.add), wait=False)
                for par in both:
                    then[par].done()
                    then[par](nc.vector.tensor_tensor(gates[:, par], mask[:, par], score[:, par], ALU.mult), wait=False)
                for par in both:
                    then[par].done()
                    then[par](nc.vector.tensor_reduce(total[:, par], gates[:, par], AX.X, ALU.add), wait=False)
                for par in both:
                    then[par].done()
                    then[par](nc.vector.tensor_scalar(total[:, par], total[:, par], 1e-12, None, ALU.max), wait=False)
                for par in both:
                    then[par].done()
                    then[par](nc.vector.reciprocal(total[:, par], total[:, par]), wait=False)
                for par in both:
                    dve.wait_ge(k[par].rows_out, 16 * i)
                    then[par].done()
                    then[par](nc.vector.tensor_tensor(rows[:, par, :, D:ROW], gates[:, par], total[:, par, :, None]
                                                      .to_broadcast([128, TILES, E0]), ALU.mult), wait=False)
                for par in both:
                    dve.wait_ge(k[par].sig1, i + 1)
                    nc.vector.tensor_tensor(sig1[:, par, :], sig1[:, par, :], up1[par][0:I0, :], ALU.mult)\
                        .then_inc(k[par].hid_part, 1)
                for par in both:
                    dve.wait_ge(k[par].hid_part, i + 1)
                    dve.wait_ge(k[par].up3, i + 1)
                    nc.vector.tensor_tensor(hid[:, par, :], sig1[:, par, :], up3[par][0:I0, :], ALU.mult)\
                        .then_inc(k[par].hid, 1)
                for par in both:
                    dve.wait_ge(k[par].mask, i + 1)
                    dve.wait_ge(c.counted, PAR * i + par)
                    then[par](nc.vector.tensor_tensor(place[:, par], small[par][:, 128:128 + TILES * E0]
                                                      .rearrange("p (j e) -> p j e", e=E0), per_tile(base[:, par, :]), ALU.add), wait=False)
                    then[1 - par].done()
                    nc.vector.tensor_tensor(base[:, 1 - par, :], base[:, par, :], small[par][:, 128 + TILES * E0:128 + (TILES + 1) * E0],
                                            ALU.add).then_inc(c.counted, 1)
                for par in both:
                    dve.wait_ge(c.counted, PAR * i + par + 1)
                    then[par].done()
                    nc.vector.tensor_tensor(by_choice(own[:, par]), by_choice(onehot[:, par]),
                                            place[:, par, :, None, :].to_broadcast([128, TILES, K0, E0]), ALU.mult)\
                        .then_inc(k[par].counted, 1)
                for par in both:
                    dve.wait_ge(k[par].counted, i + 1)
                    dve.wait_ge(k[par].slots_added, i)
                    then[par](nc.vector.tensor_reduce(slot[:, par], own[:, par], AX.X, ALU.add), wait=False)
                for par in both:
                    then[par].done()
                    for n in range(CHOICES):
                        then[par](nc.vector.tensor_scalar(by_slot[:, par, n, :], iota[:, :], slot[:, par, n:n + 1], None,
                                                          ALU.is_equal), wait=False)
                for par in both:
                    dve.wait_ge(k[par].shared_made, i + 1)
                    for j in range(BPC):
                        b = i * (PAR * BPC) + par * BPC + j
                        x = g.xT[:, bass.ds(b * T, T)]
                        last = nc.vector.scalar_tensor_tensor(x, shared[par][:, j * T:(j + 1) * T],
                                                              g.mod[:, 0, 5, bass.ds(b, 1)], x, ALU.mult, ALU.add)
                    last.then_inc(k[par].x_done, 1)
            dve.wait_ge(c.slots_done, 1)
            nc.vector.tensor_copy(held[:, :, :].rearrange("p v e -> p (v e)"), slots_ps[:, 0:3 * E0]).then_inc(c.held, 1)
            dve.wait_ge(c.held, 1)
            nc.vector.tensor_scalar(free[:, :], held[:, 0, :], -1.0, 1.0, ALU.mult, ALU.add).then_inc(c.tail, 1)
            nc.vector.scalar_tensor_tensor(held[:, 1, :], held[:, 2, :], 128.0, held[:, 1, :], ALU.mult, ALU.add)\
                .then_inc(c.tail, 1)
            dve.wait_ge(c.tail, 2)
            nc.vector.scalar_tensor_tensor(held[:, 1, :], free[:, :], g.t("past"), held[:, 1, :], ALU.mult, ALU.add)\
                .then_inc(c.tail, 1)
            dve.wait_ge(c.tail, 3)
            nc.vector.tensor_copy(g.slot_token[:, :], held[:, 1, :])

        @block.gpsimd
        def _(pool):
            wide = lambda ap: ap.to_broadcast([128, CHOICES, E0])
            with pool.Fori(0, NCH // PAR) as i:
                for par in both:
                    pool.wait_ge(k[par].slots_added, i)
                    pool.wait_ge(k[par].route, STEPS * i + 2 * TILES + 4)
                    nc.gpsimd.tensor_tensor(by_expert[:, par, 0], onehot[:, par], wide(g.t("ones")[:, 0:1, None]), ALU.mult)\
                        .then_inc(k[par].spread, 1)
                    nc.gpsimd.tensor_tensor(by_expert[:, par, 1], onehot[:, par], wide(g.t("row_no")[:, :, None]), ALU.mult)\
                        .then_inc(k[par].spread, 1)
                    tile = g.t("tile_no")[:, bass.ds(i * (PAR * TILES) + par * TILES, TILES)]
                    nc.gpsimd.tensor_tensor(by_expert[:, par, 2].rearrange("p (j c) e -> p j c e", c=K0),
                                            onehot[:, par].rearrange("p (j c) e -> p j c e", c=K0),
                                            tile[:, :, None, None].to_broadcast([128, TILES, K0, E0]), ALU.mult)\
                        .then_inc(k[par].spread, 1)


def experts_phase(nc, dram, g):
    with Scope(nc, "exp") as s:
        w13_bf = s.sb("w13_bf", [128, E0, 2 * I0], BF16)
        w2_bf = s.sb("w2_bf", [I0, E0, D], BF16)
        w13 = s.sb("w13", [128, E0, 2 * I0])
        w2 = s.sb("w2", [I0, E0, D])
        rows = s.sb("rows", [128, E0 * ROW])
        y = s.sb("y", [128, E0 * D])
        xg = s.sb("xg", [128, PAR, D])
        xgT = s.sb("xgT", [128, PAR, 128])
        sig = s.sb("sig", [128, PAR, I0])
        hid = s.sb("hid", [128, PAR, 128])
        hidT = s.sb("hidT", [I0, PAR, 128])
        ps = [[s.ps(f"{n}{par}") for n in ("x", "up", "h", "down")] for par in range(PAR)]
        w = s.sems("w_in padded w13 w2 gathered added")
        k = [s.sems("staged turned x_copied up sig part hid h_turned h_copied down y", par) for par in range(PAR)]
        block = s.block()

        @block.sync
        def _(sp):
            sp.dma_start(w13_bf[:, :, :], dram["w13"]).then_inc(w.w_in, 16)
            sp.dma_start(w2_bf[:, :, :], dram["w2"]).then_inc(w.w_in, 16)

        @block.gpsimd
        def _(pool):
            for e in range(E0):
                nc.gpsimd.indirect_dma_start(rows[:, e * ROW:(e + 1) * ROW], None, g.rows,
                                             bass.IndirectOffsetOnAxis(g.slot_token[:, e:e + 1], 0)).then_inc(w.gathered, 16)
            for e in range(E0):
                pool.wait_ge(k[e % PAR].y, e // PAR + 1)
                if e:
                    pool.wait_ge(w.added, 16 * e)
                nc.gpsimd.indirect_dma_start(g.acc, bass.IndirectOffsetOnAxis(g.slot_token[:, e:e + 1], 0),
                                             y[:, e * D:(e + 1) * D], None, compute_op=ALU.add).then_inc(w.added, 16)
            pool.wait_ge(w.added, 16 * E0)

        @block.tensor
        def _(pe):
            pe.wait_ge(w.w13, 1)
            pe.wait_ge(w.w2, 1)
            with pe.Fori(0, E0 // PAR) as i:
                for par in range(PAR):
                    pe.wait_ge(k[par].staged, i + 1)
                    nc.tensor.transpose(ps[par][0][:, 0:128], xg[:, par, :], g.t("ident")).then_inc(k[par].turned, 1)
                for par in range(PAR):
                    pe.wait_ge(k[par].x_copied, i + 1)
                    nc.tensor.matmul(ps[par][1][:, 0:2 * I0], xgT[:, par, :], w13[:, bass.ds(i * PAR + par, 1), :]
                                     .rearrange("p e i -> p (e i)"), start=True, stop=True).then_inc(k[par].up, 1)
                for par in range(PAR):
                    pe.wait_ge(k[par].hid, i + 1)
                    nc.tensor.transpose(ps[par][2][:, 0:128], hid[:, par, :], g.t("ident")).then_inc(k[par].h_turned, 1)
                for par in range(PAR):
                    pe.wait_ge(k[par].h_copied, i + 1)
                    nc.tensor.matmul(ps[par][3][:, 0:D], hidT[:, par, :], w2[:, bass.ds(i * PAR + par, 1), :]
                                     .rearrange("p e i -> p (e i)"), start=True, stop=True).then_inc(k[par].down, 1)

        @block.scalar
        def _(act):
            act.wait_ge(w.w_in, 32)
            nc.scalar.activation(w2[:, :, :], w2_bf[:, :, :], ACT.Copy).then_inc(w.w2, 1)
            with act.Fori(0, E0 // PAR) as i:
                for par in range(PAR):
                    act.wait_ge(k[par].turned, i + 1)
                    nc.scalar.activation(xgT[:, par, :], ps[par][0][:, 0:128], ACT.Copy).then_inc(k[par].x_copied, 1)
                for par in range(PAR):
                    act.wait_ge(k[par].up, i + 1)
                    nc.scalar.activation(sig[:, par, :], ps[par][1][:, 0:I0], ACT.Sigmoid).then_inc(k[par].sig, 1)
                for par in range(PAR):
                    act.wait_ge(k[par].h_turned, i + 1)
                    nc.scalar.activation(hidT[:, par, :], ps[par][2][0:I0, 0:128], ACT.Copy).then_inc(k[par].h_copied, 1)

        @block.vector
        def _(dve):
            dve.wait_ge(w.w_in, 32)
            nc.vector.tensor_copy(w13[:, :, :], w13_bf[:, :, :]).then_inc(w.w13, 1)
            nc.vector.memset(hid[:, :, :], 0.0).then_inc(w.padded, 1)
            dve.wait_ge(w.padded, 1)
            dve.wait_ge(w.gathered, 16 * E0)
            with dve.Fori(0, E0 // PAR) as i:
                for par in range(PAR):
                    dve.wait_ge(k[par].turned, i)
                    nc.vector.tensor_copy(xg[:, par, :], rows[:, bass.ds(i * (PAR * ROW) + par * ROW, D)])\
                        .then_inc(k[par].staged, 1)
                for par in range(PAR):
                    dve.wait_ge(k[par].sig, i + 1)
                    nc.vector.tensor_tensor(sig[:, par, :], sig[:, par, :], ps[par][1][:, 0:I0], ALU.mult)\
                        .then_inc(k[par].part, 1)
                for par in range(PAR):
                    dve.wait_ge(k[par].part, i + 1)
                    nc.vector.tensor_tensor(hid[:, par, 0:I0], sig[:, par, :], ps[par][1][:, I0:2 * I0], ALU.mult)\
                        .then_inc(k[par].hid, 1)
                for par in range(PAR):
                    dve.wait_ge(k[par].down, i + 1)
                    nc.vector.tensor_scalar(y[:, bass.ds(i * (PAR * D) + par * D, D)], ps[par][3][:, 0:D],
                                            rows[:, bass.ds(i * (PAR * (ROW + 1)) + par * (ROW + 1) + D, 1)], None,
                                            ALU.mult).then_inc(k[par].y, 1)


GT = 8


def project_phase(nc, dram, g):
    LEAD = CONV - 1
    HEADS_IN_BLOCK = SLOT // DH1
    ROOTS = 2 * RC * HEADS_IN_BLOCK
    with Scope(nc, "proj") as s:
        w = s.sb("w", [128, 3, 128])
        wb = s.sb("wb", [128, H1])
        wb_wide = s.sb("wb_wide", [128, H1, DH1])
        bias = s.sb("bias", [128, 4])
        taps = s.sb("taps", [128, 3, CONV])
        last_bias = s.sb("last_bias", [128, 3])
        rows = s.sb("rows", [128, PAR, TILES, D])
        unit = s.sb("unit", [128, PAR, CH])
        h3 = s.sb("h3", [128, PAR, CH])
        pad = s.sb("pad", [128, PAR, 3, BPC, LEAD + T])
        conv = s.sb("conv", [128, PAR, 3, CH])
        sq2 = s.sb("sq2", [128, PAR, 2, CH])
        rate = s.sb("rate", [128, PAR, CH])
        len_t = s.sb("len_t", [128, PAR, 2, RC, SLOT])
        inv = s.sb("inv", [128, PAR, 2, RC, HEADS_IN_BLOCK])
        rstd = [Rstd(s, f"rstd{par}", room=(sq2[:, par, 0, :], sq2[:, par, 1, :])) for par in range(PAR)]
        root = [Rstd(s, f"root{par}", ROOTS, parts=False) for par in range(PAR)]
        bank = [[s.ps(f"bank{i}{par}") for i in range(4)] for par in range(PAR)]
        turned, var, mid, made, sums = ([bank[par][0] for par in range(PAR)], [bank[par][0] for par in range(PAR)],
                                        [bank[par][1] for par in range(PAR)], bank,
                                        [bank[par][0:2] for par in range(PAR)])
        c = s.sems("w_in wide zeroed")
        k = [s.sems("rows_in turned x_added x_out centered squared var unit modulated made0 made1 made2 made3"
                    " padded0 padded1 padded2 sq2_0 sq2_1 sum0 sum1 len0 len1 sig rate conv inv v_part v_done k_done"
                    " q_done b_done spread", par) for par in range(PAR)]
        block = s.block()
        acc = g.acc[0:N, :]
        CONVS = 3 * LEAD
        cols = lambda i, par: bass.ds(i * (PAR * CH) + par * CH, CH)
        both = range(PAR)

        @block.sync
        def _(sp):
            for dst, name in ((w[:, :, :], "w1_qkv"), (wb[:, :], "w_beta"), (bias[:, :], "b1"), (taps[:, :, :], "taps")):
                sp.dma_start(dst, dram[name]).then_inc(c.w_in, 16)
            with sp.Fori(0, NCH // PAR) as i:
                for par in both:
                    sp.wait_ge(k[par].turned, i)
                    sp.dma_start(rows[:, par], acc[cols(i, par), :].rearrange("(r p) c -> p r c", p=128))\
                        .then_inc(k[par].rows_in, 16)
                for par in both:
                    sp.wait_ge(k[par].x_added, i + 1)
                    sp.dma_start(g.x_kept[:, cols(i, par)], g.xT[:, cols(i, par)]).then_inc(k[par].x_out, 16)
            for par in both:
                sp.wait_ge(k[par].x_out, 16 * (NCH // PAR))

        @block.tensor
        def _(pe):
            pe.wait_ge(c.wide, 2)
            with pe.Fori(0, NCH // PAR) as i:
                for par in both:
                    pe.wait_ge(k[par].rows_in, 16 * (i + 1))
                    pe.wait_ge(k[par].len0, i)
                    for r in range(TILES):
                        last = nc.tensor.transpose(turned[par][:, 128 * r:128 * r + 128], rows[:, par, r, :], g.t("ident"))
                    last.then_inc(k[par].turned, 1)
                for par in both:
                    pe.wait_ge(k[par].x_added, i + 1)
                    pe.wait_ge(k[par].len1, i)
                    nc.tensor.matmul(mid[par][:, :], g.t("center"), g.xT[:, cols(i, par)], start=True, stop=True)\
                        .then_inc(k[par].centered, 1)
                for par in both:
                    pe.wait_ge(k[par].squared, i + 1)
                    nc.tensor.matmul(var[par][:, :], g.t("mean"), unit[:, par, :], start=True, stop=True)\
                        .then_inc(k[par].var, 1)
                for par in both:
                    pe.wait_ge(k[par].modulated, i + 1)
                    pe.wait_ge(k[par].padded2, i)
                    for n, sem in enumerate((k[par].made0, k[par].made1, k[par].made2)):
                        nc.tensor.matmul(made[par][n][:, :], w[:, n, :], h3[:, par, :], start=True, stop=True).then_inc(sem, 1)
                    pe.wait_ge(k[par].rate, i)
                    nc.tensor.matmul(made[par][3][:, :], wb_wide[:, :, :].rearrange("p h d -> p (h d)"), h3[:, par, :],
                                     start=True, stop=True).then_inc(k[par].made3, 1)
                for n in range(2):
                    for par in both:
                        pe.wait_ge((k[par].sq2_0, k[par].sq2_1)[n], i + 1)
                        nc.tensor.matmul(sums[par][n][:, :], g.t("same_head"), sq2[:, par, n, :], start=True, stop=True)\
                            .then_inc((k[par].sum0, k[par].sum1)[n], 1)

        @block.scalar
        def _(act):
            act.wait_ge(c.wide, 2)
            act.wait_ge(c.zeroed, 1)
            with act.Fori(0, NCH // PAR) as i:
                for par in both:
                    act.wait_ge(k[par].centered, i + 1)
                    act.wait_ge(k[par].v_part, i)
                    nc.scalar.activation(unit[:, par, :], mid[par][:, :], ACT.Square).then_inc(k[par].squared, 1)
                for par in both:
                    act.wait_ge(k[par].unit, i + 1)
                    act.wait_ge(k[par].made3, i)
                    for j in range(BPC):
                        b = i * (PAR * BPC) + par * BPC + j
                        last = nc.scalar.activation(h3[:, par, j * T:(j + 1) * T], unit[:, par, j * T:(j + 1) * T],
                                                    ACT.Identity, scale=g.mod[:, 1, 1, bass.ds(b, 1)],
                                                    bias=g.mod[:, 1, 0, bass.ds(b, 1)])
                    last.then_inc(k[par].modulated, 1)
                for n in range(3):
                    for par in both:
                        if n == 0:
                            act.wait_ge(k[par].v_done, i)
                            act.wait_ge(k[par].q_done, i)
                        act.wait_ge((k[par].made0, k[par].made1, k[par].made2)[n], i + 1)
                        nc.scalar.activation(pad[:, par, n, :, LEAD:LEAD + T],
                                             made[par][n][:, :].rearrange("p (b t) -> p b t", t=T),
                                             ACT.Identity, bias=bias[:, n:n + 1])
                        nc.scalar.activation(conv[:, par, n, :], made[par][n][:, :], ACT.Identity, scale=taps[:, n, LEAD:CONV],
                                             bias=last_bias[:, n:n + 1])\
                            .then_inc((k[par].padded0, k[par].padded1, k[par].padded2)[n], 1)
                for par in both:
                    act.wait_ge(k[par].made3, i + 1)
                    act.wait_ge(k[par].b_done, i)
                    nc.scalar.activation(rate[:, par, :], made[par][3][:, :], ACT.Sigmoid, bias=bias[:, 3:4])\
                        .then_inc(k[par].rate, 1)
                for n in range(2):
                    for par in both:
                        act.wait_ge(k[par].conv, CONVS * i + LEAD * (n + 1))
                        nc.scalar.activation(sq2[:, par, n, :], conv[:, par, n, :], ACT.Square)\
                            .then_inc((k[par].sq2_0, k[par].sq2_1)[n], 1)
                for par in both:
                    act.wait_ge(k[par].conv, CONVS * (i + 1))
                    nc.scalar.activation(unit[:, par, :], conv[:, par, 2, :], ACT.Sigmoid).then_inc(k[par].sig, 1)

        @block.vector
        def _(dve):
            nc.vector.memset(pad[:, :, :, :, 0:LEAD], 0.0).then_inc(c.zeroed, 1)
            dve.wait_ge(c.w_in, 64)
            nc.vector.tensor_copy(wb_wide[:, :, :], wb[:, :, None].to_broadcast([128, H1, DH1])).then_inc(c.wide, 1)
            nc.vector.tensor_tensor(last_bias[:, :], bias[:, 0:3], taps[:, :, LEAD], ALU.mult).then_inc(c.wide, 1)
            with dve.Fori(0, NCH // PAR) as i:
                for par in both:
                    dve.wait_ge(k[par].turned, i + 1)
                    for j in range(BPC):
                        b = i * (PAR * BPC) + par * BPC + j
                        x = g.xT[:, bass.ds(b * T, T)]
                        last = nc.vector.scalar_tensor_tensor(x, turned[par][:, j * T:(j + 1) * T],
                                                              g.mod[:, 0, 5, bass.ds(b, 1)], x, ALU.mult, ALU.add)
                    last.then_inc(k[par].x_added, 1)
                run_roots(nc, dve, rstd, [var[par][:, :] for par in both], LN_EPS, i, [k[par].var for par in both])
                for par in both:
                    nc.vector.tensor_tensor(unit[:, par, :], mid[par][:, :], rstd[par].out[:, :], ALU.mult)\
                        .then_inc(k[par].unit, 1)
                then = [Chain(dve, k[par].conv, CONVS, i) for par in both]
                for n in range(3):
                    for tap in range(LEAD):
                        for par in both:
                            if tap == 0:
                                dve.wait_ge((k[par].padded0, k[par].padded1, k[par].padded2)[n], i + 1)
                            else:
                                then[par].done()
                            out = conv[:, par, n, :].rearrange("p (b t) -> p b t", t=T)
                            then[par](nc.vector.scalar_tensor_tensor(out, pad[:, par, n, :, tap:tap + T],
                                                                     taps[:, n, tap:tap + 1], out, ALU.mult, ALU.add),
                                      wait=False)
                for n in range(2):
                    for par in both:
                        dve.wait_ge((k[par].sum0, k[par].sum1)[n], i + 1)
                        nc.vector.transpose(len_t[:, par, n].rearrange("p n i -> p (n i)"), sums[par][n][:, :])\
                            .then_inc((k[par].len0, k[par].len1)[n], 1)
                STEPS = 5
                then = [Chain(dve, k[par].inv, STEPS, i) for par in both]
                own = [len_t[:, par].rearrange("p s n (h d) -> p (s n h) d", d=DH1)[:, :, 0] for par in both]
                flat = [inv[:, par].rearrange("p s n h -> p (s n h)") for par in both]
                for par in both:
                    dve.wait_ge(k[par].len0, i + 1)
                    dve.wait_ge(k[par].len1, i + 1)
                    then[par](nc.vector.tensor_scalar(root[par].v[:, :], own[par], 1e-30, None, ALU.max), wait=False)
                for par in both:
                    then[par].done()
                newton_roots(nc, dve, root, i)
                for par in both:
                    then[par](nc.vector.tensor_tensor(flat[par], own[par], root[par].y[:, :], ALU.mult), wait=False)
                for par in both:
                    then[par].done()
                    then[par](nc.vector.tensor_scalar(flat[par], flat[par], 1e-6, None, ALU.add), wait=False)
                for par in both:
                    then[par].done()
                    then[par](nc.vector.reciprocal(flat[par], flat[par]), wait=False)
                for par in both:
                    then[par].done()
                    queries = inv[:, par, 1].rearrange("p (b n) h -> p b n h", b=BPC)
                    then[par](nc.vector.tensor_tensor(queries, queries, g.t("inv_weight_t")[:, None, :, None]
                                                      .to_broadcast([128, BPC, KB, HEADS_IN_BLOCK]), ALU.mult), wait=False)
                for par in both:
                    dve.wait_ge(k[par].x_out, 16 * (i + 1))
                    then[par].done()
                for n in range(2):
                    for par in both:
                        nc.vector.tensor_copy(len_t[:, par, n].rearrange("p n (h d) -> p (n h) d", d=DH1),
                                              inv[:, par, n].rearrange("p n h -> p (n h)")[:, :, None]
                                              .to_broadcast([128, RC * HEADS_IN_BLOCK, DH1])).then_inc(k[par].spread, 1)
                    for par in both:
                        dve.wait_ge(k[par].spread, 4 * i + 2 * n + 1)
                        nc.vector.transpose(sq2[:, par, n, :], len_t[:, par, n].rearrange("p n i -> p (n i)"))\
                            .then_inc(k[par].spread, 1)
                    for par in both:
                        dve.wait_ge(k[par].spread, 4 * i + 2 * n + 2)
                        nc.vector.tensor_tensor((g.kT, g.qT)[n][:, cols(i, par)], conv[:, par, n, :], sq2[:, par, n, :],
                                                ALU.mult).then_inc((k[par].k_done, k[par].q_done)[n], 1)

        @block.gpsimd
        def _(pool):
            with pool.Fori(0, NCH // PAR) as i:
                for par in both:
                    pool.wait_ge(k[par].sig, i + 1)
                    nc.gpsimd.tensor_tensor(conv[:, par, 2, :], unit[:, par, :], conv[:, par, 2, :], ALU.mult)\
                        .then_inc(k[par].v_part, 1)
                for par in both:
                    pool.wait_ge(k[par].v_part, i + 1)
                    pool.wait_ge(k[par].rate, i + 1)
                    nc.gpsimd.tensor_tensor(g.vT[:, cols(i, par)], conv[:, par, 2, :], rate[:, par, :], ALU.mult)\
                        .then_inc(k[par].v_done, 1)
                for par in both:
                    pool.wait_ge(k[par].k_done, i + 1)
                    nc.gpsimd.tensor_tensor(g.bT[:, cols(i, par)], g.kT[:, cols(i, par)], rate[:, par, :], ALU.mult)\
                        .then_inc(k[par].b_done, 1)


def delta_phase(nc, dram, g):
    COLS = B * DH1
    HALF = DH1 // 2
    with Scope(nc, "delta") as s:
        wide = s.sb("wide", [128, 2, 3, GT, COLS])
        W = s.sb("W", [128, 2, COLS])
        A = s.sb("A", [128, COLS])
        sW = s.sb("sW", [128, 2, COLS])
        m1 = s.sb("m1", [128, 2, B, DH1 + 1])
        m2 = s.sb("m2", [128, 2, COLS])
        m3 = s.sb("m3", [128, 2, GT // 2, COLS])
        seen = s.sb("seen", [128, 1])
        u = s.sb("u", [128, 2, B])
        ps = [[s.ps(f"ps{a}{i}") for i in range(HALF)] for a in range(2)]
        k = s.sems("zeroed picked0 picked1 evac0 evac1 less_v scaled A m3_0 m3_1 out0 out1")
        half_b = [s.sems("product u m2 W", h) for h in range(2)]
        picked, evac, m3_done, out_done = ((k.picked0, k.picked1), (k.evac0, k.evac1), (k.m3_0, k.m3_1), (k.out0, k.out1))
        block = s.block()
        BODY = 2 * GT
        BODIES = T // BODY
        QUART = GT // 2
        src = (g.bT, g.kT, g.qT)

        def part(h):
            return slice(h * COLS // 2, (h + 1) * COLS // 2)

        def some(h):
            return slice(h * B // 2, (h + 1) * B // 2)

        def by_batch(x, first, count):
            return x[:, :].rearrange("p (b t) -> p b t", t=T)[:, :, bass.ds(first, count)]

        @block.tensor
        def _(pe):
            def pick(first, n):
                moving = by_batch(src[n % 3], first, GT)
                for d in range(DH1):
                    last = nc.tensor.matmul(ps[n % 2][d // 2][:, (d % 2) * COLS:(d % 2 + 1) * COLS],
                                            g.t(f"pick{d}"), moving, start=True, stop=True)
                last.then_inc(picked[n % 2], 1)
            for n in range(3):
                if n == 2:
                    pe.wait_ge(evac[0], 1)
                pick(0, n)
            def ahead(i, n):
                pe.wait_ge(evac[n % 2], 3 * i + (n - 2) // 2 + 1)
                pick(i * BODY + GT * (n // 3), n)
            with pe.Fori(0, BODIES - 1) as i:
                for n in range(3, 9):
                    ahead(i, n)
            for n in range(3, 6):
                ahead(BODIES - 1, n)

        @block.scalar
        def _(act):
            def spread(i, n, h, dd):
                to = wide[:, (n // 3) % 2, n % 3].rearrange("p t (b d) -> p d b t", d=DH1)
                return nc.scalar.activation(to[:, 2 * h + dd], ps[n % 2][h][:, dd * COLS:(dd + 1) * COLS]
                                            .rearrange("p (b t) -> p b t", t=GT), ACT.Copy)

            def less_value(i, t):
                if isinstance(i, int) and BODY * i + t == T:
                    return
                for h in range(2):
                    act.wait_ge(half_b[h].u, BODY * i + max(t - 1, 0))
                nc.scalar.activation(m1[:, t % 2, :, DH1], by_batch(g.vT, BODY * i + t, 1)[:, :, 0], ACT.Copy, scale=-1.0)\
                    .then_inc(k.less_v, 1)

            def body(i, halves_ahead):
                for half in range(2):
                    if half in halves_ahead:
                        for par in range(2):
                            act.wait_ge(half_b[par].m2, BODY * i + GT * half)
                            act.wait_ge(m3_done[par], GT * i + GT // 2 * half)
                    for t in range(GT):
                        if half in halves_ahead:
                            for piece in range(3 * t, 3 * t + 3):
                                n = 3 + 3 * half + piece // DH1
                                if piece % DH1 == 0:
                                    act.wait_ge(picked[n % 2], 3 * i + n // 2 + 1)
                                ins = spread(i, n, piece % DH1 // 2, piece % 2)
                                if piece % DH1 == DH1 - 1:
                                    ins.then_inc(evac[n % 2], 1)
                        step = BODY * i + GT * half + t
                        less_value(i, GT * half + t + 1)
                        for h in range(2):
                            act.wait_ge(half_b[h].W, step + 1)
                        act.wait_ge(k.A, BODY * i + max(GT * half + t - 1, 0))
                        nc.scalar.activation(sW[:, t % 2, :], W[:, (t + 1) % 2, :], ACT.Copy,
                                             scale=g.t("step")[:, bass.ds(step, 1)]).then_inc(k.scaled, 1)
            for n in range(3):
                act.wait_ge(picked[n % 2], n // 2 + 1)
                for piece in range(DH1):
                    last = spread(0, n, piece // 2, piece % 2)
                last.then_inc(evac[n % 2], 1)
            act.wait_ge(k.zeroed, 2)
            nc.scalar.activation(m1[:, 0, :, DH1], by_batch(g.vT, 0, 1)[:, :, 0], ACT.Copy, scale=-1.0).then_inc(k.less_v, 1)
            with act.Fori(0, BODIES - 1) as i:
                body(i, (0, 1))
            body(BODIES - 1, (0,))

        @block.vector
        def _(dve):
            nc.vector.memset(W[:, 0, :], 0.0).then_inc(k.zeroed, 1)
            nc.vector.memset(A[:, :], 0.0).then_inc(k.zeroed, 1)
            dve.wait_ge(k.zeroed, 2)
            pairs = lambda ap: ap.rearrange("p (b d) -> p b d", d=DH1)

            def outputs(i, quarter):
                nc.vector.tensor_reduce(by_batch(g.vT, i * BODY + QUART * quarter, QUART).rearrange("p b t -> p t b"),
                                        m3[:, quarter % 2, :, :].rearrange("p t (b d) -> p t b d", d=DH1), AX.X, ALU.add)\
                    .then_inc(out_done[quarter % 2], 1)

            def products(i, quarter):
                dve.wait_ge(m3_done[quarter % 2], GT * i + QUART * (quarter // 2 + 1))
            with dve.Fori(0, BODIES) as i:
                for half in range(2):
                    for a in range(2):
                        dve.wait_ge(evac[a], 3 * i + (3 if half else 2 - a))
                    for t in range(GT):
                        step = BODY * i + GT * half + t
                        quarter = (GT * half + t) // QUART
                        sums = t % QUART == QUART - 1 and quarter > 0
                        if sums:
                            products(i, quarter - 1)
                        for h in range(2):
                            if half or t:
                                dve.wait_ge(half_b[h].W, step)
                            nc.vector.tensor_tensor(m1[:, t % 2, some(h), 0:DH1], pairs(W[:, t % 2, part(h)]),
                                                    pairs(wide[:, half, 0, t, part(h)]), ALU.mult)\
                                .then_inc(half_b[h].product, 1)
                        if sums:
                            outputs(i, quarter - 1)
                        for h in range(2):
                            dve.wait_ge(k.less_v, step + 1)
                            dve.wait_ge(half_b[h].product, step + 1)
                            nc.vector.tensor_reduce(u[:, t % 2, some(h)], m1[:, t % 2, some(h), :], AX.X, ALU.add)\
                                .then_inc(half_b[h].u, 1)
                        for h in range(2):
                            dve.wait_ge(half_b[h].u, step + 1)
                            nc.vector.tensor_tensor(pairs(m2[:, t % 2, part(h)]), pairs(wide[:, half, 1, t, part(h)]),
                                                    u[:, t % 2, some(h), None].to_broadcast([128, B // 2, DH1]), ALU.mult)\
                                .then_inc(half_b[h].m2, 1)
                        for h in range(2):
                            dve.wait_ge(half_b[h].m2, step + 1)
                            dve.wait_ge(k.scaled, BODY * i + max(GT * half + t - 1, 0))
                            nc.vector.tensor_tensor(W[:, (t + 1) % 2, part(h)], W[:, t % 2, part(h)], m2[:, t % 2, part(h)],
                                                    ALU.subtract).then_inc(half_b[h].W, 1)
                for h in range(2):
                    dve.wait_ge(half_b[h].W, BODY * (i + 1))
                products(i, 3)
                nc.vector.tensor_copy(seen[:, :], m3[:, 1, 0, 0:1])
                outputs(i, 3)

        @block.gpsimd
        def _(pool):
            pool.wait_ge(k.zeroed, 2)
            with pool.Fori(0, BODIES) as i:
                for t in range(BODY):
                    step = BODY * i + t
                    par, place = t // QUART % 2, t % QUART
                    if place == 0:
                        pool.wait_ge(out_done[par], 2 * i + t // GT)
                    pool.wait_ge(k.scaled, step + 1)
                    if place:
                        pool.wait_ge(m3_done[par], GT * i + QUART * (t // GT) + place)
                    else:
                        pool.wait_ge(m3_done[1 - par], GT * i + QUART * ((t + QUART) // GT))
                    nc.gpsimd.tensor_tensor(A[:, :], A[:, :], sW[:, t % 2, :], ALU.add).then_inc(k.A, 1)
                    pool.wait_ge(k.A, step + 1)
                    nc.gpsimd.tensor_tensor(m3[:, par, place, :], A[:, :], wide[:, t // GT, 2, t % GT, :], ALU.mult)\
                        .then_inc(m3_done[par], 1)


def mix_phase(nc, dram, g):
    HEADS_IN_BLOCK = SLOT // DH1
    with Scope(nc, "mix") as s:
        w_out = s.sb("w_out", [128, D])
        router = s.sb("router", [128, E1])
        per_channel = s.sb("per_channel", [128, 3])
        sq = s.sb("sq", [128, PAR, 3, CH])
        ms = s.sb("ms", [128, PAR, RC, SLOT])
        scale = s.sb("scale", [128, PAR, CH])
        on = s.sb("on", [128, PAR, CH])
        mixed = s.sb("mixed", [128, PAR, CH])
        unit = s.sb("unit", [128, PAR, CH])
        h4 = s.sb("h4", [128, PAR, CH])
        xn = s.sb("xn", [128, PAR, CH])
        score = s.sb("score", [128, PAR, TILES, E1])
        top = s.sb("top", [128, PAR, TILES, 8])
        top_at = s.sb("top_at", [128, PAR, TILES, 8], U32)
        chosen = s.sb("chosen", [128, PAR, TILES, K1])
        onehot = s.sb("onehot", [128, PAR, TILES, E1, K1])
        mask = s.sb("mask", [128, PAR, TILES, E1])
        less = s.sb("less", [128, PAR, TILES, E1])
        ex = s.sb("ex", [128, PAR, TILES, E1])
        total = s.sb("total", [128, PAR, TILES])
        seen = s.sb("seen", [128, PAR, 2])
        gates = s.sb("gates", [128, PAR, TILES, E1])
        head_root = [Rstd(s, f"head{par}", RC * HEADS_IN_BLOCK, parts=False) for par in range(PAR)]
        rstd = [[Rstd(s, f"rstd{i}{par}") for par in range(PAR)] for i in range(2)]
        bank = [[s.ps(f"bank{i}{par}") for i in range(4)] for par in range(PAR)]
        heads, out_ps, mid, var, rms, logits, turned = ([bank[par][n] for par in range(PAR)] for n in (0, 1, 0, 1, 2, 3, 2))
        c = s.sems("w_in w_ready x_in")
        k = [s.sems("sq0 heads head_read head_steps on out_made mixed x_added centered squared var unit"
                    " modulated sq2 rms xn logits score route exp gates turned gates_out skipped xn_copied", par)
             for par in range(PAR)]
        block = s.block()
        STEPS = 2 * TILES + 7
        cols = lambda i, par: bass.ds(i * (PAR * CH) + par * CH, CH)
        both = range(PAR)

        @block.sync
        def _(sp):
            for dst, name in ((w_out[:, :], "w1_out"), (router[:, :], "router"), (per_channel[:, :], "cols1")):
                sp.dma_start(dst, dram[name]).then_inc(c.w_in, 16)
            sp.dma_start(g.keptT[:, :], g.x_kept).then_inc(c.x_in, 16)

        @block.tensor
        def _(pe):
            pe.wait_ge(c.w_ready, 1)
            pe.wait_ge(c.x_in, 16)
            with pe.Fori(0, NCH // PAR) as i:
                for par in both:
                    pe.wait_ge(k[par].sq0, i + 1)
                    pe.wait_ge(k[par].unit, i)
                    nc.tensor.matmul(heads[par][:, :], g.t("same_head"), sq[:, par, 0, :], start=True, stop=True)\
                        .then_inc(k[par].heads, 1)
                for par in both:
                    pe.wait_ge(k[par].on, i + 1)
                    nc.tensor.matmul(out_ps[par][:, :], w_out[:, :], on[:, par, :], start=True, stop=True)\
                        .then_inc(k[par].out_made, 1)
                for par in both:
                    pe.wait_ge(k[par].x_added, i + 1)
                    nc.tensor.matmul(mid[par][:, :], g.t("center"), g.keptT[:, cols(i, par)], start=True, stop=True)\
                        .then_inc(k[par].centered, 1)
                for par in both:
                    pe.wait_ge(k[par].squared, i + 1)
                    nc.tensor.matmul(var[par][:, :], g.t("mean"), sq[:, par, 1, :], start=True, stop=True)\
                        .then_inc(k[par].var, 1)
                for par in both:
                    pe.wait_ge(k[par].sq2, i + 1)
                    pe.wait_ge(k[par].gates_out, i)
                    nc.tensor.matmul(rms[par][:, :], g.t("mean"), sq[:, par, 2, :], start=True, stop=True)\
                        .then_inc(k[par].rms, 1)
                for par in both:
                    pe.wait_ge(k[par].xn, i + 1)
                    pe.wait_ge(k[par].score, i)
                    for j in range(TILES):
                        last = nc.tensor.matmul(logits[par][:, j * E1:(j + 1) * E1], xn[:, par, 128 * j:128 * j + 128],
                                                router[:, :], start=True, stop=True)
                    last.then_inc(k[par].logits, 1)
                for par in both:
                    pe.wait_ge(k[par].gates, i + 1)
                    for j in range(TILES):
                        last = nc.tensor.transpose(turned[par][0:E1, 128 * j:128 * j + 128], gates[:, par, j, :],
                                                   g.t("ident"))
                    last.then_inc(k[par].turned, 1)

        @block.scalar
        def _(act):
            act.wait_ge(c.w_in, 48)

            def head_squares(i):
                for par in both:
                    nc.scalar.activation(sq[:, par, 0, :], g.vT[:, cols(i, par)], ACT.Square).then_inc(k[par].sq0, 1)

            with act.Fori(0, NCH // PAR) as i:
                for par in both:
                    act.wait_ge(k[par].heads, i)
                head_squares(i)
                for par in both:
                    act.wait_ge(k[par].out_made, i + 1)
                    nc.scalar.activation(mixed[:, par, :], out_ps[par][:, :], ACT.Identity, bias=per_channel[:, 1:2])\
                        .then_inc(k[par].mixed, 1)
                for par in both:
                    act.wait_ge(k[par].centered, i + 1)
                    nc.scalar.activation(sq[:, par, 1, :], mid[par][:, :], ACT.Square).then_inc(k[par].squared, 1)
                for par in both:
                    act.wait_ge(k[par].unit, i + 1)
                    act.wait_ge(k[par].skipped, i)
                    for j in range(BPC):
                        b = i * (PAR * BPC) + par * BPC + j
                        last = nc.scalar.activation(h4[:, par, j * T:(j + 1) * T], unit[:, par, j * T:(j + 1) * T],
                                                    ACT.Identity, scale=g.mod[:, 1, 4, bass.ds(b, 1)],
                                                    bias=g.mod[:, 1, 3, bass.ds(b, 1)])
                    last.then_inc(k[par].modulated, 1)
                for par in both:
                    act.wait_ge(k[par].modulated, i + 1)
                    nc.scalar.activation(sq[:, par, 2, :], h4[:, par, :], ACT.Square).then_inc(k[par].sq2, 1)
                for par in both:
                    act.wait_ge(k[par].xn, i + 1)
                    nc.scalar.activation(g.normT[:, cols(i, par)], xn[:, par, :], ACT.Copy).then_inc(k[par].xn_copied, 1)
                for par in both:
                    act.wait_ge(k[par].logits, i + 1)
                    nc.scalar.activation(score[:, par].rearrange("p j e -> p (j e)"), logits[par][:, 0:TILES * E1], ACT.Copy)\
                        .then_inc(k[par].score, 1)
                for par in both:
                    act.wait_ge(k[par].route, STEPS * i + 2 * TILES + 1)
                    nc.scalar.activation(ex[:, par], less[:, par], ACT.Exp).then_inc(k[par].exp, 1)
                for par in both:
                    act.wait_ge(k[par].turned, i + 1)
                    nc.scalar.activation(g.gatesT[:, cols(i, par)], turned[par][0:E1, :], ACT.Copy).then_inc(k[par].gates_out, 1)

        @block.vector
        def _(dve):
            dve.wait_ge(c.w_in, 48)
            nc.vector.tensor_scalar(w_out[:, :], w_out[:, :], per_channel[:, 0:1], None, ALU.mult).then_inc(c.w_ready, 1)
            dve.wait_ge(c.x_in, 16)
            with dve.Fori(0, NCH // PAR) as i:
                for par in both:
                    dve.wait_ge(k[par].heads, i + 1)
                    nc.vector.transpose(ms[:, par].rearrange("p n i -> p (n i)"), heads[par][:, :]).then_inc(k[par].head_read, 1)
                then = [Chain(dve, k[par].head_steps, 3, i) for par in both]
                by_head = [ms[:, par].rearrange("p n (h d) -> p (n h) d", d=DH1) for par in both]
                for par in both:
                    dve.wait_ge(k[par].head_read, i + 1)
                    then[par](nc.vector.tensor_scalar(head_root[par].v[:, :], by_head[par][:, :, 0], 1.0 / DH1, RMS_EPS,
                                                      ALU.mult, ALU.add), wait=False)
                for par in both:
                    then[par].done()
                newton_roots(nc, dve, head_root, i)
                for par in both:
                    then[par](nc.vector.tensor_copy(by_head[par], head_root[par].y[:, :, None]
                                                    .to_broadcast([128, RC * HEADS_IN_BLOCK, DH1])), wait=False)
                for par in both:
                    then[par].done()
                    then[par](nc.vector.transpose(scale[:, par, :], ms[:, par].rearrange("p n i -> p (n i)")), wait=False)
                for par in both:
                    then[par].done()
                    nc.vector.tensor_tensor(on[:, par, :], g.vT[:, cols(i, par)], scale[:, par, :], ALU.mult)\
                        .then_inc(k[par].on, 1)
                for par in both:
                    dve.wait_ge(k[par].mixed, i + 1)
                    for j in range(BPC):
                        b = i * (PAR * BPC) + par * BPC + j
                        x = g.keptT[:, bass.ds(b * T, T)]
                        last = nc.vector.scalar_tensor_tensor(x, mixed[:, par, j * T:(j + 1) * T],
                                                              g.mod[:, 1, 2, bass.ds(b, 1)], x, ALU.mult, ALU.add)
                    last.then_inc(k[par].x_added, 1)
                run_roots(nc, dve, rstd[0], [var[par][:, :] for par in both], LN_EPS, i, [k[par].var for par in both])
                for par in both:
                    nc.vector.tensor_tensor(unit[:, par, :], mid[par][:, :], rstd[0][par].out[:, :], ALU.mult)\
                        .then_inc(k[par].unit, 1)
                run_roots(nc, dve, rstd[1], [rms[par][:, :] for par in both], RMS_EPS, i, [k[par].rms for par in both])
                for par in both:
                    dve.wait_ge(k[par].xn_copied, i)
                    dve.wait_ge(k[par].logits, i)
                    nc.vector.scalar_tensor_tensor(xn[:, par, :], h4[:, par, :], per_channel[:, 2:3], rstd[1][par].out[:, :],
                                                   ALU.mult, ALU.mult).then_inc(k[par].xn, 1)
                for par in both:
                    dve.wait_ge(k[par].centered, i + 1)
                    for j in range(BPC):
                        b = i * (PAR * BPC) + par * BPC + j
                        x = g.keptT[:, bass.ds(b * T, T)]
                        last = nc.vector.scalar_tensor_tensor(x, h4[:, par, j * T:(j + 1) * T],
                                                              g.mod[:, 1, 5, bass.ds(b, 1)], x, ALU.mult, ALU.add)
                    last.then_inc(k[par].skipped, 1)
                then = [Chain(dve, k[par].route, STEPS, i) for par in both]
                for par in both:
                    dve.wait_ge(k[par].score, i + 1)
                    nc.vector.tensor_copy(seen[:, par, 0:1], score[:, par, 0, 0:1])
                    for j in range(TILES):
                        then[par](nc.vector.max(top[:, par, j, :], score[:, par, j, :]), wait=False)
                for par in both:
                    then[par].done()
                    nc.vector.tensor_copy(seen[:, par, 1:2], top[:, par, 0, 0:1])
                    for j in range(TILES):
                        then[par](nc.vector.max_index(top_at[:, par, j, :], top[:, par, j, :], score[:, par, j, :]), wait=False)
                    then[par](nc.vector.tensor_tensor(less[:, par], score[:, par], top[:, par, :, 0:1]
                                                      .to_broadcast([128, TILES, E1]), ALU.subtract), wait=False)
                for par in both:
                    then[par].done()
                    then[par](nc.vector.tensor_copy(chosen[:, par], top_at[:, par, :, 0:K1]), wait=False)
                for par in both:
                    then[par].done()
                    then[par](nc.vector.tensor_tensor(onehot[:, par], g.t("iota")[:, None, 0:E1, None]
                                                      .to_broadcast([128, TILES, E1, K1]),
                                                      chosen[:, par, :, None, :].to_broadcast([128, TILES, E1, K1]),
                                                      ALU.is_equal), wait=False)
                for par in both:
                    then[par].done()
                    then[par](nc.vector.tensor_reduce(mask[:, par], onehot[:, par], AX.X, ALU.add), wait=False)
                for par in both:
                    dve.wait_ge(k[par].exp, i + 1)
                    then[par].done()
                    then[par](nc.vector.tensor_tensor(mask[:, par], mask[:, par], ex[:, par], ALU.mult), wait=False)
                    then[par](nc.vector.tensor_reduce(total[:, par], ex[:, par], AX.X, ALU.add), wait=False)
                for par in both:
                    then[par].done()
                    then[par](nc.vector.reciprocal(total[:, par], total[:, par]), wait=False)
                for par in both:
                    then[par].done()
                    nc.vector.tensor_tensor(gates[:, par], mask[:, par], total[:, par, :, None]
                                            .to_broadcast([128, TILES, E1]), ALU.mult).then_inc(k[par].gates, 1)


def ffn_phase(nc, dram, g, out):
    P = len(HC)
    with Scope(nc, "ffn") as s:
        w_up = s.sb("w_up", [128, E1, 2 * HID])
        w_down = s.sb("w_down", [128, E1, P, D])
        xs = s.sb("xs", [128, 2, CH])
        sg = s.sb("sg", [128, P, CH])
        hid = s.sb("hid", [128, 2, P, CH])
        y = s.sb("y", [128, CH])
        rows = s.sb("rows", [128, TILES, D])
        gates_ps = s.ps("gates")
        acc = s.ps("acc")
        val = [s.ps(f"val{p}") for p in range(P)]
        gate = [s.ps(f"gate{p}") for p in range(P)]
        k = s.sems("w_in spread xs val0 val1 val2 gate0 gate1 gate2 sg0 sg1 sg2 hid0 hid1 hid2 down acc y turned rows out")
        val_made, gate_made = (k.val0, k.val1, k.val2), (k.gate0, k.gate1, k.gate2)
        sg_made, hid_made = (k.sg0, k.sg1, k.sg2), (k.hid0, k.hid1, k.hid2)
        block = s.block()
        out_rows = out.rearrange("b t c -> (b t) c")

        @block.sync
        def _(sp):
            sp.dma_start(w_up[:, :, :], dram["w_up"]).then_inc(k.w_in, 16)
            sp.dma_start(w_down[:, :, :, :], dram["w_down"]).then_inc(k.w_in, 16)
            with sp.Fori(0, NCH) as it:
                sp.wait_ge(k.rows, it + 1)
                sp.dma_start(out_rows[bass.ds(it * CH, CH), :].rearrange("(r p) c -> p r c", p=128), rows[:, :, :])\
                    .then_inc(k.out, 16)
            sp.wait_ge(k.out, 16 * NCH)

        @block.tensor
        def _(pe):
            pe.wait_ge(k.w_in, 32)
            with pe.Fori(0, NCH) as it:
                cols = bass.ds(it * CH, CH)

                def spread(e):
                    nc.tensor.matmul(gates_ps[:, :], g.t("ident")[0:E1, e:e + 1].to_broadcast([E1, 128]),
                                     g.gatesT[:, cols], start=True, stop=True).then_inc(k.spread, 1)

                def down(e):
                    if e == 0:
                        pe.wait_ge(k.y, it)
                    for p, (at, size) in enumerate(HC):
                        pe.wait_ge(hid_made[p], E1 * it + e + 1)
                        last = nc.tensor.matmul(acc[:, :], w_down[0:size, e, p, :], hid[0:size, e % 2, p, :],
                                                start=e == 0 and p == 0, stop=e == E1 - 1 and p == P - 1)
                    last.then_inc(k.down, 1)
                for e in range(E1):
                    for p, (at, size) in enumerate(HC):
                        pe.wait_ge(sg_made[p], E1 * it + e)
                        if e == 0 and p == 1:
                            pe.wait_ge(k.rows, it)
                        nc.tensor.matmul(gate[p][0:size, :], w_up[:, e, HID + at:HID + at + size], g.normT[:, cols],
                                         start=True, stop=True).then_inc(gate_made[p], 1)
                        if e == 0 and p == 1:
                            spread(0)
                    if e:
                        down(e - 1)
                    pe.wait_ge(k.xs, E1 * it + e + 1)
                    for p, (at, size) in enumerate(HC):
                        pe.wait_ge(hid_made[p], E1 * it + e)
                        nc.tensor.matmul(val[p][0:size, :], w_up[:, e, at:at + size], xs[:, e % 2, :],
                                         start=True, stop=True).then_inc(val_made[p], 1)
                    if e < E1 - 1:
                        spread(e + 1)
                down(E1 - 1)
                pe.wait_ge(k.y, it + 1)
                for r in range(TILES):
                    last = nc.tensor.transpose(gates_ps[:, 128 * r:128 * r + 128], y[:, 128 * r:128 * r + 128], g.t("ident"))
                last.then_inc(k.turned, 1)

        @block.scalar
        def _(act):
            with act.Fori(0, NCH) as it:
                for e in range(E1):
                    for p, (at, size) in enumerate(HC):
                        act.wait_ge(gate_made[p], E1 * it + e + 1)
                        act.wait_ge(hid_made[p], E1 * it + e)
                        nc.scalar.activation(sg[0:size, p, :], gate[p][0:size, :], ACT.Silu).then_inc(sg_made[p], 1)
                act.wait_ge(k.turned, it + 1)
                act.wait_ge(k.out, 16 * it)
                nc.scalar.activation(rows[:, :, :], gates_ps[:, :].rearrange("p (r c) -> p r c", c=D), ACT.Copy)\
                    .then_inc(k.rows, 1)

        @block.vector
        def _(dve):
            with dve.Fori(0, NCH) as it:
                cols = bass.ds(it * CH, CH)
                for e in range(E1):
                    dve.wait_ge(val_made[P - 1], E1 * it + max(e - 1, 0))
                    dve.wait_ge(k.spread, E1 * it + e + 1)
                    nc.vector.tensor_tensor(xs[:, e % 2, :], g.normT[:, cols], gates_ps[:, :], ALU.mult).then_inc(k.xs, 1)
                    dve.wait_ge(k.down, E1 * it + max(e - 1, 0))
                    for p, (at, size) in enumerate(HC):
                        dve.wait_ge(val_made[p], E1 * it + e + 1)
                        dve.wait_ge(sg_made[p], E1 * it + e + 1)
                        nc.vector.tensor_tensor(hid[0:size, e % 2, p, :], sg[0:size, p, :], val[p][0:size, :], ALU.mult)\
                            .then_inc(hid_made[p], 1)
                dve.wait_ge(k.down, E1 * (it + 1))
                dve.wait_ge(k.turned, it)
                for j in range(BPC):
                    last = nc.vector.scalar_tensor_tensor(y[:, j * T:(j + 1) * T], acc[:, j * T:(j + 1) * T],
                                                          g.mod[:, 1, 5, bass.ds(it * BPC + j, 1)],
                                                          g.keptT[:, bass.ds(it * CH + j * T, T)], ALU.mult, ALU.add)
                last.then_inc(k.y, 1)


def launch_arrays(inputs):
    a = {k: np.asarray(v) for k, v in inputs.items()}
    out = {}
    f, bf = constants()
    out["tables"] = np.concatenate(list(f.values()), 1)
    out["tables_bf"] = np.concatenate(list(bf.values()), 1)
    out["x"] = a["L0_attn_x"]
    for layer in range(2):
        out[f"c{layer}"] = a[f"L{layer}_c"].T
        out[f"wmod{layer}"] = a[f"L{layer}_wmod"]
    out["ln"] = np.stack([a["L0_attn_ln_g"], a["L0_attn_ln_b"]], 1)

    def slots(w):
        z = np.zeros((H0, SLOT) + w.shape[1:], w.dtype)
        z[:, :DH0] = w.reshape((H0, DH0) + w.shape[1:])
        return z.reshape((GROUPS, PER * SLOT) + w.shape[1:])
    half = DH0 // 2
    turn = np.concatenate([np.arange(half, DH0), np.arange(half)])
    turned = lambda w: w.reshape(H0, DH0, D)[:, turn].reshape(D, D)
    wq, wk, wv = (a[f"L0_attn_W{n}"] for n in "qkv")
    out["w_attn"] = np.stack([slots(w).transpose(2, 0, 1) for w in (wq, turned(wq), wk, turned(wk), wv)], 1)
    out["wo"] = slots(a["L0_attn_Wo"].T).transpose(1, 0, 2)
    rows = np.zeros((GROUPS, PER, SLOT, PER, SLOT), np.float32)
    wide = np.zeros((GROUPS, PER, SLOT, PER, SLOT), np.float32)
    for gr in range(GROUPS):
        for h in range(PER):
            rows[gr, h, :GEO_D, h, gr] = a["L0_attn_head_dirs"][gr * PER + h]
            wide[gr, h, :GEO_D, h, :] = a["L0_attn_head_dirs"][gr * PER + h][:, None]
    out["dirs"] = np.stack([rows, wide]).reshape(2, GROUPS, 128, 128).transpose(2, 0, 1, 3)
    out["hs"] = np.repeat(a["L0_attn_head_scales"].reshape(GROUPS, PER), SLOT, 1).T
    out["gate_w"] = a["L0_ffn_gate_w"].T
    out["gate_bias"] = a["L0_ffn_bias"][None, :]
    out["sw13"] = np.stack([a["L0_ffn_sw1"].T, a["L0_ffn_sw3"].T], 1)
    out["sw2"] = a["L0_ffn_sw2"].T
    out["w13"] = np.concatenate([a["L0_ffn_W1"], a["L0_ffn_W3"]], 2).transpose(1, 0, 2)
    out["w2"] = a["L0_ffn_W2"].transpose(1, 0, 2)
    out["w1_qkv"] = np.stack([a[f"L1_attn_W{n}"].T for n in "kqv"], 1)
    out["w_beta"] = a["L1_attn_Wbeta"].T
    out["b1"] = np.stack([a[f"L1_attn_b{n}"] for n in "kqv"] + [np.repeat(a["L1_attn_bbeta"], DH1)], 1)
    out["taps"] = np.stack([a[f"L1_attn_conv_{n}"] for n in "kqv"], 1)
    out["w1_out"] = a["L1_attn_Wout"].T
    out["cols1"] = np.stack([np.tile(a["L1_attn_rms_w"], H1), a["L1_attn_bout"], a["L1_ffn_norm_scale"]], 1)
    out["router"] = a["L1_ffn_w_router"].T
    out["w_up"] = a["L1_ffn_w_up"].transpose(2, 0, 1)
    down = np.zeros((E1, len(HC) * 128, D), np.float32)
    down[:, :HID] = a["L1_ffn_w_down"].transpose(0, 2, 1)
    out["w_down"] = down.reshape(E1, len(HC), 128, D).transpose(2, 0, 1, 3)
    return {k: np.ascontiguousarray(v) for k, v in out.items()}


def build(nc, dram, out):
    f, bf = constants()
    cols, nf = table_columns(f)
    cols_bf, nb = table_columns(bf)
    with ExitStack() as ctx:
        g = Shared()
        g.tab = ctx.enter_context(nc.sbuf_tensor("tables_sb", [128, nf], F32))
        g.tab_bf = ctx.enter_context(nc.sbuf_tensor("tables_bf_sb", [128, nb], BF16))

        def t(name):
            if name in cols:
                return g.tab[:, cols[name][0]:cols[name][1]]
            return g.tab_bf[:, cols_bf[name][0]:cols_bf[name][1]]
        g.t = t
        g.mod = ctx.enter_context(nc.sbuf_tensor("mod", [128, 2, 6, B], F32))
        g.xT = ctx.enter_context(nc.sbuf_tensor("xT", [128, N], F32))
        g.xnT = ctx.enter_context(nc.sbuf_tensor("xnT", [128, N], F32))
        g.slot_token = ctx.enter_context(nc.sbuf_tensor("slot_token", [128, E0], U32))
        g.rows = nc.dram_tensor("rows", (N + CAP, ROW), F32, kind="Internal").ap()
        g.acc = nc.dram_tensor("acc", (N + CAP, D), F32, kind="Internal").ap()
        g.x_kept = nc.dram_tensor("x_kept", (128, N), F32, kind="Internal").ap()
        setup_phase(nc, dram, g)
        load_phase(nc, dram, g)
        attention_phase(nc, dram, g)
        route_phase(nc, dram, g)
        experts_phase(nc, dram, g)
        g.kT, g.vT = g.xT, g.xnT
        g.qT = ctx.enter_context(nc.sbuf_tensor("qT", [128, N], F32))
        rates = ctx.enter_context(ExitStack())
        g.bT = rates.enter_context(nc.sbuf_tensor("bT", [128, N], F32))
        project_phase(nc, dram, g)
        delta_phase(nc, dram, g)
        rates.close()
        g.keptT, g.normT = g.xT, g.qT
        g.gatesT = ctx.enter_context(nc.sbuf_tensor("gatesT", [E1, N], F32))
        mix_phase(nc, dram, g)
        ffn_phase(nc, dram, g, out)


def kernel(**inputs):
    import concourse.bacc as bacc
    from concourse.bass_utils import run_bass_kernel_spmd

    nc = bacc.Bacc("TRN2", target_bir_lowering=False, num_devices=1)
    arrays = {f"in_{name}": a for name, a in launch_arrays(inputs).items()}
    dram = {name[3:]: nc.dram_tensor(name, a.shape, mybir.dt.from_np(a.dtype), kind="ExternalInput").ap()
            for name, a in arrays.items()}
    out = nc.dram_tensor("out", (B, T, D), F32, kind="ExternalOutput").ap()
    build(nc, dram, out)
    return run_bass_kernel_spmd(nc, [arrays], core_ids=[0]).results[0]["out"]
```

```python
from contextlib import ExitStack

import numpy as np

import concourse.bass as bass
from concourse import mybir

F32 = mybir.dt.float32
BF16 = mybir.dt.bfloat16
U32 = mybir.dt.uint32
ALU = mybir.AluOpType
ACT = mybir.ActivationFunctionType
AX = mybir.AxisListType

B, T, D = 32, 256, 128
N = B * T
LN_EPS = 1e-5
RMS_EPS = 1e-6
CH = 512
NCH = N // CH
BPC = CH // T

H0, DH0 = 8, 16
GROUPS, PER = 2, 4
SLOT = 32
KB = T // SLOT
NEG = -1e30
SCALE0 = 1.0 / DH0 ** 0.5
GEO_D = 3
E0, I0, K0, CAP = 32, 64, 4, 2 * 512 * 4 // 32
H1, DH1, CONV = 16, 8, 4
E1, HID, K1 = 8, 352, 2
TILES1 = K1 * N // 128 + E1
HC = [(0, 128), (128, 128), (256, 96)]


def constants():
    p = np.arange(128)
    quad, slot = p // SLOT, p % SLOT
    f = {}
    f["ident"] = np.eye(128)
    f["center"] = np.eye(128) - 1.0 / 128
    f["mean"] = np.full((128, 128), 1.0 / 128)
    half = DH0 // 2
    inv = (1.0 / np.float32(10000.0) ** (np.arange(0, DH0, 2, dtype=np.float32) / np.float32(DH0))).astype(np.float32)
    freqs = np.outer(np.arange(T, dtype=np.float32), inv).astype(np.float32).astype(np.float64)
    cos, sin = np.zeros((128, T)), np.zeros((128, T))
    for i in range(128):
        if slot[i] < DH0:
            cos[i] = np.cos(freqs[:, slot[i] % half])
            sin[i] = np.sin(freqs[:, slot[i] % half]) * (-1 if slot[i] < half else 1)
    f["cos"], f["sin"] = cos, sin
    f["own_head"] = quad[:, None] == np.arange(PER)[None, :]
    f["own_head_scaled"] = SCALE0 * f["own_head"]
    f["mask_own"] = np.where(slot[:, None] < np.arange(SLOT)[None, :], NEG, 0.0)
    h = p // DH1
    f["same_head"] = h[:, None] == h[None, :]
    for d in range(DH1):
        f[f"pick{d}"] = (h[:, None] == h[None, :]) & (p % DH1 == d)[:, None]
    t = np.arange(1, T + 1, dtype=np.float64)
    f["step"] = np.broadcast_to(t, (128, T))
    at = SLOT * np.arange(KB)[None, :] + slot[:, None] + 1.0
    f["inv_weight_t"] = 1.0 / (at * (at + 1) / 2)
    f["before"] = p[:, None] < p[None, :]
    f["ones"] = np.ones((128, 128))
    f["iota"] = np.broadcast_to(np.arange(TILES1, dtype=np.float64), (128, TILES1))
    f["row_no"] = p[:, None]
    f["tile_no"] = np.broadcast_to(np.arange(N // 128, dtype=np.float64), (128, N // 128))
    f["past"] = N + p[:, None]
    tile, choice = np.meshgrid(np.arange(N // 128), np.arange(K1), indexing="ij")
    f["choice_row"] = 128.0 * (tile + choice * (N // 128) + 1.0).reshape(1, -1) + p[:, None]
    f = {k: np.ascontiguousarray(v, dtype=np.float32) for k, v in f.items()}
    b = {}
    b["ident_bf"] = np.eye(128)
    late = slot[:, None] < np.arange(2 * SLOT)[None, :]
    b["mask_max"] = np.where(late, NEG, 0.0)
    b = {k: np.ascontiguousarray(v, dtype=np.float32) for k, v in b.items()}
    return f, b


def table_columns(tables):
    at, out = 0, {}
    for k, v in tables.items():
        out[k] = (at, at + v.shape[1])
        at += v.shape[1]
    return out, at


class Named(dict):

    def __getattr__(self, name):
        return self[name]


class Shared:
    pass


class Scope(ExitStack):

    def __init__(self, nc, name):
        super().__init__()
        self.nc, self.name, self.taken = nc, name, []

    def sb(self, name, shape, dt=F32):
        return self.enter_context(self.nc.sbuf_tensor(f"{self.name}_{name}", shape, dt))

    def ps(self, name, shape=(128, 512), dt=F32):
        return self.enter_context(self.nc.psum_tensor(f"{self.name}_{name}", list(shape), dt))

    def sems(self, names, tag=""):
        made = {n: self.nc.alloc_semaphore(f"{self.name}_{n}{tag}") for n in names.split()}
        self.taken += made.values()
        return Named(made)

    def __exit__(self, *exc):
        super().__exit__(*exc)
        if exc[0] is None:
            self.nc.clear_and_free_semaphores(self.taken)
            self.nc.all_engine_barrier()

    def block(self):
        return self.enter_context(self.nc.Block())


def setup_phase(nc, dram, g):
    with Scope(nc, "setup") as s:
        c_sb = s.sb("c", [128, 2, B])
        silu = s.sb("silu", [128, 2, B])
        wmod = s.sb("wmod", [128, 2, 6 * 128])
        absv = s.sb("absv", [128, 2, 2, B])
        sign = s.sb("sign", [128, 2, 2, B])
        tab_f = s.sb("tab_f", g.tab_bf.shape)
        ps = s.ps("mod", (128, 2, 6, B))
        k = s.sems("tables_in tab_bf weights_in silu_done mod_done mod_read raw_gates abs_done sign_done sign_scaled")
        block = s.block()

        @block.sync
        def _(sp):
            sp.dma_start(c_sb[:, 0, :], dram["c0"]).then_inc(k.weights_in, 16)
            sp.dma_start(c_sb[:, 1, :], dram["c1"]).then_inc(k.weights_in, 16)
            sp.dma_start(wmod[:, 0, :], dram["wmod0"]).then_inc(k.weights_in, 16)
            sp.dma_start(wmod[:, 1, :], dram["wmod1"]).then_inc(k.weights_in, 16)
            sp.dma_start(g.tab[:, :], dram["tables"]).then_inc(k.tables_in, 16)
            sp.dma_start(tab_f[:, :], dram["tables_bf"]).then_inc(k.tables_in, 16)
            sp.wait_ge(k.tables_in, 32)

        @block.scalar
        def _(act):
            act.wait_ge(k.weights_in, 64)
            nc.scalar.activation(silu[:, :, :], c_sb[:, :, :], ACT.Silu).then_inc(k.silu_done, 1)

        @block.tensor
        def _(pe):
            pe.wait_ge(k.silu_done, 1)
            for layer in range(2):
                for j in range(6):
                    last = nc.tensor.matmul(ps[:, layer, j, :], wmod[:, layer, 128 * j:128 * j + 128],
                                            silu[:, layer, :], start=True, stop=True)
            last.then_inc(k.mod_done, 1)

        @block.vector
        def _(dve):
            dve.wait_ge(k.tables_in, 32)
            nc.vector.tensor_copy(g.tab_bf[:, :], tab_f[:, :]).then_inc(k.tab_bf, 1)
            dve.wait_ge(k.mod_done, 1)
            nc.vector.tensor_copy(g.mod[:, :, :, :], ps[:, :, :, :]).then_inc(k.mod_read, 1)
            dve.wait_ge(k.mod_read, 1)
            for layer in range(2):
                for half in range(2):
                    nc.vector.tensor_scalar(g.mod[:, layer, 3 * half + 1, :], g.mod[:, layer, 3 * half + 1, :],
                                            1.0, None, ALU.add)
                    gate = g.mod[:, layer, 3 * half + 2, :]
                    nc.vector.scalar_tensor_tensor(absv[:, layer, half, :], gate, -1.0, gate, ALU.mult, ALU.max)\
                        .then_inc(k.abs_done, 1)
                    nc.vector.tensor_scalar(sign[:, layer, half, :], gate, 0.0, 2.0, ALU.is_ge, ALU.mult)\
                        .then_inc(k.sign_done, 1)
            dve.wait_ge(k.sign_done, 4)
            nc.vector.tensor_scalar(sign[:, :, :, :], sign[:, :, :, :], -1.0, None, ALU.add).then_inc(k.sign_scaled, 1)
            dve.wait_ge(k.sign_scaled, 1)
            dve.wait_ge(k.abs_done, 4)
            for layer in range(2):
                for half in range(2):
                    nc.vector.scalar_tensor_tensor(g.mod[:, layer, 3 * half + 2, :], absv[:, layer, half, :], 0.25,
                                                   sign[:, layer, half, :], ALU.max, ALU.mult)


RC = CH // SLOT


class Rstd:
    STEPS = 3
    MAGIC = float(0x5F3759DF)

    def __init__(self, s, name, count=RC, parts=True, room=None):
        if room is not None:
            self.turned, self.out = room[0].rearrange("p (n i) -> p n i", i=SLOT), room[1]
        elif parts:
            self.turned = s.sb(f"{name}_turned", [128, count, SLOT])
            self.out = s.sb(f"{name}_out", [128, count * SLOT])
        self.v = s.sb(f"{name}_v", [128, count])
        self.y = s.sb(f"{name}_y", [128, count])
        self.t = s.sb(f"{name}_t", [128, count])
        self.count = count
        s.sems(f"{name}_turn {name}_v {name}_guess {name}_newton {name}_out")
        self.turn_done, self.v_done, self.guess_done, self.newton_done, self.out_done = s.taken[-5:]

    def run(self, nc, dve, psum, eps, it):
        run_roots(nc, dve, [self], [psum], eps, it)

    def root(self, nc, dve, it):
        newton_roots(nc, dve, [self], it)


def run_roots(nc, dve, group, psums, eps, it, made=None):
    for n, (r, psum) in enumerate(zip(group, psums)):
        if made:
            dve.wait_ge(made[n], it + 1)
        nc.vector.transpose(r.turned[:, :, :].rearrange("p n i -> p (n i)"), psum).then_inc(r.turn_done, 1)
    for r in group:
        dve.wait_ge(r.turn_done, it + 1)
        nc.vector.tensor_scalar(r.v[:, :], r.turned[:, :, 0], eps, None, ALU.add).then_inc(r.v_done, 1)
    for r in group:
        dve.wait_ge(r.v_done, it + 1)
    newton_roots(nc, dve, group, it)
    for r in group:
        nc.vector.transpose(r.out[:, :].rearrange("p (n i) -> p n i", i=SLOT),
                            r.y[:, :, None].to_broadcast([128, r.count, SLOT])).then_inc(r.out_done, 1)
    for r in group:
        dve.wait_ge(r.out_done, it + 1)


def newton_roots(nc, dve, group, it):
    for r in group:
        nc.vector.tensor_scalar(r.y[:, :].bitcast(mybir.dt.int32), r.v[:, :].bitcast(mybir.dt.int32),
                                -0.5, Rstd.MAGIC, ALU.mult, ALU.add).then_inc(r.guess_done, 1)
    for n in range(Rstd.STEPS):
        before = 3 * Rstd.STEPS * it + 3 * n
        for r in group:
            if n == 0:
                dve.wait_ge(r.guess_done, it + 1)
            else:
                dve.wait_ge(r.newton_done, before)
            nc.vector.scalar_tensor_tensor(r.t[:, :], r.y[:, :], -0.5, r.y[:, :], ALU.mult, ALU.mult)\
                .then_inc(r.newton_done, 1)
        for r in group:
            dve.wait_ge(r.newton_done, before + 1)
            nc.vector.tensor_tensor(r.t[:, :], r.t[:, :], r.v[:, :], ALU.mult).then_inc(r.newton_done, 1)
        for r in group:
            dve.wait_ge(r.newton_done, before + 2)
            nc.vector.scalar_tensor_tensor(r.y[:, :], r.t[:, :], 1.5, r.y[:, :], ALU.add, ALU.mult)\
                .then_inc(r.newton_done, 1)
    for r in group:
        dve.wait_ge(r.newton_done, 3 * Rstd.STEPS * (it + 1))


PAR = 2


def load_phase(nc, dram, g):
    with Scope(nc, "load") as s:
        rows = s.sb("rows", [128, PAR, CH // 128, D])
        sq = s.sb("sq", [128, PAR, 2, CH])
        unit = s.sb("unit", [128, PAR, CH])
        h = s.sb("h", [128, PAR, CH])
        unit2 = s.sb("unit2", [128, PAR, CH])
        ln = s.sb("ln", [128, 2])
        rstd = [[Rstd(s, f"rstd{i}{par}") for i in range(2)] for par in range(PAR)]
        mid = [[s.ps(f"mid{i}{par}") for i in range(2)] for par in range(PAR)]
        var = [[s.ps(f"var{i}{par}") for i in range(2)] for par in range(PAR)]
        turned = [var[par][0] for par in range(PAR)]
        ln_in = s.sems("ln_in").ln_in
        k = [s.sems("rows_in turned x_copied centered0 centered1 squared0 squared1 var0 var1"
                    " unit modulated passed unit2 xn", par) for par in range(PAR)]
        block = s.block()
        x_rows = dram["x"].rearrange("b t c -> (b t) c")
        cols = lambda i, par: bass.ds(i * (PAR * CH) + par * CH, CH)

        @block.sync
        def _(sp):
            sp.dma_start(ln[:, :], dram["ln"]).then_inc(ln_in, 16)
            with sp.Fori(0, NCH // PAR) as i:
                for par in range(PAR):
                    sp.wait_ge(k[par].turned, i)
                    sp.dma_start(rows[:, par], x_rows[cols(i, par), :].rearrange("(r p) c -> p r c", p=128))\
                        .then_inc(k[par].rows_in, 16)

        @block.tensor
        def _(pe):
            def turn(i):
                for par in range(PAR):
                    pe.wait_ge(k[par].rows_in, 16 * (i + 1))
                    pe.wait_ge(k[par].unit, i)
                    for r in range(CH // 128):
                        last = nc.tensor.transpose(turned[par][:, 128 * r:128 * r + 128], rows[:, par, r, :], g.t("ident"))
                    last.then_inc(k[par].turned, 1)

            def center0(i):
                for par in range(PAR):
                    pe.wait_ge(k[par].x_copied, i + 1)
                    nc.tensor.matmul(mid[par][0][:, :], g.t("center"), g.xT[:, cols(i, par)], start=True, stop=True)\
                        .then_inc(k[par].centered0, 1)

            def var0(i):
                for par in range(PAR):
                    pe.wait_ge(k[par].squared0, i + 1)
                    nc.tensor.matmul(var[par][0][:, :], g.t("mean"), sq[:, par, 0, :], start=True, stop=True)\
                        .then_inc(k[par].var0, 1)

            def center1(i):
                for par in range(PAR):
                    pe.wait_ge(k[par].modulated, i + 1)
                    pe.wait_ge(k[par].unit2, i)
                    nc.tensor.matmul(mid[par][1][:, :], g.t("center"), h[:, par, :], start=True, stop=True)\
                        .then_inc(k[par].centered1, 1)

            def var1(i):
                for par in range(PAR):
                    pe.wait_ge(k[par].squared1, i + 1)
                    nc.tensor.matmul(var[par][1][:, :], g.t("mean"), sq[:, par, 1, :], start=True, stop=True)\
                        .then_inc(k[par].var1, 1)
            turn(0)
            center0(0)
            var0(0)
            with pe.Fori(0, NCH // PAR - 1) as i:
                turn(i + 1)
                center1(i)
                center0(i + 1)
                var1(i)
                var0(i + 1)
            center1(NCH // PAR - 1)
            var1(NCH // PAR - 1)

        @block.scalar
        def _(act):
            act.wait_ge(ln_in, 16)

            def copy_x(i):
                for par in range(PAR):
                    act.wait_ge(k[par].turned, i + 1)
                    nc.scalar.activation(g.xT[:, cols(i, par)], turned[par][:, :], ACT.Copy).then_inc(k[par].x_copied, 1)

            def square0(i):
                for par in range(PAR):
                    act.wait_ge(k[par].centered0, i + 1)
                    nc.scalar.activation(sq[:, par, 0, :], mid[par][0][:, :], ACT.Square).then_inc(k[par].squared0, 1)

            def modulate(i):
                for par in range(PAR):
                    act.wait_ge(k[par].unit, i + 1)
                    act.wait_ge(k[par].centered1, i)
                    act.wait_ge(k[par].passed, i)
                    for j in range(BPC):
                        b = i * (PAR * BPC) + par * BPC + j
                        last = nc.scalar.activation(h[:, par, j * T:(j + 1) * T], unit[:, par, j * T:(j + 1) * T],
                                                    ACT.Identity, scale=g.mod[:, 0, 1, bass.ds(b, 1)],
                                                    bias=g.mod[:, 0, 0, bass.ds(b, 1)])
                    last.then_inc(k[par].modulated, 1)

            def square1(i):
                for par in range(PAR):
                    act.wait_ge(k[par].centered1, i + 1)
                    nc.scalar.activation(sq[:, par, 1, :], mid[par][1][:, :], ACT.Square).then_inc(k[par].squared1, 1)

            def affine(i):
                for par in range(PAR):
                    act.wait_ge(k[par].unit2, i + 1)
                    nc.scalar.activation(g.xnT[:, cols(i, par)], unit2[:, par, :], ACT.Identity,
                                         scale=ln[:, 0:1], bias=ln[:, 1:2]).then_inc(k[par].xn, 1)
            copy_x(0)
            square0(0)
            modulate(0)
            with act.Fori(0, NCH // PAR - 1) as i:
                copy_x(i + 1)
                square1(i)
                square0(i + 1)
                affine(i)
                modulate(i + 1)
            square1(NCH // PAR - 1)
            affine(NCH // PAR - 1)

        @block.vector
        def _(dve):
            def norm0(i):
                run_roots(nc, dve, [rstd[par][0] for par in range(PAR)], [var[par][0][:, :] for par in range(PAR)], LN_EPS, i,
                          [k[par].var0 for par in range(PAR)])
                for par in range(PAR):
                    dve.wait_ge(k[par].modulated, i)
                    nc.vector.tensor_tensor(unit[:, par, :], mid[par][0][:, :], rstd[par][0].out[:, :], ALU.mult)\
                        .then_inc(k[par].unit, 1)

            def norm1(i):
                run_roots(nc, dve, [rstd[par][1] for par in range(PAR)], [var[par][1][:, :] for par in range(PAR)], LN_EPS, i,
                          [k[par].var1 for par in range(PAR)])
                for par in range(PAR):
                    dve.wait_ge(k[par].xn, i)
                    nc.vector.tensor_tensor(unit2[:, par, :], mid[par][1][:, :], rstd[par][1].out[:, :], ALU.mult)\
                        .then_inc(k[par].unit2, 1)
            def pass_on(i):
                for par in range(PAR):
                    dve.wait_ge(k[par].centered0, i + 1)
                    dve.wait_ge(k[par].modulated, i + 1)
                    for j in range(BPC):
                        b = i * (PAR * BPC) + par * BPC + j
                        x = g.xT[:, bass.ds(b * T, T)]
                        last = nc.vector.scalar_tensor_tensor(x, h[:, par, j * T:(j + 1) * T], g.mod[:, 0, 2, bass.ds(b, 1)], x,
                                                              ALU.mult, ALU.add)
                    last.then_inc(k[par].passed, 1)
            norm0(0)
            with dve.Fori(0, NCH // PAR - 1) as i:
                norm1(i)
                pass_on(i)
                norm0(i + 1)
            pass_on(NCH // PAR - 1)
            norm1(NCH // PAR - 1)


KEYS_AT = {6: (0, 0, 256), 7: (0, 256, 256), 4: (1, 0, 192), 5: (1, 192, 192), 0: (1, 384, 64), 1: (1, 448, 64),
           2: (2, 0, 128), 3: (2, 128, 128)}
BANKS = 3
ROW_OFF = [SLOT * n * (n + 1) // 2 for n in range(KB + 1)]
EARLY_OFF = [SLOT * n * (n - 1) // 2 for n in range(KB + 1)]


def attention_phase(nc, dram, g):
    with Scope(nc, "attn") as s:
        w = s.sb("w", [128, 5, GROUPS, 128])
        wo = s.sb("wo", [128, GROUPS, 128])
        dirs = s.sb("dirs", [128, 2, GROUPS, 128])
        hs = s.sb("hs", [128, GROUPS])
        share = s.sb("share", [128, 2, GROUPS])
        tq = s.sb("tq", [128, 2, GROUPS, T])
        tk = s.sb("tk", [128, 2, GROUPS, T])
        q = s.sb("q", [128, 2, GROUPS, T])
        kk = s.sb("k", [128, 2, GROUPS, T])
        q_diag = s.sb("q_diag", [128, GROUPS, KB, PER, SLOT])
        v_rows = s.sb("v_rows", [128, GROUPS * KB, SLOT])
        v_diag = s.sb("v_diag", [128, GROUPS * KB, PER, SLOT])
        geo_rows = s.sb("geo_rows", [128, 2, T])
        less_qp = s.sb("less_qp", [128, T])
        run_max = s.sb("run_max", [128, T])
        run_min = s.sb("run_min", [128, T])
        geo_cols = s.sb("geo_cols", [128, 2, 2, KB, SLOT])
        kp_wide = s.sb("kp_wide", [128, 2, GROUPS, KB, SLOT])
        geo_own = s.sb("geo_own", [128, 2, GROUPS, KB, SLOT])
        mx = s.sb("mx", [128, GROUPS, KB])
        p_att = s.sb("p_att", [128, GROUPS, ROW_OFF[KB]])
        p_geo = s.sb("p_geo", [128, GROUPS, EARLY_OFF[KB]])
        p_own = s.sb("p_own", [128, GROUPS, KB, SLOT])
        PITCH = T + SLOT
        turned = s.sb("turned", [128, 2, GROUPS, KB * PITCH])
        oT = s.sb("oT", [128, 2, GROUPS * KB, SLOT])
        coef = s.sb("coef", [128, 2, GROUPS * KB])
        ow = s.sb("ow", [128, 2, GROUPS * KB, DH0])
        aoT = s.sb("aoT", [128, GROUPS * KB, SLOT])
        ao = s.sb("ao", [128, GROUPS, T])
        score = [s.ps(f"score{i}") for i in range(BANKS)]
        F = [s.ps(f"front{i}") for i in range(3)]
        O = [s.ps(f"out{i}") for i in range(2)]
        k = s.sems("w_in cleared ones share_ready q_made qr_made k_made kr_made v_made q_row k_row kp_made"
                   " tq1 tq2 tk1 tk2 q_ready k_ready v_turned v_diag rows_copied less_qp kp_copied ran_max ran_min"
                   " ga_made gb_made less_max geo_cols geo_own turned_g turned_a recip coef weighted combined summed"
                   " out_made x_done")
        by_bank = [s.sems("scored max_read att_exp", n) for n in range(BANKS)]
        by_group = [s.sems("q_diag geo_exp att_turned geo_turned att_weighed geo_weighed", gr) for gr in range(GROUPS)]
        block = s.block()
        tokens = lambda b: bass.ds(b * T, T)
        halves = lambda ap: ap[:, :].rearrange("p (g t) -> p g t", g=GROUPS)

        def steps(eng, front, step):
            front(0, 0)
            step(0, 0, front)
            with eng.Fori(0, B // 2 - 1) as i:
                step(2 * i + 1, 1, front)
                step(2 * i + 2, 0, front)
            step(B - 1, 1, None)

        @block.sync
        def _(sp):
            sp.dma_start(w[:, :, :, :], dram["w_attn"]).then_inc(k.w_in, 16)
            sp.dma_start(wo[:, :, :], dram["wo"]).then_inc(k.w_in, 16)
            sp.dma_start(dirs[:, :, :, :], dram["dirs"]).then_inc(k.w_in, 16)
            sp.dma_start(hs[:, :], dram["hs"]).then_inc(k.w_in, 16)

        @block.tensor
        def _(pe):
            pe.wait_ge(k.w_in, 64)
            pe.wait_ge(k.cleared, 3)
            pe.wait_ge(k.ones, PER)

            def project(out, n, b, sem):
                for gr in range(GROUPS):
                    last = nc.tensor.matmul(out[:, gr * T:(gr + 1) * T], w[:, n, gr, :], g.xnT[:, tokens(b)],
                                            start=True, stop=True)
                last.then_inc(sem, 1)

            def front_qk(b):
                pe.wait_ge(k.kp_copied, b)
                project(F[0], 0, b, k.q_made)
                pe.wait_ge(k.v_turned, b)
                project(F[1], 1, b, k.qr_made)
                pe.wait_ge(k.less_qp, b)
                if not isinstance(b, int) or b > 0:
                    pe.wait_ge(k.x_done, b - 1)
                project(F[2], 2, b, k.k_made)

            def front_v(b):
                pe.wait_ge(k.tq1, b + 1)
                project(F[0], 3, b, k.kr_made)
                pe.wait_ge(k.tq2, b + 1)
                project(F[1], 4, b, k.v_made)

            def front_geo(b, par):
                pe.wait_ge(k.tk1, b + 1)
                pe.wait_ge(k.q_ready, b + 1)
                for gr in range(GROUPS):
                    last = nc.tensor.matmul(F[2][:, 0:T], dirs[:, 0, gr, :], q[:, par, gr, :], start=gr == 0, stop=gr == 1)
                last.then_inc(k.q_row, 1)
                pe.wait_ge(k.k_ready, b + 1)
                for gr in range(GROUPS):
                    last = nc.tensor.matmul(F[2][:, T:2 * T], dirs[:, 0, gr, :], kk[:, par, gr, :],
                                            start=gr == 0, stop=gr == 1)
                last.then_inc(k.k_row, 1)
                pe.wait_ge(k.tk2, b + 1)
                for gr in range(GROUPS):
                    last = nc.tensor.matmul(F[0][:, gr * T:(gr + 1) * T], dirs[:, 1, gr, :], kk[:, par, gr, :],
                                            start=True, stop=True)
                last.then_inc(k.kp_made, 1)

            def scores(b, par, gr):
                pe.wait_ge(by_group[gr].q_diag, b + 1)
                pe.wait_ge(k.k_ready, b + 1)
                for bank in range(BANKS):
                    pe.wait_ge(by_bank[bank].att_exp, GROUPS * b + gr)
                    for n, (at, c, size) in KEYS_AT.items():
                        if at == bank:
                            masked = SLOT if n % 2 else 2 * SLOT
                            nc.tensor.matmul(score[at][:, c:c + size], q_diag[:, gr, n], kk[:, par, gr, 0:size],
                                             start=True, stop=False)
                            last = nc.tensor.matmul(score[at][:, c + size - masked:c + size], g.t("ident_bf"),
                                                    g.t("mask_max")[:, 0:masked], start=False, stop=True)
                    last.then_inc(by_bank[bank].scored, 1)

            def weigh(b, kind, gr):
                pe.wait_ge(k.v_diag, b + 1)
                pe.wait_ge((k.turned_a, k.turned_g)[kind], b)
                pe.wait_ge((by_group[gr].att_turned, by_group[gr].geo_turned)[kind], b + 1)
                for n in range(KB):
                    last = nc.tensor.matmul(O[kind][:, gr * T + SLOT * n:(gr + 1) * T], v_diag[:, gr * KB + n],
                                            turned[:, kind, gr, n * T + SLOT * n:(n + 1) * T],
                                            start=n == 0, stop=n == KB - 1)
                last.then_inc((by_group[gr].att_weighed, by_group[gr].geo_weighed)[kind], 1)

            def front(b, par):
                front_qk(b)
                front_v(b)
                front_geo(b, par)

            def mix(b):
                pe.wait_ge(k.less_qp, b + 2 if not isinstance(b, int) or b < B - 1 else B)
                pe.wait_ge(k.summed, b + 1)
                for gr in range(GROUPS):
                    last = nc.tensor.matmul(F[2][:, 0:T], wo[:, gr, :], ao[:, gr, :], start=gr == 0, stop=gr == 1)
                last.then_inc(k.out_made, 1)

            def step(b, par, ahead):
                scores(b, par, 0)
                if not isinstance(b, int) or b > 0:
                    mix(b - 1)
                if ahead:
                    front_qk(b + 1)
                scores(b, par, 1)
                if ahead:
                    front_v(b + 1)
                weigh(b, 0, 0)
                weigh(b, 1, 0)
                if ahead:
                    front_geo(b + 1, 1 - par)
                weigh(b, 0, 1)
                weigh(b, 1, 1)
                if not ahead:
                    mix(b)
            steps(pe, front, step)

        @block.scalar
        def _(act):
            act.wait_ge(k.cleared, 3)

            def geo_exps(b, par, gr):
                act.wait_ge(k.geo_cols, b + 1)
                act.wait_ge(k.kp_copied, b + 1)
                act.wait_ge(by_group[gr].geo_turned, b)
                for n in range(1, KB):
                    nc.scalar.activation(p_geo[:, gr, EARLY_OFF[n]:EARLY_OFF[n + 1]],
                                         kp_wide[:, par, gr, 0:n, :].rearrange("p n i -> p (n i)"), ACT.Exp,
                                         scale=geo_cols[:, par, 0, n, gr:gr + 1], bias=geo_cols[:, par, 1, n, gr:gr + 1])
                act.wait_ge(k.geo_own, 3 * (b + 1))
                nc.scalar.activation(p_own[:, gr], geo_own[:, par, gr], ACT.Exp).then_inc(by_group[gr].geo_exp, 1)

            def att_exps(b, gr):
                act.wait_ge(by_group[gr].att_turned, b)
                for bank in range(BANKS):
                    act.wait_ge(by_bank[bank].max_read, GROUPS * b + gr + 1)
                    for n, (at, c, size) in KEYS_AT.items():
                        if at == bank:
                            last = nc.scalar.activation(p_att[:, gr, ROW_OFF[n]:ROW_OFF[n + 1]],
                                                        score[at][:, c:c + SLOT * (n + 1)], ACT.Exp, bias=mx[:, gr, n:n + 1])
                    last.then_inc(by_bank[bank].att_exp, 1)

            def front(b, par):
                act.wait_ge(k.q_row, b + 1)
                act.wait_ge(k.k_row, b + 1)
                act.wait_ge(k.geo_cols, b)
                nc.scalar.activation(geo_rows[:, :, :].rearrange("p s t -> p (s t)"), F[2][:, :], ACT.Copy)\
                    .then_inc(k.rows_copied, 1)
                act.wait_ge(k.ga_made, b)
                act.wait_ge(k.gb_made, b)
                nc.scalar.activation(less_qp[:, :], F[2][:, 0:T], ACT.Copy, scale=-1.0).then_inc(k.less_qp, 1)
                act.wait_ge(k.kp_made, b + 1)
                nc.scalar.activation(kp_wide[:, par].rearrange("p g n i -> p (g n i)"), F[0][:, :], ACT.Copy)\
                    .then_inc(k.kp_copied, 1)

            def step(b, par, ahead):
                att_exps(b, 0)
                geo_exps(b, par, 0)
                att_exps(b, 1)
                geo_exps(b, par, 1)
                if ahead:
                    ahead(b + 1, 1 - par)
            steps(act, front, step)

        @block.vector
        def _(dve):
            nc.vector.memset(v_diag[:, :, :, :], 0.0).then_inc(k.cleared, 1)
            nc.vector.memset(aoT[:, :, :], 0.0).then_inc(k.cleared, 1)
            nc.vector.memset(mx[:, :, :], 0.0).then_inc(k.cleared, 1)
            dve.wait_ge(k.cleared, 3)
            for h in range(PER):
                nc.vector.memset(v_diag[SLOT * h:SLOT * h + SLOT, :, h, DH0:DH0 + 1], 1.0).then_inc(k.ones, 1)
            dve.wait_ge(k.w_in, 64)
            nc.vector.tensor_copy(share[:, 1, :], hs[:, :]).then_inc(k.share_ready, 1)
            nc.vector.tensor_scalar(share[:, 0, :], hs[:, :], -1.0, 1.0, ALU.mult, ALU.add).then_inc(k.share_ready, 1)
            dve.wait_ge(k.share_ready, 2)

            def both(ap):
                return ap[:, None, :].to_broadcast([128, GROUPS, T])

            def front_q(b):
                dve.wait_ge(k.q_ready, b)
                dve.wait_ge(k.q_made, b + 1)
                nc.vector.tensor_tensor(tq[:, 0], halves(F[0]), both(g.t("cos")), ALU.mult).then_inc(k.tq1, 1)
                dve.wait_ge(k.qr_made, b + 1)
                nc.vector.tensor_tensor(tq[:, 1], halves(F[1]), both(g.t("sin")), ALU.mult).then_inc(k.tq2, 1)

            def front_k(b):
                dve.wait_ge(k.k_ready, b)
                dve.wait_ge(k.k_made, b + 1)
                nc.vector.tensor_tensor(tk[:, 0], halves(F[2]), both(g.t("cos")), ALU.mult).then_inc(k.tk1, 1)
                dve.wait_ge(k.kr_made, b + 1)
                nc.vector.tensor_tensor(tk[:, 1], halves(F[0]), both(g.t("sin")), ALU.mult).then_inc(k.tk2, 1)

            def front_v(b):
                dve.wait_ge(k.v_made, b + 1)
                dve.wait_ge(k.v_diag, b)
                nc.vector.transpose(v_rows[:, :, :].rearrange("p n d -> p (n d)"), F[1][:, :]).then_inc(k.v_turned, 1)

            def front_extremes(b):
                dve.wait_ge(k.rows_copied, b + 1)
                dve.wait_ge(k.less_max, b)
                kp = geo_rows[:, 1, :]
                nc.vector.tensor_tensor_scan(run_max[:, :], kp, kp, -3e38, ALU.max, ALU.max).then_inc(k.ran_max, 1)
                nc.vector.tensor_tensor_scan(run_min[:, :], kp, kp, 3e38, ALU.min, ALU.min).then_inc(k.ran_min, 1)

            def front_cols(b, par):
                dve.wait_ge(k.ran_min, b + 1)
                dve.wait_ge(k.ga_made, b + 1)
                dve.wait_ge(k.gb_made, b + 1)
                nc.vector.tensor_tensor(geo_rows[:, 1, :], run_max[:, :], run_min[:, :], ALU.min).then_inc(k.less_max, 1)
                if not isinstance(b, int) or b > 1:
                    dve.wait_ge(by_group[1].geo_exp, b - 1)
                dve.wait_ge(k.less_max, b + 1)
                nc.vector.transpose(geo_cols[:, par].rearrange("p s n i -> p (s n i)"),
                                    geo_rows[:, :, :].rearrange("p s t -> p (s t)")).then_inc(k.geo_cols, 1)

            def read_max(b, gr):
                for bank in range(BANKS):
                    dve.wait_ge(by_bank[bank].scored, GROUPS * b + gr + 1)
                    for at, c, size, n in ((0, 0, 256, 6), (1, 0, 192, 4), (1, 384, 64, 0), (2, 0, 128, 2)):
                        if at == bank:
                            last = nc.vector.tensor_reduce(mx[:, gr, n:n + 2], score[at][:, c:c + 2 * size]
                                                           .rearrange("p (n j) -> p n j", n=2), AX.X, ALU.max, negate=True)
                    last.then_inc(by_bank[bank].max_read, 1)

            def by_key(kind, gr):
                return turned[:, kind, gr, 0:KB * T].rearrange("p (j q) -> p j q", q=T)

            def turn_att(b, gr):
                for bank in range(BANKS):
                    dve.wait_ge(by_bank[bank].att_exp, GROUPS * b + gr + 1)
                dve.wait_ge(by_group[gr].att_weighed, b)
                for n in range(KB):
                    last = nc.vector.transpose(by_key(0, gr)[:, 0:n + 1, SLOT * n:SLOT * n + SLOT],
                                               p_att[:, gr, ROW_OFF[n]:ROW_OFF[n + 1]].rearrange("p (j i) -> p j i", i=SLOT))
                last.then_inc(by_group[gr].att_turned, 1)

            def turn_geo(b, gr):
                dve.wait_ge(by_group[gr].geo_exp, b + 1)
                dve.wait_ge(by_group[gr].geo_weighed, b)
                for n in range(1, KB):
                    nc.vector.transpose(by_key(1, gr)[:, 0:n, SLOT * n:SLOT * n + SLOT],
                                        p_geo[:, gr, EARLY_OFF[n]:EARLY_OFF[n + 1]].rearrange("p (j i) -> p j i", i=SLOT))
                nc.vector.transpose(turned[:, 1, gr, :].rearrange("p (n i) -> p n i", i=PITCH)[:, :, 0:SLOT], p_own[:, gr])\
                    .then_inc(by_group[gr].geo_turned, 1)

            def outputs(b):
                for gr in range(GROUPS):
                    dve.wait_ge(by_group[gr].att_weighed, b + 1)
                nc.vector.transpose(oT[:, 0].rearrange("p n i -> p (n i)"), O[0][:, :]).then_inc(k.turned_a, 1)
                for gr in range(GROUPS):
                    dve.wait_ge(by_group[gr].geo_weighed, b + 1)
                nc.vector.transpose(oT[:, 1].rearrange("p n i -> p (n i)"), O[1][:, :]).then_inc(k.turned_g, 1)
                dve.wait_ge(k.turned_g, b + 1)
                dve.wait_ge(k.turned_a, b + 1)
                nc.vector.reciprocal(coef[:, :, :], oT[:, :, :, DH0]).then_inc(k.recip, 1)
                dve.wait_ge(k.recip, b + 1)
                grouped = coef[:, :, :].rearrange("p s (g n) -> p (s g) n", g=GROUPS)
                nc.vector.tensor_tensor(grouped, grouped, share[:, :, :].rearrange("p s g -> p (s g)")[:, :, None]
                                        .to_broadcast([128, 2 * GROUPS, KB]), ALU.mult).then_inc(k.coef, 1)
                dve.wait_ge(k.coef, b + 1)
                nc.vector.tensor_tensor(ow[:, :, :, :].rearrange("p s n d -> p (s n) d"),
                                        oT[:, :, :, 0:DH0].rearrange("p s n d -> p (s n) d"),
                                        coef[:, :, :].rearrange("p s n -> p (s n)")[:, :, None]
                                        .to_broadcast([128, 2 * GROUPS * KB, DH0]), ALU.mult).then_inc(k.weighted, 1)
                dve.wait_ge(k.weighted, b + 1)
                nc.vector.tensor_tensor(aoT[:, :, 0:DH0], ow[:, 0], ow[:, 1], ALU.add).then_inc(k.combined, 1)
                dve.wait_ge(k.combined, b + 1)
                nc.vector.transpose(ao[:, :, :].rearrange("p g t -> p (g t)"), aoT[:, :, :].rearrange("p n i -> p (n i)"))\
                    .then_inc(k.summed, 1)

            def add(b):
                dve.wait_ge(k.out_made, b + 1)
                x = g.xT[:, tokens(b)]
                nc.vector.scalar_tensor_tensor(x, F[2][:, 0:T], g.mod[:, 0, 2, bass.ds(b, 1)], x, ALU.mult, ALU.add)\
                    .then_inc(k.x_done, 1)

            def front(b, par):
                front_q(b)
                front_k(b)
                front_v(b)
                front_extremes(b)
                front_cols(b, par)

            def step(b, par, ahead):
                read_max(b, 0)
                if not isinstance(b, int) or b > 0:
                    add(b - 1)
                if ahead:
                    front_q(b + 1)
                turn_att(b, 0)
                read_max(b, 1)
                if ahead:
                    front_k(b + 1)
                turn_geo(b, 0)
                if ahead:
                    front_v(b + 1)
                turn_att(b, 1)
                if ahead:
                    front_extremes(b + 1)
                turn_geo(b, 1)
                if ahead:
                    front_cols(b + 1, 1 - par)
                outputs(b)
                if not ahead:
                    add(b)
            steps(dve, front, step)

        @block.gpsimd
        def _(pool):
            def diagonal(out, rows, mask, count, size):
                return nc.gpsimd.tensor_tensor(out, rows[:, :, None, :].to_broadcast([128, count, PER, size]),
                                               mask[:, None, :, None].to_broadcast([128, count, PER, size]), ALU.mult)

            def front(b, par):
                later = not isinstance(b, int) or b > 0
                pool.wait_ge(k.tq1, b + 1)
                pool.wait_ge(k.tq2, b + 1)
                if later:
                    pool.wait_ge(k.q_row, b - 1)
                    pool.wait_ge(by_group[1].q_diag, b - 1)
                nc.gpsimd.tensor_tensor(q[:, par], tq[:, 0], tq[:, 1], ALU.add).then_inc(k.q_ready, 1)
                pool.wait_ge(k.tk1, b + 1)
                pool.wait_ge(k.tk2, b + 1)
                if later:
                    for bank in range(BANKS):
                        pool.wait_ge(by_bank[bank].scored, GROUPS * (b - 1))
                    pool.wait_ge(k.kp_made, b - 1)
                nc.gpsimd.tensor_tensor(kk[:, par], tk[:, 0], tk[:, 1], ALU.add).then_inc(k.k_ready, 1)
                for gr in range(GROUPS):
                    pool.wait_ge(k.q_ready, b + 1)
                    if later:
                        for bank in range(BANKS):
                            pool.wait_ge(by_bank[bank].scored, GROUPS * b + gr - 1)
                    diagonal(q_diag[:, gr], q[:, par, gr].rearrange("p (n i) -> p n i", i=SLOT), g.t("own_head_scaled"),
                             KB, SLOT).then_inc(by_group[gr].q_diag, 1)
                pool.wait_ge(k.less_qp, b + 1)
                pool.wait_ge(k.ran_max, b + 1)
                nc.gpsimd.tensor_tensor(run_max[:, :], run_max[:, :], less_qp[:, :], ALU.mult).then_inc(k.ga_made, 1)
                pool.wait_ge(k.ran_min, b + 1)
                nc.gpsimd.tensor_tensor(run_min[:, :], run_min[:, :], less_qp[:, :], ALU.mult).then_inc(k.gb_made, 1)
                shape = [128, GROUPS, KB, SLOT]
                by_query = [geo_cols[:, par, n, :, 0:GROUPS].rearrange("p n g -> p g n")[:, :, :, None].to_broadcast(shape)
                            for n in range(2)]
                pool.wait_ge(k.geo_cols, b + 1)
                pool.wait_ge(k.kp_copied, b + 1)
                nc.gpsimd.tensor_tensor(geo_own[:, par], kp_wide[:, par], by_query[0], ALU.mult).then_inc(k.geo_own, 1)
                pool.wait_ge(k.geo_own, 3 * b + 1)
                nc.gpsimd.tensor_tensor(geo_own[:, par], geo_own[:, par], by_query[1], ALU.add).then_inc(k.geo_own, 1)
                pool.wait_ge(k.geo_own, 3 * b + 2)
                nc.gpsimd.tensor_tensor(geo_own[:, par], geo_own[:, par], g.t("mask_own")[:, None, None, :].to_broadcast(shape),
                                        ALU.add).then_inc(k.geo_own, 1)
                pool.wait_ge(k.v_turned, b + 1)
                for kind in ("att_weighed", "geo_weighed"):
                    pool.wait_ge(by_group[1][kind], b)
                diagonal(v_diag[:, :, :, 0:DH0], v_rows[:, :, 0:DH0], g.t("own_head"), GROUPS * KB, DH0).then_inc(k.v_diag, 1)

            def step(b, par, ahead):
                if ahead:
                    ahead(b + 1, 1 - par)
            pool.wait_ge(k.ones, PER)
            steps(pool, front, step)


class Chain:

    def __init__(self, eng, sem, per, it):
        self.eng, self.sem, self.per, self.it, self.n = eng, sem, per, it, 0

    def __call__(self, ins, wait=True):
        ins.then_inc(self.sem, 1)
        self.n += 1
        assert self.n <= self.per
        if wait:
            self.done()

    def done(self):
        self.eng.wait_ge(self.sem, self.per * self.it + self.n)


TILES = CH // 128
ROW = D + E0


def route_phase(nc, dram, g):
    CHOICES = TILES * K0
    with Scope(nc, "route") as s:
        gate_w = s.sb("gate_w", [128, E0], BF16)
        gate_wf = s.sb("gate_wf", [128, E0])
        bias = s.sb("bias", [128, E0])
        sw_bf = s.sb("sw_bf", [128, 2, I0], BF16)
        sw = s.sb("sw", [128, 2, I0])
        sw2_bf = s.sb("sw2_bf", [I0, D], BF16)
        sw2 = s.sb("sw2", [I0, D])
        iota = s.sb("iota", [128, CAP], BF16)
        before = s.sb("before", [128, 128], BF16)
        ones = s.sb("ones", [128, 128], BF16)
        zero = s.sb("zero", [128, 13 * D])
        zero_bf = s.sb("zero_bf", [128, 128], BF16)
        sq = s.sb("sq", [128, PAR, CH])
        unit = s.sb("unit", [128, PAR, CH])
        h2 = s.sb("h2", [128, PAR, CH])
        rows = s.sb("rows", [128, PAR, TILES, ROW])
        score = s.sb("score", [128, PAR, TILES, E0])
        biased = s.sb("biased", [128, PAR, TILES, E0])
        top = s.sb("top", [128, PAR, TILES, 8])
        top_at = s.sb("top_at", [128, PAR, TILES, 8], U32)
        chosen = s.sb("chosen", [128, PAR, TILES, K0])
        onehot = s.sb("onehot", [128, PAR, CHOICES, E0], BF16)
        by_expert = s.sb("by_expert", [128, PAR, 3, CHOICES, E0], BF16)
        mask = s.sb("mask", [128, PAR, TILES, E0], BF16)
        gates = s.sb("gates", [128, PAR, TILES, E0])
        total = s.sb("total", [128, PAR, TILES])
        seen = s.sb("seen", [128, PAR, 1])
        place = s.sb("place", [128, PAR, TILES, E0])
        base = s.sb("base", [128, PAR, E0])
        own = s.sb("own", [128, PAR, CHOICES, E0])
        slot = s.sb("slot", [128, PAR, CHOICES])
        by_slot = s.sb("by_slot", [128, PAR, CHOICES, CAP], BF16)
        sig1 = s.sb("sig1", [I0, PAR, CH])
        hid = s.sb("hid", [I0, PAR, CH])
        held = s.sb("held", [128, 3, E0])
        free = s.sb("free", [128, E0])
        rstd = [Rstd(s, f"rstd{par}") for par in range(PAR)]
        slots_ps, turned = s.ps("slots_ps"), s.ps("turned")
        bank = [[s.ps(f"bank{n}{par}") for n in range(3)] for par in range(PAR)]
        mid, up1, shared, var, up3, small = ([bank[par][n] for par in range(PAR)] for n in (0, 0, 0, 1, 1, 2))
        c = s.sems("w_in zeroed consts cleared zero_out rows_read counted slots_done held tail")
        k = [s.sems("rows_out centered squared var unit modulated logits up1 up3 turned score sig1 mask counted"
                    " route spread hid_part hid shared_made x_done slots_added", par) for par in range(PAR)]
        block = s.block()
        STEPS = 2 * TILES + 11 + CHOICES
        LAST = NCH // PAR - 1
        cols = lambda i, par: bass.ds(i * (PAR * CH) + par * CH, CH)
        both = range(PAR)

        @block.sync
        def _(sp):
            sp.dma_start(gate_w[:, :], dram["gate_w"]).then_inc(c.w_in, 16)
            sp.dma_start(bias[:, :], dram["gate_bias"].to_broadcast([128, E0])).then_inc(c.w_in, 16)
            sp.dma_start(sw_bf[:, :, :], dram["sw13"]).then_inc(c.w_in, 16)
            sp.dma_start(sw2_bf[:, :], dram["sw2"]).then_inc(c.w_in, 16)
            sp.wait_ge(c.zeroed, 1)
            acc = g.acc.rearrange("(p r) c -> p (r c)", p=128)
            for i in range(5):
                sp.dma_start(acc[:, i * 13 * D:(i + 1) * 13 * D], zero[:, :]).then_inc(c.zero_out, 16)
            sp.dma_start(g.rows[N:N + CAP, :], zero[:, 0:ROW]).then_inc(c.zero_out, 16)
            with sp.Fori(0, NCH // PAR) as i:
                for par in both:
                    sp.wait_ge(c.rows_read, PAR * i + par + 1)
                    sp.wait_ge(k[par].route, STEPS * i + 2 * TILES + 9)
                    sp.dma_start(g.rows[cols(i, par), :].rearrange("(r p) c -> p r c", p=128), rows[:, par])\
                        .then_inc(k[par].rows_out, 16)
            for par in both:
                sp.wait_ge(k[par].rows_out, 16 * (NCH // PAR))
            sp.wait_ge(c.zero_out, 16 * 6)

        @block.tensor
        def _(pe):
            pe.wait_ge(c.consts, 5)
            nc.tensor.matmul(slots_ps[:, 0:3 * E0], zero_bf[:, :], zero_bf[:, 0:3 * E0], start=True, stop=False)

            def norm(i):
                for par in both:
                    pe.wait_ge(k[par].x_done, i)
                    nc.tensor.matmul(mid[par][:, :], g.t("center"), g.xT[:, cols(i, par)], start=True, stop=True)\
                        .then_inc(k[par].centered, 1)
                for par in both:
                    pe.wait_ge(k[par].squared, i + 1)
                    nc.tensor.matmul(var[par][:, :], g.t("mean"), sq[:, par, :], start=True, stop=True)\
                        .then_inc(k[par].var, 1)

            def up_and_turn(i):
                for par in both:
                    pe.wait_ge(k[par].modulated, i + 1)
                    pe.wait_ge(k[par].counted, i)
                    for j in range(TILES):
                        last = nc.tensor.matmul(small[par][:, j * E0:(j + 1) * E0], h2[:, par, 128 * j:128 * j + 128],
                                                gate_wf[:, :], start=True, stop=True)
                    last.then_inc(k[par].logits, 1)
                for par in both:
                    nc.tensor.matmul(up1[par][0:I0, :], sw[:, 0, :], h2[:, par, :], start=True, stop=True)\
                        .then_inc(k[par].up1, 1)
                    nc.tensor.matmul(up3[par][0:I0, :], sw[:, 1, :], h2[:, par, :], start=True, stop=True)\
                        .then_inc(k[par].up3, 1)
                for par in both:
                    pe.wait_ge(c.rows_read, PAR * i + par)
                    for j in range(TILES):
                        last = nc.tensor.transpose(turned[:, 128 * j:128 * j + 128], h2[:, par, 128 * j:128 * j + 128],
                                                   g.t("ident"))
                    last.then_inc(k[par].turned, 1)

            def count(i):
                for par in both:
                    pe.wait_ge(k[par].route, STEPS * i + 2 * TILES + 4)
                    for j in range(TILES + 1):
                        out = small[par][:, 128 + j * E0:128 + (j + 1) * E0]
                        for n in range(min(j, TILES)):
                            last = nc.tensor.matmul(out, ones[:, :], mask[:, par, n, :], start=n == 0, stop=n == TILES - 1)
                        if j < TILES:
                            last = nc.tensor.matmul(out, before[:, :], mask[:, par, j, :], start=j == 0, stop=True)
                    last.then_inc(k[par].mask, 1)

            def share(i):
                for par in both:
                    pe.wait_ge(k[par].hid, i + 1)
                    nc.tensor.matmul(shared[par][:, :], sw2[:, :], hid[:, par, :], start=True, stop=True)\
                        .then_inc(k[par].shared_made, 1)

            def add_slots(i):
                for par in both:
                    pe.wait_ge(k[par].route, STEPS * (i + 1))
                    pe.wait_ge(k[par].spread, 3 * (i + 1))
                    for n in range(CHOICES):
                        last = nc.tensor.matmul(slots_ps[:, 0:3 * E0], by_slot[:, par, n, :], by_expert[:, par, :, n, :],
                                                start=False, stop=False)
                    last.then_inc(k[par].slots_added, 1)
            norm(0)
            up_and_turn(0)
            with pe.Fori(0, LAST) as i:
                count(i)
                share(i)
                norm(i + 1)
                up_and_turn(i + 1)
                add_slots(i)
            count(LAST)
            share(LAST)
            add_slots(LAST)
            nc.tensor.matmul(slots_ps[:, 0:3 * E0], zero_bf[:, :], zero_bf[:, 0:3 * E0], start=False, stop=True)\
                .then_inc(c.slots_done, 1)

        @block.scalar
        def _(act):
            def modulate(i):
                for par in both:
                    act.wait_ge(k[par].centered, i + 1)
                    nc.scalar.activation(sq[:, par, :], mid[par][:, :], ACT.Square).then_inc(k[par].squared, 1)
                for par in both:
                    act.wait_ge(k[par].unit, i + 1)
                    act.wait_ge(k[par].turned, i)
                    for j in range(BPC):
                        b = i * (PAR * BPC) + par * BPC + j
                        last = nc.scalar.activation(h2[:, par, j * T:(j + 1) * T], unit[:, par, j * T:(j + 1) * T],
                                                    ACT.Identity, scale=g.mod[:, 0, 4, bass.ds(b, 1)],
                                                    bias=g.mod[:, 0, 3, bass.ds(b, 1)])
                    last.then_inc(k[par].modulated, 1)

            def score_and_rows(i):
                for par in both:
                    act.wait_ge(k[par].logits, i + 1)
                    act.wait_ge(k[par].hid_part, i)
                    nc.scalar.activation(score[:, par].rearrange("p j e -> p (j e)"), small[par][:, 0:TILES * E0],
                                         ACT.Sigmoid).then_inc(k[par].score, 1)
                for par in both:
                    act.wait_ge(k[par].up1, i + 1)
                    act.wait_ge(k[par].hid, i)
                    nc.scalar.activation(sig1[:, par, :], up1[par][0:I0, :], ACT.Sigmoid).then_inc(k[par].sig1, 1)
                for par in both:
                    act.wait_ge(k[par].turned, i + 1)
                    act.wait_ge(k[par].rows_out, 16 * i)
                    nc.scalar.activation(rows[:, par, :, 0:D], turned[:, :].rearrange("p (j c) -> p j c", c=D), ACT.Copy)\
                        .then_inc(c.rows_read, 1)
            modulate(0)
            with act.Fori(0, LAST) as i:
                score_and_rows(i)
                modulate(i + 1)
            score_and_rows(LAST)

        @block.vector
        def _(dve):
            nc.vector.memset(zero[:, :], 0.0).then_inc(c.zeroed, 1)
            nc.vector.memset(base[:, 0, :], 0.0).then_inc(c.cleared, 1)
            nc.vector.memset(zero_bf[:, :], 0.0).then_inc(c.consts, 1)
            nc.vector.tensor_copy(before[:, :], g.t("before")).then_inc(c.consts, 1)
            nc.vector.tensor_copy(ones[:, :], g.t("ones")).then_inc(c.consts, 1)
            nc.vector.tensor_copy(iota[:, :], g.t("iota")[:, 0:CAP]).then_inc(c.cleared, 1)
            dve.wait_ge(c.w_in, 64)
            nc.vector.tensor_copy(gate_wf[:, :], gate_w[:, :]).then_inc(c.consts, 1)
            nc.vector.tensor_copy(sw[:, :, :], sw_bf[:, :, :])
            nc.vector.tensor_copy(sw2[:, :], sw2_bf[:, :]).then_inc(c.consts, 1)
            dve.wait_ge(c.cleared, 2)

            def per_tile(ap):
                return ap[:, None, :].to_broadcast([128, TILES, E0])

            def by_choice(ap):
                return ap.rearrange("p (j c) e -> p j c e", c=K0)

            def norm(i):
                run_roots(nc, dve, rstd, [var[par][:, :] for par in both], LN_EPS, i, [k[par].var for par in both])
                for par in both:
                    nc.vector.tensor_tensor(unit[:, par, :], mid[par][:, :], rstd[par].out[:, :], ALU.mult)\
                        .then_inc(k[par].unit, 1)

            def choose(i):
                then = [Chain(dve, k[par].route, STEPS, i) for par in both]
                for par in both:
                    dve.wait_ge(k[par].score, i + 1)
                    then[par](nc.vector.tensor_tensor(biased[:, par], score[:, par], per_tile(bias), ALU.add), wait=False)
                for par in both:
                    then[par].done()
                    nc.vector.tensor_copy(seen[:, par, 0:1], biased[:, par, 0, 0:1])
                    for j in range(TILES):
                        then[par](nc.vector.max(top[:, par, j, :], biased[:, par, j, :]), wait=False)
                for par in both:
                    then[par].done()
                    nc.vector.tensor_copy(seen[:, par, 0:1], top[:, par, 0, 0:1])
                    for j in range(TILES):
                        then[par](nc.vector.max_index(top_at[:, par, j, :], top[:, par, j, :], biased[:, par, j, :]), wait=False)
                for par in both:
                    then[par].done()
                    then[par](nc.vector.tensor_copy(chosen[:, par], top_at[:, par, :, 0:K0]), wait=False)
                for par in both:
                    dve.wait_ge(k[par].spread, 3 * i)
                    then[par].done()
                    then[par](nc.vector.tensor_tensor(onehot[:, par], g.t("iota")[:, None, 0:E0]
                                                      .to_broadcast([128, CHOICES, E0]),
                                                      chosen[:, par].rearrange("p j c -> p (j c)")[:, :, None]
                                                      .to_broadcast([128, CHOICES, E0]), ALU.is_equal), wait=False)
                for par in both:
                    then[par].done()
                    with nc.allow_low_precision(reason="sums of one-hot rows are 0 or 1"):
                        then[par](nc.vector.tensor_reduce(mask[:, par], onehot[:, par].rearrange("p (j c) e -> p j e c", c=K0),
                                                          AX.X, ALU.add), wait=False)
                for par in both:
                    then[par].done()
                    then[par](nc.vector.tensor_tensor(gates[:, par], mask[:, par], score[:, par], ALU.mult), wait=False)
                for par in both:
                    then[par].done()
                    then[par](nc.vector.tensor_reduce(total[:, par], gates[:, par], AX.X, ALU.add), wait=False)
                for par in both:
                    then[par].done()
                    then[par](nc.vector.tensor_scalar(total[:, par], total[:, par], 1e-12, None, ALU.max), wait=False)
                for par in both:
                    then[par].done()
                    then[par](nc.vector.reciprocal(total[:, par], total[:, par]), wait=False)
                for par in both:
                    dve.wait_ge(k[par].rows_out, 16 * i)
                    then[par].done()
                    then[par](nc.vector.tensor_tensor(rows[:, par, :, D:ROW], gates[:, par], total[:, par, :, None]
                                                      .to_broadcast([128, TILES, E0]), ALU.mult), wait=False)
                for par in both:
                    dve.wait_ge(k[par].sig1, i + 1)
                    nc.vector.tensor_tensor(sig1[:, par, :], sig1[:, par, :], up1[par][0:I0, :], ALU.mult)\
                        .then_inc(k[par].hid_part, 1)
                for par in both:
                    dve.wait_ge(k[par].hid_part, i + 1)
                    dve.wait_ge(k[par].up3, i + 1)
                    nc.vector.tensor_tensor(hid[:, par, :], sig1[:, par, :], up3[par][0:I0, :], ALU.mult)\
                        .then_inc(k[par].hid, 1)
                for par in both:
                    dve.wait_ge(k[par].mask, i + 1)
                    dve.wait_ge(c.counted, PAR * i + par)
                    then[par](nc.vector.tensor_tensor(place[:, par], small[par][:, 128:128 + TILES * E0]
                                                      .rearrange("p (j e) -> p j e", e=E0), per_tile(base[:, par, :]), ALU.add), wait=False)
                    then[1 - par].done()
                    nc.vector.tensor_tensor(base[:, 1 - par, :], base[:, par, :], small[par][:, 128 + TILES * E0:128 + (TILES + 1) * E0],
                                            ALU.add).then_inc(c.counted, 1)
                for par in both:
                    dve.wait_ge(c.counted, PAR * i + par + 1)
                    then[par].done()
                    nc.vector.tensor_tensor(by_choice(own[:, par]), by_choice(onehot[:, par]),
                                            place[:, par, :, None, :].to_broadcast([128, TILES, K0, E0]), ALU.mult)\
                        .then_inc(k[par].counted, 1)
                for par in both:
                    dve.wait_ge(k[par].shared_made, i + 1)
                    for j in range(BPC):
                        b = i * (PAR * BPC) + par * BPC + j
                        x = g.xT[:, bass.ds(b * T, T)]
                        last = nc.vector.scalar_tensor_tensor(x, shared[par][:, j * T:(j + 1) * T],
                                                              g.mod[:, 0, 5, bass.ds(b, 1)], x, ALU.mult, ALU.add)
                    last.then_inc(k[par].x_done, 1)
                for par in both:
                    dve.wait_ge(k[par].counted, i + 1)
                    dve.wait_ge(k[par].slots_added, i)
                    then[par](nc.vector.tensor_reduce(slot[:, par], own[:, par], AX.X, ALU.add), wait=False)
                return then

            def spread_slots(then, par):
                then[par].done()
                for n in range(CHOICES):
                    then[par](nc.vector.tensor_scalar(by_slot[:, par, n, :], iota[:, :], slot[:, par, n:n + 1], None,
                                                      ALU.is_equal), wait=False)
            norm(0)
            with dve.Fori(0, LAST) as i:
                then = choose(i)
                spread_slots(then, 0)
                norm(i + 1)
                spread_slots(then, 1)
            then = choose(LAST)
            for par in both:
                spread_slots(then, par)
            dve.wait_ge(c.slots_done, 1)
            nc.vector.tensor_copy(held[:, :, :].rearrange("p v e -> p (v e)"), slots_ps[:, 0:3 * E0]).then_inc(c.held, 1)
            dve.wait_ge(c.held, 1)
            nc.vector.tensor_scalar(free[:, :], held[:, 0, :], -1.0, 1.0, ALU.mult, ALU.add).then_inc(c.tail, 1)
            nc.vector.scalar_tensor_tensor(held[:, 1, :], held[:, 2, :], 128.0, held[:, 1, :], ALU.mult, ALU.add)\
                .then_inc(c.tail, 1)
            dve.wait_ge(c.tail, 2)
            nc.vector.scalar_tensor_tensor(held[:, 1, :], free[:, :], g.t("past"), held[:, 1, :], ALU.mult, ALU.add)\
                .then_inc(c.tail, 1)
            dve.wait_ge(c.tail, 3)
            nc.vector.tensor_copy(g.slot_token[:, :], held[:, 1, :])

        @block.gpsimd
        def _(pool):
            wide = lambda ap: ap.to_broadcast([128, CHOICES, E0])
            with pool.Fori(0, NCH // PAR) as i:
                for par in both:
                    pool.wait_ge(k[par].slots_added, i)
                    pool.wait_ge(k[par].route, STEPS * i + 2 * TILES + 4)
                    nc.gpsimd.tensor_tensor(by_expert[:, par, 0], onehot[:, par], wide(g.t("ones")[:, 0:1, None]), ALU.mult)\
                        .then_inc(k[par].spread, 1)
                    nc.gpsimd.tensor_tensor(by_expert[:, par, 1], onehot[:, par], wide(g.t("row_no")[:, :, None]), ALU.mult)\
                        .then_inc(k[par].spread, 1)
                    tile = g.t("tile_no")[:, bass.ds(i * (PAR * TILES) + par * TILES, TILES)]
                    nc.gpsimd.tensor_tensor(by_expert[:, par, 2].rearrange("p (j c) e -> p j c e", c=K0),
                                            onehot[:, par].rearrange("p (j c) e -> p j c e", c=K0),
                                            tile[:, :, None, None].to_broadcast([128, TILES, K0, E0]), ALU.mult)\
                        .then_inc(k[par].spread, 1)


def experts_phase(nc, dram, g):
    with Scope(nc, "exp") as s:
        w13_bf = s.sb("w13_bf", [128, E0, 2 * I0], BF16)
        w2_bf = s.sb("w2_bf", [I0, E0, D], BF16)
        w13 = s.sb("w13", [128, E0, 2 * I0])
        w2 = s.sb("w2", [I0, E0, D])
        rows = s.sb("rows", [128, E0 * ROW])
        y = s.sb("y", [128, E0 * D])
        xg = s.sb("xg", [128, PAR, D])
        xgT = s.sb("xgT", [128, PAR, 128])
        sig = s.sb("sig", [128, PAR, I0])
        hid = s.sb("hid", [128, PAR, 128])
        hidT = s.sb("hidT", [I0, PAR, 128])
        ps = [[s.ps(f"{n}{par}") for n in ("x", "up", "h", "down")] for par in range(PAR)]
        PART = 8
        w = s.sems("w_in padded w13 w2 added")
        gathered = [s.sems("gathered", q).gathered for q in range(E0 // PART)]
        k = [s.sems("staged turned x_copied up sig part hid h_turned h_copied down y", par) for par in range(PAR)]
        block = s.block()

        @block.sync
        def _(sp):
            sp.dma_start(w13_bf[:, :, :], dram["w13"]).then_inc(w.w_in, 16)
            sp.dma_start(w2_bf[:, :, :], dram["w2"]).then_inc(w.w_in, 16)

        @block.gpsimd
        def _(pool):
            def gather(e):
                nc.gpsimd.indirect_dma_start(rows[:, e * ROW:(e + 1) * ROW], None, g.rows,
                                             bass.IndirectOffsetOnAxis(g.slot_token[:, e:e + 1], 0))\
                    .then_inc(gathered[e // PART], 16)
            for e in range(PART):
                gather(e)
            for e in range(E0):
                if e + PART < E0:
                    gather(e + PART)
                pool.wait_ge(k[e % PAR].y, e // PAR + 1)
                if e:
                    pool.wait_ge(w.added, 16 * e)
                nc.gpsimd.indirect_dma_start(g.acc, bass.IndirectOffsetOnAxis(g.slot_token[:, e:e + 1], 0),
                                             y[:, e * D:(e + 1) * D], None, compute_op=ALU.add).then_inc(w.added, 16)
            pool.wait_ge(w.added, 16 * E0)

        @block.tensor
        def _(pe):
            pe.wait_ge(w.w13, 1)
            pe.wait_ge(w.w2, 1)
            with pe.Fori(0, E0 // PAR) as i:
                for par in range(PAR):
                    pe.wait_ge(k[par].staged, i + 1)
                    nc.tensor.transpose(ps[par][0][:, 0:128], xg[:, par, :], g.t("ident")).then_inc(k[par].turned, 1)
                for par in range(PAR):
                    pe.wait_ge(k[par].x_copied, i + 1)
                    nc.tensor.matmul(ps[par][1][:, 0:2 * I0], xgT[:, par, :], w13[:, bass.ds(i * PAR + par, 1), :]
                                     .rearrange("p e i -> p (e i)"), start=True, stop=True).then_inc(k[par].up, 1)
                for par in range(PAR):
                    pe.wait_ge(k[par].hid, i + 1)
                    nc.tensor.transpose(ps[par][2][:, 0:128], hid[:, par, :], g.t("ident")).then_inc(k[par].h_turned, 1)
                for par in range(PAR):
                    pe.wait_ge(k[par].h_copied, i + 1)
                    nc.tensor.matmul(ps[par][3][:, 0:D], hidT[:, par, :], w2[:, bass.ds(i * PAR + par, 1), :]
                                     .rearrange("p e i -> p (e i)"), start=True, stop=True).then_inc(k[par].down, 1)

        @block.scalar
        def _(act):
            act.wait_ge(w.w_in, 32)
            nc.scalar.activation(w2[:, :, :], w2_bf[:, :, :], ACT.Copy).then_inc(w.w2, 1)
            with act.Fori(0, E0 // PAR) as i:
                for par in range(PAR):
                    act.wait_ge(k[par].turned, i + 1)
                    nc.scalar.activation(xgT[:, par, :], ps[par][0][:, 0:128], ACT.Copy).then_inc(k[par].x_copied, 1)
                for par in range(PAR):
                    act.wait_ge(k[par].up, i + 1)
                    nc.scalar.activation(sig[:, par, :], ps[par][1][:, 0:I0], ACT.Sigmoid).then_inc(k[par].sig, 1)
                for par in range(PAR):
                    act.wait_ge(k[par].h_turned, i + 1)
                    nc.scalar.activation(hidT[:, par, :], ps[par][2][0:I0, 0:128], ACT.Copy).then_inc(k[par].h_copied, 1)

        @block.vector
        def _(dve):
            dve.wait_ge(w.w_in, 32)
            nc.vector.tensor_copy(w13[:, :, :], w13_bf[:, :, :]).then_inc(w.w13, 1)
            nc.vector.memset(hid[:, :, :], 0.0).then_inc(w.padded, 1)
            dve.wait_ge(w.padded, 1)
            for q in range(E0 // PART):
                dve.wait_ge(gathered[q], 16 * PART)
                with dve.Fori(q * PART // PAR, (q + 1) * PART // PAR) as i:
                    for par in range(PAR):
                        dve.wait_ge(k[par].turned, i)
                        nc.vector.tensor_copy(xg[:, par, :], rows[:, bass.ds(i * (PAR * ROW) + par * ROW, D)])\
                            .then_inc(k[par].staged, 1)
                    for par in range(PAR):
                        dve.wait_ge(k[par].sig, i + 1)
                        nc.vector.tensor_tensor(sig[:, par, :], sig[:, par, :], ps[par][1][:, 0:I0], ALU.mult)\
                            .then_inc(k[par].part, 1)
                    for par in range(PAR):
                        dve.wait_ge(k[par].part, i + 1)
                        nc.vector.tensor_tensor(hid[:, par, 0:I0], sig[:, par, :], ps[par][1][:, I0:2 * I0], ALU.mult)\
                            .then_inc(k[par].hid, 1)
                    for par in range(PAR):
                        dve.wait_ge(k[par].down, i + 1)
                        nc.vector.tensor_scalar(y[:, bass.ds(i * (PAR * D) + par * D, D)], ps[par][3][:, 0:D],
                                                rows[:, bass.ds(i * (PAR * (ROW + 1)) + par * (ROW + 1) + D, 1)], None,
                                                ALU.mult).then_inc(k[par].y, 1)


GT = 8


def project_phase(nc, dram, g):
    LEAD = CONV - 1
    HEADS_IN_BLOCK = SLOT // DH1
    ROOTS = 2 * RC * HEADS_IN_BLOCK
    with Scope(nc, "proj") as s:
        w = s.sb("w", [128, 3, 128])
        wb = s.sb("wb", [128, H1])
        wb_wide = s.sb("wb_wide", [128, H1, DH1])
        bias = s.sb("bias", [128, 4])
        taps = s.sb("taps", [128, 3, CONV])
        last_bias = s.sb("last_bias", [128, 3])
        rows = s.sb("rows", [128, PAR, TILES, D])
        unit = s.sb("unit", [128, PAR, CH])
        h3 = s.sb("h3", [128, PAR, CH])
        pad = s.sb("pad", [128, PAR, 3, BPC, LEAD + T])
        conv = s.sb("conv", [128, PAR, 3, CH])
        sq2 = s.sb("sq2", [128, PAR, 2, CH])
        rate = s.sb("rate", [128, PAR, CH])
        len_t = s.sb("len_t", [128, PAR, 2, RC, SLOT])
        inv = s.sb("inv", [128, PAR, 2, RC, HEADS_IN_BLOCK])
        rstd = [Rstd(s, f"rstd{par}", room=(sq2[:, par, 0, :], sq2[:, par, 1, :])) for par in range(PAR)]
        root = [Rstd(s, f"root{par}", ROOTS, parts=False) for par in range(PAR)]
        bank = [[s.ps(f"bank{i}{par}") for i in range(4)] for par in range(PAR)]
        turned, var, mid, made, sums = ([bank[par][0] for par in range(PAR)], [bank[par][0] for par in range(PAR)],
                                        [bank[par][1] for par in range(PAR)], bank,
                                        [bank[par][0:2] for par in range(PAR)])
        c = s.sems("w_in wide zeroed")
        k = [s.sems("rows_in turned x_added x_out centered squared var unit modulated made0 made1 made2 made3"
                    " padded0 padded1 padded2 sq2_0 sq2_1 sum0 sum1 len0 len1 sig rate conv inv v_part v_done k_done"
                    " q_done b_done spread", par) for par in range(PAR)]
        block = s.block()
        acc = g.acc[0:N, :]
        CONVS = 3 * LEAD
        LAST = NCH // PAR - 1
        cols = lambda i, par: bass.ds(i * (PAR * CH) + par * CH, CH)
        both = range(PAR)

        @block.sync
        def _(sp):
            for dst, name in ((w[:, :, :], "w1_qkv"), (wb[:, :], "w_beta"), (bias[:, :], "b1"), (taps[:, :, :], "taps")):
                sp.dma_start(dst, dram[name]).then_inc(c.w_in, 16)
            with sp.Fori(0, NCH // PAR) as i:
                for par in both:
                    sp.wait_ge(k[par].turned, i)
                    sp.dma_start(rows[:, par], acc[cols(i, par), :].rearrange("(r p) c -> p r c", p=128))\
                        .then_inc(k[par].rows_in, 16)
                for par in both:
                    sp.wait_ge(k[par].x_added, i + 1)
                    sp.dma_start(g.x_kept[:, cols(i, par)], g.xT[:, cols(i, par)]).then_inc(k[par].x_out, 16)
            for par in both:
                sp.wait_ge(k[par].x_out, 16 * (NCH // PAR))

        @block.tensor
        def _(pe):
            pe.wait_ge(c.wide, 2)

            def turn(i):
                for par in both:
                    pe.wait_ge(k[par].rows_in, 16 * (i + 1))
                    pe.wait_ge(k[par].padded0, i)
                    for r in range(TILES):
                        last = nc.tensor.transpose(turned[par][:, 128 * r:128 * r + 128], rows[:, par, r, :], g.t("ident"))
                    last.then_inc(k[par].turned, 1)

            def center(i):
                for par in both:
                    pe.wait_ge(k[par].x_added, i + 1)
                    pe.wait_ge(k[par].padded1, i)
                    nc.tensor.matmul(mid[par][:, :], g.t("center"), g.xT[:, cols(i, par)], start=True, stop=True)\
                        .then_inc(k[par].centered, 1)

            def variance(i):
                for par in both:
                    pe.wait_ge(k[par].squared, i + 1)
                    nc.tensor.matmul(var[par][:, :], g.t("mean"), unit[:, par, :], start=True, stop=True)\
                        .then_inc(k[par].var, 1)

            def make(i):
                for par in both:
                    pe.wait_ge(k[par].modulated, i + 1)
                    pe.wait_ge(k[par].len0, i)
                    pe.wait_ge(k[par].len1, i)
                    pe.wait_ge(k[par].padded2, i)
                    for n, sem in enumerate((k[par].made0, k[par].made1, k[par].made2)):
                        nc.tensor.matmul(made[par][n][:, :], w[:, n, :], h3[:, par, :], start=True, stop=True).then_inc(sem, 1)
                    pe.wait_ge(k[par].rate, i)
                    nc.tensor.matmul(made[par][3][:, :], wb_wide[:, :, :].rearrange("p h d -> p (h d)"), h3[:, par, :],
                                     start=True, stop=True).then_inc(k[par].made3, 1)

            def sum_squares(i):
                for n in range(2):
                    for par in both:
                        pe.wait_ge((k[par].sq2_0, k[par].sq2_1)[n], i + 1)
                        nc.tensor.matmul(sums[par][n][:, :], g.t("same_head"), sq2[:, par, n, :], start=True, stop=True)\
                            .then_inc((k[par].sum0, k[par].sum1)[n], 1)
            turn(0)
            center(0)
            variance(0)
            make(0)
            with pe.Fori(0, LAST) as i:
                turn(i + 1)
                center(i + 1)
                variance(i + 1)
                sum_squares(i)
                make(i + 1)
            sum_squares(LAST)

        @block.scalar
        def _(act):
            act.wait_ge(c.wide, 2)
            act.wait_ge(c.zeroed, 1)

            def square(i, first=False):
                for par in both:
                    act.wait_ge(k[par].centered, i + 1)
                    if not first:
                        act.wait_ge(k[par].v_part, i - 1)
                    nc.scalar.activation(unit[:, par, :], mid[par][:, :], ACT.Square).then_inc(k[par].squared, 1)

            def modulate(i):
                for par in both:
                    act.wait_ge(k[par].unit, i + 1)
                    act.wait_ge(k[par].made3, i)
                    for j in range(BPC):
                        b = i * (PAR * BPC) + par * BPC + j
                        last = nc.scalar.activation(h3[:, par, j * T:(j + 1) * T], unit[:, par, j * T:(j + 1) * T],
                                                    ACT.Identity, scale=g.mod[:, 1, 1, bass.ds(b, 1)],
                                                    bias=g.mod[:, 1, 0, bass.ds(b, 1)])
                    last.then_inc(k[par].modulated, 1)

            def pads(i):
                for n in range(3):
                    for par in both:
                        act.wait_ge((k[par].k_done, k[par].q_done, k[par].v_done)[n], i)
                        act.wait_ge((k[par].made0, k[par].made1, k[par].made2)[n], i + 1)
                        nc.scalar.activation(pad[:, par, n, :, LEAD:LEAD + T],
                                             made[par][n][:, :].rearrange("p (b t) -> p b t", t=T),
                                             ACT.Identity, bias=bias[:, n:n + 1])
                        nc.scalar.activation(conv[:, par, n, :], made[par][n][:, :], ACT.Identity, scale=taps[:, n, LEAD:CONV],
                                             bias=last_bias[:, n:n + 1])\
                            .then_inc((k[par].padded0, k[par].padded1, k[par].padded2)[n], 1)

            def square_convs(i, last=False):
                for n in range(2):
                    for par in both:
                        act.wait_ge(k[par].conv, CONVS * i + LEAD * (n + 1))
                        if not last:
                            act.wait_ge(k[par].unit, i + 2)
                        nc.scalar.activation(sq2[:, par, n, :], conv[:, par, n, :], ACT.Square)\
                            .then_inc((k[par].sq2_0, k[par].sq2_1)[n], 1)

            def sigmoids(i, last=False):
                for par in both:
                    act.wait_ge(k[par].made3, i + 1)
                    act.wait_ge(k[par].b_done, i)
                    nc.scalar.activation(rate[:, par, :], made[par][3][:, :], ACT.Sigmoid, bias=bias[:, 3:4])\
                        .then_inc(k[par].rate, 1)
                for par in both:
                    act.wait_ge(k[par].conv, CONVS * (i + 1))
                    if not last:
                        act.wait_ge(k[par].modulated, i + 2)
                    nc.scalar.activation(unit[:, par, :], conv[:, par, 2, :], ACT.Sigmoid).then_inc(k[par].sig, 1)
            square(0, first=True)
            modulate(0)
            with act.Fori(0, LAST) as i:
                pads(i)
                square(i + 1)
                square_convs(i)
                modulate(i + 1)
                sigmoids(i)
            pads(LAST)
            square_convs(LAST, last=True)
            sigmoids(LAST, last=True)

        @block.vector
        def _(dve):
            nc.vector.memset(pad[:, :, :, :, 0:LEAD], 0.0).then_inc(c.zeroed, 1)
            dve.wait_ge(c.w_in, 64)
            nc.vector.tensor_copy(wb_wide[:, :, :], wb[:, :, None].to_broadcast([128, H1, DH1])).then_inc(c.wide, 1)
            nc.vector.tensor_tensor(last_bias[:, :], bias[:, 0:3], taps[:, :, LEAD], ALU.mult).then_inc(c.wide, 1)

            def add_experts(i):
                for par in both:
                    dve.wait_ge(k[par].turned, i + 1)
                    for j in range(BPC):
                        b = i * (PAR * BPC) + par * BPC + j
                        x = g.xT[:, bass.ds(b * T, T)]
                        last = nc.vector.scalar_tensor_tensor(x, turned[par][:, j * T:(j + 1) * T],
                                                              g.mod[:, 0, 5, bass.ds(b, 1)], x, ALU.mult, ALU.add)
                    last.then_inc(k[par].x_added, 1)

            def norm(i):
                run_roots(nc, dve, rstd, [var[par][:, :] for par in both], LN_EPS, i, [k[par].var for par in both])
                for par in both:
                    nc.vector.tensor_tensor(unit[:, par, :], mid[par][:, :], rstd[par].out[:, :], ALU.mult)\
                        .then_inc(k[par].unit, 1)

            def convolve(then, i, n):
                for tap in range(LEAD):
                    for par in both:
                        if tap == 0:
                            dve.wait_ge((k[par].padded0, k[par].padded1, k[par].padded2)[n], i + 1)
                        else:
                            then[par].done()
                        out = conv[:, par, n, :].rearrange("p (b t) -> p b t", t=T)
                        then[par](nc.vector.scalar_tensor_tensor(out, pad[:, par, n, :, tap:tap + T],
                                                                 taps[:, n, tap:tap + 1], out, ALU.mult, ALU.add),
                                  wait=False)

            def scale(i):
                for n in range(2):
                    for par in both:
                        dve.wait_ge((k[par].sum0, k[par].sum1)[n], i + 1)
                        nc.vector.transpose(len_t[:, par, n].rearrange("p n i -> p (n i)"), sums[par][n][:, :])\
                            .then_inc((k[par].len0, k[par].len1)[n], 1)
                STEPS = 5
                then = [Chain(dve, k[par].inv, STEPS, i) for par in both]
                own = [len_t[:, par].rearrange("p s n (h d) -> p (s n h) d", d=DH1)[:, :, 0] for par in both]
                flat = [inv[:, par].rearrange("p s n h -> p (s n h)") for par in both]
                for par in both:
                    dve.wait_ge(k[par].len0, i + 1)
                    dve.wait_ge(k[par].len1, i + 1)
                    then[par](nc.vector.tensor_scalar(root[par].v[:, :], own[par], 1e-30, None, ALU.max), wait=False)
                for par in both:
                    then[par].done()
                newton_roots(nc, dve, root, i)
                for par in both:
                    then[par](nc.vector.tensor_tensor(flat[par], own[par], root[par].y[:, :], ALU.mult), wait=False)
                for par in both:
                    then[par].done()
                    then[par](nc.vector.tensor_scalar(flat[par], flat[par], 1e-6, None, ALU.add), wait=False)
                for par in both:
                    then[par].done()
                    then[par](nc.vector.reciprocal(flat[par], flat[par]), wait=False)
                for par in both:
                    then[par].done()
                    queries = inv[:, par, 1].rearrange("p (b n) h -> p b n h", b=BPC)
                    then[par](nc.vector.tensor_tensor(queries, queries, g.t("inv_weight_t")[:, None, :, None]
                                                      .to_broadcast([128, BPC, KB, HEADS_IN_BLOCK]), ALU.mult), wait=False)
                for par in both:
                    dve.wait_ge(k[par].x_out, 16 * (i + 1))
                    then[par].done()
                for n in range(2):
                    for par in both:
                        nc.vector.tensor_copy(len_t[:, par, n].rearrange("p n (h d) -> p (n h) d", d=DH1),
                                              inv[:, par, n].rearrange("p n h -> p (n h)")[:, :, None]
                                              .to_broadcast([128, RC * HEADS_IN_BLOCK, DH1])).then_inc(k[par].spread, 1)
                    for par in both:
                        dve.wait_ge(k[par].spread, 4 * i + 2 * n + 1)
                        nc.vector.transpose(sq2[:, par, n, :], len_t[:, par, n].rearrange("p n i -> p (n i)"))\
                            .then_inc(k[par].spread, 1)
                    for par in both:
                        dve.wait_ge(k[par].spread, 4 * i + 2 * n + 2)
                        nc.vector.tensor_tensor((g.kT, g.qT)[n][:, cols(i, par)], conv[:, par, n, :], sq2[:, par, n, :],
                                                ALU.mult).then_inc((k[par].k_done, k[par].q_done)[n], 1)
            add_experts(0)
            norm(0)
            with dve.Fori(0, LAST) as i:
                then = [Chain(dve, k[par].conv, CONVS, i) for par in both]
                convolve(then, i, 0)
                add_experts(i + 1)
                convolve(then, i, 1)
                norm(i + 1)
                convolve(then, i, 2)
                scale(i)
            then = [Chain(dve, k[par].conv, CONVS, LAST) for par in both]
            for n in range(3):
                convolve(then, LAST, n)
            scale(LAST)

        @block.gpsimd
        def _(pool):
            with pool.Fori(0, NCH // PAR) as i:
                for par in both:
                    pool.wait_ge(k[par].sig, i + 1)
                    nc.gpsimd.tensor_tensor(conv[:, par, 2, :], unit[:, par, :], conv[:, par, 2, :], ALU.mult)\
                        .then_inc(k[par].v_part, 1)
                for par in both:
                    pool.wait_ge(k[par].v_part, i + 1)
                    pool.wait_ge(k[par].rate, i + 1)
                    nc.gpsimd.tensor_tensor(g.vT[:, cols(i, par)], conv[:, par, 2, :], rate[:, par, :], ALU.mult)\
                        .then_inc(k[par].v_done, 1)
                for par in both:
                    pool.wait_ge(k[par].k_done, i + 1)
                    nc.gpsimd.tensor_tensor(g.bT[:, cols(i, par)], g.kT[:, cols(i, par)], rate[:, par, :], ALU.mult)\
                        .then_inc(k[par].b_done, 1)


def delta_phase(nc, dram, g):
    COLS = B * DH1
    HALF = DH1 // 2
    with Scope(nc, "delta") as s:
        wide = s.sb("wide", [128, 2, 3, GT, COLS])
        W = s.sb("W", [128, 2, COLS])
        A = s.sb("A", [128, COLS])
        sW = s.sb("sW", [128, 2, COLS])
        m1 = s.sb("m1", [128, 2, B, DH1 + 1])
        m2 = s.sb("m2", [128, 2, COLS])
        m3 = s.sb("m3", [128, 2, GT // 2, COLS])
        seen = s.sb("seen", [128, 1])
        u = s.sb("u", [128, 2, B])
        ps = [[s.ps(f"ps{a}{i}") for i in range(HALF)] for a in range(2)]
        k = s.sems("zeroed picked0 picked1 evac0 evac1 less_v scaled A m3_0 m3_1 out0 out1")
        half_b = [s.sems("product u m2 W", h) for h in range(2)]
        picked, evac, m3_done, out_done = ((k.picked0, k.picked1), (k.evac0, k.evac1), (k.m3_0, k.m3_1), (k.out0, k.out1))
        block = s.block()
        BODY = 2 * GT
        BODIES = T // BODY
        QUART = GT // 2
        src = (g.bT, g.kT, g.qT)

        def part(h):
            return slice(h * COLS // 2, (h + 1) * COLS // 2)

        def some(h):
            return slice(h * B // 2, (h + 1) * B // 2)

        def by_batch(x, first, count):
            return x[:, :].rearrange("p (b t) -> p b t", t=T)[:, :, bass.ds(first, count)]

        @block.tensor
        def _(pe):
            def pick(first, n):
                moving = by_batch(src[n % 3], first, GT)
                for d in range(DH1):
                    last = nc.tensor.matmul(ps[n % 2][d // 2][:, (d % 2) * COLS:(d % 2 + 1) * COLS],
                                            g.t(f"pick{d}"), moving, start=True, stop=True)
                last.then_inc(picked[n % 2], 1)
            for n in range(3):
                if n == 2:
                    pe.wait_ge(evac[0], 1)
                pick(0, n)
            def ahead(i, n):
                pe.wait_ge(evac[n % 2], 3 * i + (n - 2) // 2 + 1)
                pick(i * BODY + GT * (n // 3), n)
            with pe.Fori(0, BODIES - 1) as i:
                for n in range(3, 9):
                    ahead(i, n)
            for n in range(3, 6):
                ahead(BODIES - 1, n)

        @block.scalar
        def _(act):
            def spread(i, n, h, dd):
                to = wide[:, (n // 3) % 2, n % 3].rearrange("p t (b d) -> p d b t", d=DH1)
                return nc.scalar.activation(to[:, 2 * h + dd], ps[n % 2][h][:, dd * COLS:(dd + 1) * COLS]
                                            .rearrange("p (b t) -> p b t", t=GT), ACT.Copy)

            def less_value(i, t):
                if isinstance(i, int) and BODY * i + t == T:
                    return
                for h in range(2):
                    act.wait_ge(half_b[h].u, BODY * i + max(t - 1, 0))
                nc.scalar.activation(m1[:, t % 2, :, DH1], by_batch(g.vT, BODY * i + t, 1)[:, :, 0], ACT.Copy, scale=-1.0)\
                    .then_inc(k.less_v, 1)

            def body(i, halves_ahead):
                for half in range(2):
                    if half in halves_ahead:
                        for par in range(2):
                            act.wait_ge(half_b[par].m2, BODY * i + GT * half)
                            act.wait_ge(m3_done[par], GT * i + GT // 2 * half)
                    for t in range(GT):
                        if half in halves_ahead:
                            for piece in range(3 * t, 3 * t + 3):
                                n = 3 + 3 * half + piece // DH1
                                if piece % DH1 == 0:
                                    act.wait_ge(picked[n % 2], 3 * i + n // 2 + 1)
                                ins = spread(i, n, piece % DH1 // 2, piece % 2)
                                if piece % DH1 == DH1 - 1:
                                    ins.then_inc(evac[n % 2], 1)
                        step = BODY * i + GT * half + t
                        less_value(i, GT * half + t + 1)
                        for h in range(2):
                            act.wait_ge(half_b[h].W, step + 1)
                        act.wait_ge(k.A, BODY * i + max(GT * half + t - 1, 0))
                        nc.scalar.activation(sW[:, t % 2, :], W[:, (t + 1) % 2, :], ACT.Copy,
                                             scale=g.t("step")[:, bass.ds(step, 1)]).then_inc(k.scaled, 1)
            for n in range(3):
                act.wait_ge(picked[n % 2], n // 2 + 1)
                for piece in range(DH1):
                    last = spread(0, n, piece // 2, piece % 2)
                last.then_inc(evac[n % 2], 1)
            act.wait_ge(k.zeroed, 2)
            nc.scalar.activation(m1[:, 0, :, DH1], by_batch(g.vT, 0, 1)[:, :, 0], ACT.Copy, scale=-1.0).then_inc(k.less_v, 1)
            with act.Fori(0, BODIES - 1) as i:
                body(i, (0, 1))
            body(BODIES - 1, (0,))

        @block.vector
        def _(dve):
            nc.vector.memset(W[:, 0, :], 0.0).then_inc(k.zeroed, 1)
            nc.vector.memset(A[:, :], 0.0).then_inc(k.zeroed, 1)
            dve.wait_ge(k.zeroed, 2)
            pairs = lambda ap: ap.rearrange("p (b d) -> p b d", d=DH1)

            def outputs(i, quarter):
                nc.vector.tensor_reduce(by_batch(g.vT, i * BODY + QUART * quarter, QUART).rearrange("p b t -> p t b"),
                                        m3[:, quarter % 2, :, :].rearrange("p t (b d) -> p t b d", d=DH1), AX.X, ALU.add)\
                    .then_inc(out_done[quarter % 2], 1)

            def products(i, quarter):
                dve.wait_ge(m3_done[quarter % 2], GT * i + QUART * (quarter // 2 + 1))
            with dve.Fori(0, BODIES) as i:
                for half in range(2):
                    for a in range(2):
                        dve.wait_ge(evac[a], 3 * i + (3 if half else 2 - a))
                    for t in range(GT):
                        step = BODY * i + GT * half + t
                        quarter = (GT * half + t) // QUART
                        sums = t % QUART == QUART - 1 and quarter > 0
                        if sums:
                            products(i, quarter - 1)
                        for h in range(2):
                            if half or t:
                                dve.wait_ge(half_b[h].W, step)
                            nc.vector.tensor_tensor(m1[:, t % 2, some(h), 0:DH1], pairs(W[:, t % 2, part(h)]),
                                                    pairs(wide[:, half, 0, t, part(h)]), ALU.mult)\
                                .then_inc(half_b[h].product, 1)
                        if sums:
                            outputs(i, quarter - 1)
                        for h in range(2):
                            dve.wait_ge(k.less_v, step + 1)
                            dve.wait_ge(half_b[h].product, step + 1)
                            nc.vector.tensor_reduce(u[:, t % 2, some(h)], m1[:, t % 2, some(h), :], AX.X, ALU.add)\
                                .then_inc(half_b[h].u, 1)
                        for h in range(2):
                            dve.wait_ge(half_b[h].u, step + 1)
                            nc.vector.tensor_tensor(pairs(m2[:, t % 2, part(h)]), pairs(wide[:, half, 1, t, part(h)]),
                                                    u[:, t % 2, some(h), None].to_broadcast([128, B // 2, DH1]), ALU.mult)\
                                .then_inc(half_b[h].m2, 1)
                        for h in range(2):
                            dve.wait_ge(half_b[h].m2, step + 1)
                            dve.wait_ge(k.scaled, BODY * i + max(GT * half + t - 1, 0))
                            nc.vector.tensor_tensor(W[:, (t + 1) % 2, part(h)], W[:, t % 2, part(h)], m2[:, t % 2, part(h)],
                                                    ALU.subtract).then_inc(half_b[h].W, 1)
                for h in range(2):
                    dve.wait_ge(half_b[h].W, BODY * (i + 1))
                products(i, 3)
                nc.vector.tensor_copy(seen[:, :], m3[:, 1, 0, 0:1])
                outputs(i, 3)

        @block.gpsimd
        def _(pool):
            pool.wait_ge(k.zeroed, 2)
            with pool.Fori(0, BODIES) as i:
                for t in range(BODY):
                    step = BODY * i + t
                    par, place = t // QUART % 2, t % QUART
                    if place == 0:
                        pool.wait_ge(out_done[par], 2 * i + t // GT)
                    pool.wait_ge(k.scaled, step + 1)
                    if place:
                        pool.wait_ge(m3_done[par], GT * i + QUART * (t // GT) + place)
                    else:
                        pool.wait_ge(m3_done[1 - par], GT * i + QUART * ((t + QUART) // GT))
                    nc.gpsimd.tensor_tensor(A[:, :], A[:, :], sW[:, t % 2, :], ALU.add).then_inc(k.A, 1)
                    pool.wait_ge(k.A, step + 1)
                    nc.gpsimd.tensor_tensor(m3[:, par, place, :], A[:, :], wide[:, t // GT, 2, t % GT, :], ALU.mult)\
                        .then_inc(m3_done[par], 1)


def mix_phase(nc, dram, g):
    HEADS_IN_BLOCK = SLOT // DH1
    with Scope(nc, "mix") as s:
        w_out = s.sb("w_out", [128, D])
        router = s.sb("router", [128, E1])
        per_channel = s.sb("per_channel", [128, 3])
        sq = s.sb("sq", [128, PAR, 3, CH])
        ms = s.sb("ms", [128, PAR, RC, SLOT])
        scale = s.sb("scale", [128, PAR, CH])
        on = s.sb("on", [128, PAR, CH])
        mixed = s.sb("mixed", [128, PAR, CH])
        unit = s.sb("unit", [128, PAR, CH])
        h4 = s.sb("h4", [128, PAR, CH])
        xn = s.sb("xn", [128, PAR, CH])
        rows = s.sb("rows", [128, PAR, TILES, D])
        before = s.sb("before", [128, 128], BF16)
        ones = s.sb("ones", [128, 128], BF16)
        score = s.sb("score", [128, PAR, TILES, E1])
        top = s.sb("top", [128, PAR, TILES, 8])
        top_at = s.sb("top_at", [128, PAR, TILES, 8], U32)
        onehot = s.sb("onehot", [128, PAR, TILES, K1, E1])
        mask = s.sb("mask", [128, PAR, TILES, E1], BF16)
        less = s.sb("less", [128, PAR, TILES, E1])
        ex = s.sb("ex", [128, PAR, TILES, E1])
        total = s.sb("total", [128, PAR, TILES])
        place = s.sb("place", [128, PAR, TILES, E1])
        own = s.sb("own", [128, PAR, TILES, K1, E1])
        base = s.sb("base", [128, PAR, E1])
        seen = s.sb("seen", [128, PAR, 2])
        head_root = [Rstd(s, f"head{par}", RC * HEADS_IN_BLOCK, parts=False) for par in range(PAR)]
        rstd = [[Rstd(s, f"rstd{i}{par}") for par in range(PAR)] for i in range(2)]
        bank = [[s.ps(f"bank{i}{par}") for i in range(4)] for par in range(PAR)]
        heads, out_ps, mid, var, rms, logits, turned = ([bank[par][n] for par in range(PAR)] for n in (0, 1, 0, 1, 2, 3, 2))
        c = s.sems("w_in w_ready x_in consts counted")
        k = [s.sems("sq0 heads head_read head_steps on out_made mixed x_added centered squared var unit"
                    " modulated sq2 rms xn logits score route exp turned rows_read rows_out mask place_read skipped", par)
             for par in range(PAR)]
        block = s.block()
        STEPS = 2 * TILES + 9
        LAST = NCH // PAR - 1
        PLACED = 2 * TILES + 4
        cols = lambda i, par: bass.ds(i * (PAR * CH) + par * CH, CH)
        both = range(PAR)

        @block.sync
        def _(sp):
            for dst, name in ((w_out[:, :], "w1_out"), (router[:, :], "router"), (per_channel[:, :], "cols1")):
                sp.dma_start(dst, dram[name]).then_inc(c.w_in, 16)
            sp.dma_start(g.keptT[:, :], g.x_kept).then_inc(c.x_in, 16)
            with sp.Fori(0, NCH // PAR) as i:
                for par in both:
                    sp.wait_ge(k[par].rows_read, i + 1)
                    sp.dma_start(g.rows1[cols(i, par), :].rearrange("(r p) c -> p r c", p=128), rows[:, par])\
                        .then_inc(k[par].rows_out, 16)
            for par in both:
                sp.wait_ge(k[par].rows_out, 16 * (NCH // PAR))

        @block.tensor
        def _(pe):
            pe.wait_ge(c.w_ready, 1)
            pe.wait_ge(c.x_in, 16)
            pe.wait_ge(c.consts, 3)

            def heads_mean(i):
                for par in both:
                    pe.wait_ge(k[par].sq0, i + 1)
                    pe.wait_ge(k[par].unit, i)
                    nc.tensor.matmul(heads[par][:, :], g.t("same_head"), sq[:, par, 0, :], start=True, stop=True)\
                        .then_inc(k[par].heads, 1)

            def project_out(i):
                for par in both:
                    pe.wait_ge(k[par].on, i + 1)
                    nc.tensor.matmul(out_ps[par][:, :], w_out[:, :], on[:, par, :], start=True, stop=True)\
                        .then_inc(k[par].out_made, 1)

            def center(i):
                for par in both:
                    pe.wait_ge(k[par].x_added, i + 1)
                    nc.tensor.matmul(mid[par][:, :], g.t("center"), g.keptT[:, cols(i, par)], start=True, stop=True)\
                        .then_inc(k[par].centered, 1)

            def variance(i):
                for par in both:
                    pe.wait_ge(k[par].squared, i + 1)
                    nc.tensor.matmul(var[par][:, :], g.t("mean"), sq[:, par, 1, :], start=True, stop=True)\
                        .then_inc(k[par].var, 1)

            def mean_square(i):
                for par in both:
                    pe.wait_ge(k[par].sq2, i + 1)
                    pe.wait_ge(k[par].rows_read, i)
                    nc.tensor.matmul(rms[par][:, :], g.t("mean"), sq[:, par, 2, :], start=True, stop=True)\
                        .then_inc(k[par].rms, 1)

            def router_and_rows(i):
                for par in both:
                    pe.wait_ge(k[par].xn, i + 1)
                    pe.wait_ge(k[par].place_read, i)
                    for j in range(TILES):
                        last = nc.tensor.matmul(logits[par][:, j * E1:(j + 1) * E1], xn[:, par, 128 * j:128 * j + 128],
                                                router[:, :], start=True, stop=True)
                    last.then_inc(k[par].logits, 1)
                for par in both:
                    for j in range(TILES):
                        last = nc.tensor.transpose(turned[par][:, 128 * j:128 * j + 128], xn[:, par, 128 * j:128 * j + 128],
                                                   g.t("ident"))
                    last.then_inc(k[par].turned, 1)

            def count(i):
                for par in both:
                    pe.wait_ge(k[par].route, STEPS * i + PLACED)
                    for j in range(TILES + 1):
                        out = logits[par][:, 128 + j * E1:128 + (j + 1) * E1]
                        for n in range(min(j, TILES)):
                            last = nc.tensor.matmul(out, ones[:, :], mask[:, par, n, :], start=n == 0, stop=n == TILES - 1)
                        if j < TILES:
                            last = nc.tensor.matmul(out, before[:, :], mask[:, par, j, :], start=j == 0, stop=True)
                    last.then_inc(k[par].mask, 1)
            heads_mean(0)
            project_out(0)
            center(0)
            variance(0)
            heads_mean(1)
            mean_square(0)
            project_out(1)
            center(1)
            router_and_rows(0)
            with pe.Fori(0, LAST - 1) as i:
                variance(i + 1)
                count(i)
                heads_mean(i + 2)
                mean_square(i + 1)
                project_out(i + 2)
                center(i + 2)
                router_and_rows(i + 1)
            variance(LAST)
            count(LAST - 1)
            mean_square(LAST)
            router_and_rows(LAST)
            count(LAST)

        @block.scalar
        def _(act):
            act.wait_ge(c.w_in, 48)

            def head_squares(i):
                for par in both:
                    act.wait_ge(k[par].heads, i)
                for par in both:
                    nc.scalar.activation(sq[:, par, 0, :], g.vT[:, cols(i, par)], ACT.Square).then_inc(k[par].sq0, 1)

            def add_bias(i):
                for par in both:
                    act.wait_ge(k[par].out_made, i + 1)
                    nc.scalar.activation(mixed[:, par, :], out_ps[par][:, :], ACT.Identity, bias=per_channel[:, 1:2])\
                        .then_inc(k[par].mixed, 1)

            def square(i):
                for par in both:
                    act.wait_ge(k[par].centered, i + 1)
                    nc.scalar.activation(sq[:, par, 1, :], mid[par][:, :], ACT.Square).then_inc(k[par].squared, 1)

            def modulate(i):
                for par in both:
                    act.wait_ge(k[par].unit, i + 1)
                    act.wait_ge(k[par].skipped, i)
                    for j in range(BPC):
                        b = i * (PAR * BPC) + par * BPC + j
                        last = nc.scalar.activation(h4[:, par, j * T:(j + 1) * T], unit[:, par, j * T:(j + 1) * T],
                                                    ACT.Identity, scale=g.mod[:, 1, 4, bass.ds(b, 1)],
                                                    bias=g.mod[:, 1, 3, bass.ds(b, 1)])
                    last.then_inc(k[par].modulated, 1)
                for par in both:
                    act.wait_ge(k[par].modulated, i + 1)
                    nc.scalar.activation(sq[:, par, 2, :], h4[:, par, :], ACT.Square).then_inc(k[par].sq2, 1)

            def copy_out(i):
                for par in both:
                    act.wait_ge(k[par].logits, i + 1)
                    nc.scalar.activation(score[:, par].rearrange("p j e -> p (j e)"), logits[par][:, 0:TILES * E1], ACT.Copy)\
                        .then_inc(k[par].score, 1)
                for par in both:
                    act.wait_ge(k[par].turned, i + 1)
                    act.wait_ge(k[par].rows_out, 16 * i)
                    nc.scalar.activation(rows[:, par].rearrange("p j c -> p (j c)"), turned[par][:, :], ACT.Copy)\
                        .then_inc(k[par].rows_read, 1)

            def exps(i):
                for par in both:
                    act.wait_ge(k[par].route, STEPS * i + TILES + 1)
                    nc.scalar.activation(ex[:, par], less[:, par], ACT.Exp).then_inc(k[par].exp, 1)
            head_squares(0)
            add_bias(0)
            square(0)
            head_squares(1)
            modulate(0)
            add_bias(1)
            square(1)
            copy_out(0)
            with act.Fori(0, LAST - 1) as i:
                head_squares(i + 2)
                modulate(i + 1)
                exps(i)
                add_bias(i + 2)
                square(i + 2)
                copy_out(i + 1)
            modulate(LAST)
            exps(LAST - 1)
            copy_out(LAST)
            exps(LAST)

        @block.vector
        def _(dve):
            dve.wait_ge(c.w_in, 48)
            nc.vector.tensor_scalar(w_out[:, :], w_out[:, :], per_channel[:, 0:1], None, ALU.mult).then_inc(c.w_ready, 1)
            nc.vector.tensor_copy(before[:, :], g.t("before")).then_inc(c.consts, 1)
            nc.vector.tensor_copy(ones[:, :], g.t("ones")).then_inc(c.consts, 1)
            nc.vector.memset(base[:, 0, :], 0.0).then_inc(c.consts, 1)
            dve.wait_ge(c.consts, 3)
            dve.wait_ge(c.x_in, 16)
            tiles = lambda i, par: bass.ds(i * (PAR * TILES) + par * TILES, TILES)

            def norm_heads(i):
                for par in both:
                    dve.wait_ge(k[par].heads, i + 1)
                    nc.vector.transpose(ms[:, par].rearrange("p n i -> p (n i)"), heads[par][:, :]).then_inc(k[par].head_read, 1)
                then = [Chain(dve, k[par].head_steps, 3, i) for par in both]
                by_head = [ms[:, par].rearrange("p n (h d) -> p (n h) d", d=DH1) for par in both]
                for par in both:
                    dve.wait_ge(k[par].head_read, i + 1)
                    then[par](nc.vector.tensor_scalar(head_root[par].v[:, :], by_head[par][:, :, 0], 1.0 / DH1, RMS_EPS,
                                                      ALU.mult, ALU.add), wait=False)
                for par in both:
                    then[par].done()
                newton_roots(nc, dve, head_root, i)
                for par in both:
                    then[par](nc.vector.tensor_copy(by_head[par], head_root[par].y[:, :, None]
                                                    .to_broadcast([128, RC * HEADS_IN_BLOCK, DH1])), wait=False)
                for par in both:
                    then[par].done()
                    then[par](nc.vector.transpose(scale[:, par, :], ms[:, par].rearrange("p n i -> p (n i)")), wait=False)
                for par in both:
                    then[par].done()
                    nc.vector.tensor_tensor(on[:, par, :], g.vT[:, cols(i, par)], scale[:, par, :], ALU.mult)\
                        .then_inc(k[par].on, 1)

            def add_mixed(i):
                for par in both:
                    dve.wait_ge(k[par].mixed, i + 1)
                    for j in range(BPC):
                        b = i * (PAR * BPC) + par * BPC + j
                        x = g.keptT[:, bass.ds(b * T, T)]
                        last = nc.vector.scalar_tensor_tensor(x, mixed[:, par, j * T:(j + 1) * T],
                                                              g.mod[:, 1, 2, bass.ds(b, 1)], x, ALU.mult, ALU.add)
                    last.then_inc(k[par].x_added, 1)

            def layer_norm(i):
                run_roots(nc, dve, rstd[0], [var[par][:, :] for par in both], LN_EPS, i, [k[par].var for par in both])
                for par in both:
                    nc.vector.tensor_tensor(unit[:, par, :], mid[par][:, :], rstd[0][par].out[:, :], ALU.mult)\
                        .then_inc(k[par].unit, 1)

            def rms_root(i):
                run_roots(nc, dve, rstd[1], [rms[par][:, :] for par in both], RMS_EPS, i, [k[par].rms for par in both])

            def norm_and_skip(i):
                for par in both:
                    dve.wait_ge(k[par].turned, i)
                    nc.vector.scalar_tensor_tensor(xn[:, par, :], h4[:, par, :], per_channel[:, 2:3], rstd[1][par].out[:, :],
                                                   ALU.mult, ALU.mult).then_inc(k[par].xn, 1)
                for par in both:
                    dve.wait_ge(k[par].centered, i + 1)
                    for j in range(BPC):
                        b = i * (PAR * BPC) + par * BPC + j
                        x = g.keptT[:, bass.ds(b * T, T)]
                        last = nc.vector.scalar_tensor_tensor(x, h4[:, par, j * T:(j + 1) * T],
                                                              g.mod[:, 1, 5, bass.ds(b, 1)], x, ALU.mult, ALU.add)
                    last.then_inc(k[par].skipped, 1)

            def choose(i):
                then = [Chain(dve, k[par].route, STEPS, i) for par in both]
                for par in both:
                    dve.wait_ge(k[par].score, i + 1)
                    nc.vector.tensor_copy(seen[:, par, 0:1], score[:, par, 0, 0:1])
                    for j in range(TILES):
                        then[par](nc.vector.max(top[:, par, j, :], score[:, par, j, :]), wait=False)
                for par in both:
                    then[par].done()
                    then[par](nc.vector.tensor_tensor(less[:, par], top[:, par], top[:, par, :, 0:1]
                                                      .to_broadcast([128, TILES, E1]), ALU.subtract), wait=False)
                    for j in range(TILES):
                        then[par](nc.vector.max_index(top_at[:, par, j, :], top[:, par, j, :], score[:, par, j, :]), wait=False)
                for par in both:
                    then[par].done()
                    then[par](nc.vector.tensor_copy(g.chosen1[:, tiles(i, par), :], top_at[:, par, :, 0:K1]), wait=False)
                for par in both:
                    then[par].done()
                    then[par](nc.vector.tensor_tensor(onehot[:, par], g.t("iota")[:, None, None, 0:E1]
                                                      .to_broadcast([128, TILES, K1, E1]),
                                                      g.chosen1[:, tiles(i, par), :][:, :, :, None]
                                                      .to_broadcast([128, TILES, K1, E1]), ALU.is_equal), wait=False)
                for par in both:
                    then[par].done()
                    with nc.allow_low_precision(reason="sums of one-hot rows are 0 or 1"):
                        then[par](nc.vector.tensor_reduce(mask[:, par], onehot[:, par].rearrange("p j c e -> p j e c"),
                                                          AX.X, ALU.add), wait=False)
                return then

            def share(i, then):
                for par in both:
                    dve.wait_ge(k[par].exp, i + 1)
                    then[par](nc.vector.tensor_reduce(total[:, par], ex[:, par], AX.X, ALU.add), wait=False)
                for par in both:
                    then[par].done()
                    then[par](nc.vector.reciprocal(total[:, par], total[:, par]), wait=False)
                for par in both:
                    then[par].done()
                    then[par](nc.vector.tensor_tensor(g.gate1[:, tiles(i, par), :], ex[:, par, :, 0:K1], total[:, par, :, None]
                                                      .to_broadcast([128, TILES, K1]), ALU.mult), wait=False)

            def count(i, then):
                for par in both:
                    dve.wait_ge(k[par].mask, i + 1)
                    dve.wait_ge(c.counted, PAR * i + par)
                    then[par](nc.vector.tensor_tensor(place[:, par], logits[par][:, 128:128 + TILES * E1]
                                                      .rearrange("p (j e) -> p j e", e=E1),
                                                      base[:, par, None, :].to_broadcast([128, TILES, E1]), ALU.add), wait=False)
                    then[1 - par].done()
                    nc.vector.tensor_tensor(base[:, 1 - par, :], base[:, par, :],
                                            logits[par][:, 128 + TILES * E1:128 + (TILES + 1) * E1], ALU.add)\
                        .then_inc(c.counted, 1)
                for par in both:
                    dve.wait_ge(c.counted, PAR * i + par + 1)
                    then[par].done()
                    nc.vector.tensor_tensor(own[:, par], onehot[:, par], place[:, par, :, None, :]
                                            .to_broadcast([128, TILES, K1, E1]), ALU.mult).then_inc(k[par].place_read, 1)
                for par in both:
                    dve.wait_ge(k[par].place_read, i + 1)
                    then[par](nc.vector.tensor_reduce(g.rank1[:, tiles(i, par), :], own[:, par], AX.X, ALU.add))

            norm_heads(0)
            add_mixed(0)
            layer_norm(0)
            norm_heads(1)
            rms_root(0)
            add_mixed(1)
            norm_and_skip(0)
            with dve.Fori(0, LAST - 1) as i:
                then = choose(i)
                layer_norm(i + 1)
                count(i, then)
                norm_heads(i + 2)
                share(i, then)
                rms_root(i + 1)
                add_mixed(i + 2)
                norm_and_skip(i + 1)
            then = choose(LAST - 1)
            layer_norm(LAST)
            count(LAST - 1, then)
            share(LAST - 1, then)
            rms_root(LAST)
            norm_and_skip(LAST)
            then = choose(LAST)
            count(LAST, then)
            share(LAST, then)
            nc.vector.tensor_copy(g.count1[:, :], base[:, 0, :])


def dispatch_phase(nc, dram, g):
    CH1 = K1 * N // 128
    RING = 4
    I32 = mybir.dt.int32
    with Scope(nc, "disp") as s:
        ints = s.sb("ints", [128, E1], I32)
        tiles = s.sb("tiles", [128, E1])
        ends = s.sb("ends", [128, E1])
        start = s.sb("start", [128, E1])
        onehot = s.sb("onehot", [128, CH1, E1])
        slot = s.sb("slot", [128, CH1])
        slot_i = s.sb("slot_i", [128, CH1], I32)
        place_i = s.sb("place_i", [128, 2, CH1], I32)
        place = s.sb("place", [128, 2, CH1])
        by_place = s.sb("by_place", [128, RING, 128])
        by_tile = s.sb("by_tile", [128, RING, TILES1])
        held = s.sb("held", [128, TILES1])
        unused = s.sb("unused", [128, TILES1])
        spare = s.sb("spare", [128, TILES1])
        second = s.sb("second", [128, TILES1])
        dest = s.sb("dest", [128, TILES1])
        past = s.sb("past", [128, TILES1, E1])
        of_tile = s.sb("of_tile", [128, TILES1])
        zero = s.sb("zero", [128, TILES1])
        ps = s.ps("held_ps")
        k = s.sems("step zeroed opened closed")
        made = [s.sems("made added", n) for n in range(RING)]
        block = s.block()
        out = ps[:, 0:TILES1]

        @block.tensor
        def _(pe):
            pe.wait_ge(k.zeroed, 1)
            nc.tensor.matmul(out, zero[:, 0:128], zero[:, :], start=True, stop=False)
            with pe.Fori(0, CH1 // RING) as i:
                for n in range(RING):
                    pe.wait_ge(made[n].made, 2 * (i + 1))
                    nc.tensor.matmul(out, by_place[:, n, :], by_tile[:, n, :],
                                     start=False, stop=False).then_inc(made[n].added, 1)
            nc.tensor.matmul(out, zero[:, 0:128], zero[:, :], start=False, stop=True).then_inc(k.closed, 1)

        @block.vector
        def _(dve):
            nc.vector.memset(zero[:, :], 0.0).then_inc(k.zeroed, 1)
            STEPS = 30
            then = Chain(dve, k.step, STEPS, 0)
            then(nc.vector.tensor_scalar(ints[:, :], g.count1[:, :], 127.0, None, ALU.add))
            then(nc.vector.tensor_scalar(ints[:, :], ints[:, :], 7, None, ALU.arith_shift_right))
            then(nc.vector.tensor_copy(tiles[:, :], ints[:, :]))
            then(nc.vector.tensor_tensor_scan(ends[:, :], g.t("ones")[:, 0:E1], tiles[:, :], 0.0, ALU.mult, ALU.add))
            then(nc.vector.tensor_tensor(start[:, :], ends[:, :], tiles[:, :], ALU.subtract))
            chosen = g.chosen1[:, :, :].rearrange("p t c -> p (t c)")
            then(nc.vector.tensor_tensor(onehot[:, :, :], g.t("iota")[:, None, 0:E1].to_broadcast([128, CH1, E1]),
                                         chosen[:, :, None].to_broadcast([128, CH1, E1]), ALU.is_equal))
            then(nc.vector.tensor_tensor(onehot[:, :, :], onehot[:, :, :], start[:, None, :].to_broadcast([128, CH1, E1]),
                                         ALU.mult))
            then(nc.vector.tensor_reduce(slot[:, :], onehot[:, :, :], AX.X, ALU.add))
            then(nc.vector.scalar_tensor_tensor(slot[:, :], slot[:, :], 128.0, g.rank1[:, :, :].rearrange("p t c -> p (t c)"),
                                                ALU.mult, ALU.add))
            then(nc.vector.tensor_copy(slot_i[:, :], slot[:, :]))
            then(nc.vector.tensor_scalar(place_i[:, 0, :], slot_i[:, :], 127, None, ALU.bitwise_and), wait=False)
            then(nc.vector.tensor_scalar(place_i[:, 1, :], slot_i[:, :], 7, None, ALU.arith_shift_right))
            then(nc.vector.tensor_copy(place[:, :, :], place_i[:, :, :]))
            with dve.Fori(0, CH1 // RING) as i:
                for n in range(RING):
                    at = bass.ds(i * RING + n, 1)
                    dve.wait_ge(made[n].added, i)
                    nc.vector.tensor_scalar(by_place[:, n, :], g.t("iota")[:, 0:128], place[:, 0, at], None, ALU.is_equal)\
                        .then_inc(made[n].made, 1)
                    nc.vector.tensor_scalar(by_tile[:, n, :], g.t("iota"), place[:, 1, at], g.t("choice_row")[:, at],
                                            ALU.is_equal, ALU.mult).then_inc(made[n].made, 1)
            then(nc.vector.tensor_tensor(past[:, :, :], g.t("iota")[:, :, None].to_broadcast([128, TILES1, E1]),
                                         ends[:, None, :].to_broadcast([128, TILES1, E1]), ALU.is_ge))
            then(nc.vector.tensor_reduce(of_tile[:, :], past[:, :, :], AX.X, ALU.add))
            then(nc.vector.tensor_scalar(of_tile[:, :], of_tile[:, :], E1 - 1.0, None, ALU.min))
            then(nc.vector.tensor_copy(g.tile_expert[:, :], of_tile[:, :]))
            dve.wait_ge(k.closed, 1)
            then(nc.vector.tensor_copy(held[:, :], out))
            then(nc.vector.tensor_scalar(unused[:, :], held[:, :], 0.0, None, ALU.is_equal), wait=False)
            then(nc.vector.tensor_scalar(second[:, :], held[:, :], N + 128.0, float(N), ALU.is_ge, ALU.mult), wait=False)
            then(nc.vector.tensor_scalar(dest[:, :], held[:, :], -128.0, None, ALU.add))
            then(nc.vector.tensor_tensor(second[:, :], dest[:, :], second[:, :], ALU.subtract), wait=False)
            then(nc.vector.tensor_scalar(spare[:, :], g.t("iota"), 128.0, g.t("row_no"), ALU.mult, ALU.add))
            then(nc.vector.tensor_scalar(spare[:, :], spare[:, :], K1 * N + 128.0, None, ALU.add))
            then(nc.vector.tensor_tensor(unused[:, :], unused[:, :], spare[:, :], ALU.mult))
            then(nc.vector.tensor_tensor(dest[:, :], dest[:, :], unused[:, :], ALU.add), wait=False)
            then(nc.vector.tensor_scalar(second[:, :], second[:, :], 0.0, None, ALU.max))
            then(nc.vector.tensor_copy(g.slot_from[:, :], second[:, :]), wait=False)
            then(nc.vector.tensor_copy(g.slot_to[:, :], dest[:, :]))


def ffn_phase(nc, dram, g):
    P = len(HC)
    RING = 8
    BODIES = TILES1 // RING
    AHEAD = 5
    with Scope(nc, "ffn") as s:
        w_up = s.sb("w_up", [128, E1 * 2 * HID])
        w_down = s.sb("w_down", [128, E1 * P, D])
        idx = s.sb("idx", [128, RING, 2], U32)
        carry = s.sb("carry", [128, 2])
        carried = s.sb("carried", [128, 2, RING])
        xg = s.sb("xg", [128, RING, D])
        y = s.sb("y", [128, RING, D])
        xgT = s.sb("xgT", [128, 2, 128])
        sg = s.sb("sg", [128, 2, HID])
        hid = s.sb("hid", [128, 2, P * 128])
        hidT = s.sb("hidT", [128, 2, P * 128])
        x_ps, val_ps, gate_ps, h_ps = ([s.ps(f"{n}{par}") for par in range(2)] for n in ("x", "val", "gate", "h"))
        w = s.sems("w_in zeroed")
        ring = [s.sems("gathered scattered staged_in staged_out carried_in carried_out", n) for n in range(RING)]
        k = [s.sems("turned x_copied gate val sg hid h_turned h_copied down y", par) for par in range(2)]
        block = s.block()

        @block.sync
        def _(sp):
            sp.dma_start(w_up[:, :], dram["w_up"].rearrange("c e h -> c (e h)")).then_inc(w.w_in, 16)
            sp.dma_start(w_down[:, :, :], dram["w_down"].rearrange("h e p d -> h (e p) d")).then_inc(w.w_in, 16)

        def bodies(eng, step):
            for u in range(RING):
                step(0, u)
            with eng.Fori(1, BODIES - 1) as i:
                for u in range(RING):
                    step(i, u)
            for u in range(RING):
                step(BODIES - 1, u)

        def ahead(i, u, d):
            j, v = (u + d) // RING, (u + d) % RING
            if isinstance(i, int) and not 0 <= i + j < BODIES:
                return None
            return i + j, v

        def nth(i, u):
            return i * (RING // 2) + u // 2

        @block.gpsimd
        def _(pool):
            pool.wait_ge(w.zeroed, 4)

            def gather(i, u):
                pool.wait_ge(ring[u].carried_in, i)
                pool.wait_ge(ring[u].staged_in, i + 1)
                nc.gpsimd.tensor_tensor(carried[:, 0, u:u + 1], carry[:, 0:1], carry[:, 1:2], ALU.add)\
                    .then_inc(ring[u].carried_in, 1)
                nc.gpsimd.indirect_dma_start(xg[:, u, :], None, g.rows1, bass.IndirectOffsetOnAxis(idx[:, u, 0:1], 0))\
                    .then_inc(ring[u].gathered, 16)

            def scatter(i, u):
                pool.wait_ge(ring[u].staged_out, i + 1)
                pool.wait_ge(k[u % 2].y, nth(i, u) + 1)
                pool.wait_ge(ring[u].carried_out, i)
                nc.gpsimd.tensor_tensor(carried[:, 1, u:u + 1], carry[:, 0:1], carry[:, 1:2], ALU.add)\
                    .then_inc(ring[u].carried_out, 1)
                nc.gpsimd.indirect_dma_start(g.choice_rows, bass.IndirectOffsetOnAxis(idx[:, u, 1:2], 0), y[:, u, :], None)\
                    .then_inc(ring[u].scattered, 16)

            def step(i, u):
                if (at := ahead(i, u, AHEAD)):
                    gather(*at)
                if (at := ahead(i, u, -3)):
                    scatter(*at)
            for u in range(AHEAD):
                gather(0, u)
            bodies(pool, step)
            for u in range(RING - 3, RING):
                scatter(BODIES - 1, u)
            for u in range(RING):
                pool.wait_ge(ring[u].scattered, 16 * BODIES)

        @block.tensor
        def _(pe):
            pe.wait_ge(w.w_in, 32)
            pe.wait_ge(w.zeroed, 4)

            def expert(i, u):
                return nc.tensor.value_load(g.tile_expert[0:1, bass.ds(i * RING + u, 1)], min_val=0, max_val=E1 - 1)

            def turn(i, u):
                par = u % 2
                pe.wait_ge(ring[u].gathered, 16 * (i + 1))
                pe.wait_ge(k[par].x_copied, nth(i, u))
                nc.tensor.transpose(x_ps[par][:, 0:128], xg[:, u, :], g.t("ident")).then_inc(k[par].turned, 1)

            def up(e, i, u):
                par = u % 2
                pe.wait_ge(k[par].x_copied, nth(i, u) + 1)
                pe.wait_ge(k[par].sg, nth(i, u))
                nc.tensor.matmul(gate_ps[par][:, 0:HID], xgT[:, par, :], w_up[:, bass.ds(e * (2 * HID) + HID, HID)],
                                 start=True, stop=True).then_inc(k[par].gate, 1)
                pe.wait_ge(k[par].hid, nth(i, u))
                nc.tensor.matmul(val_ps[par][:, 0:HID], xgT[:, par, :], w_up[:, bass.ds(e * (2 * HID), HID)],
                                 start=True, stop=True).then_inc(k[par].val, 1)

            def turn_hidden(i, u):
                par = u % 2
                pe.wait_ge(k[par].hid, nth(i, u) + 1)
                pe.wait_ge(k[par].y, nth(i, u))
                for p in range(P):
                    last = nc.tensor.transpose(h_ps[par][:, 128 * p:128 * p + 128], hid[:, par, 128 * p:128 * p + 128],
                                               g.t("ident"))
                last.then_inc(k[par].h_turned, 1)

            def down(e, i, u):
                par = u % 2
                pe.wait_ge(k[par].h_copied, nth(i, u) + 1)
                for p in range(P):
                    last = nc.tensor.matmul(h_ps[par][:, P * 128:P * 128 + D], hidT[:, par, 128 * p:128 * p + 128],
                                            w_down[:, bass.ds(e * P + p, 1), :].rearrange("h o d -> h (o d)"),
                                            start=p == 0, stop=p == P - 1)
                last.then_inc(k[par].down, 1)

            def step(i, u):
                last = ahead(i, u, -2)
                e, last_e = expert(i, u), expert(*last) if last else None
                if (at := ahead(i, u, 2)):
                    turn(*at)
                up(e, i, u)
                if (at := ahead(i, u, -1)):
                    turn_hidden(*at)
                if last:
                    down(last_e, *last)
            turn(0, 0)
            turn(0, 1)
            bodies(pe, step)
            turn_hidden(BODIES - 1, RING - 1)
            for u in range(RING - 2, RING):
                down(expert(BODIES - 1, u), BODIES - 1, u)

        @block.scalar
        def _(act):
            def copy_x(i, u):
                par = u % 2
                act.wait_ge(k[par].turned, nth(i, u) + 1)
                act.wait_ge(k[par].val, nth(i, u))
                nc.scalar.activation(xgT[:, par, :], x_ps[par][:, 0:128], ACT.Copy).then_inc(k[par].x_copied, 1)

            def silu(i, u):
                par = u % 2
                act.wait_ge(k[par].gate, nth(i, u) + 1)
                act.wait_ge(k[par].hid, nth(i, u))
                nc.scalar.activation(sg[:, par, :], gate_ps[par][:, 0:HID], ACT.Silu).then_inc(k[par].sg, 1)

            def copy_hidden(i, u):
                par = u % 2
                act.wait_ge(k[par].h_turned, nth(i, u) + 1)
                act.wait_ge(k[par].down, nth(i, u))
                nc.scalar.activation(hidT[:, par, :], h_ps[par][:, 0:P * 128], ACT.Copy).then_inc(k[par].h_copied, 1)

            def step(i, u):
                silu(i, u)
                if (at := ahead(i, u, -1)):
                    copy_hidden(*at)
                if (at := ahead(i, u, 2)):
                    copy_x(*at)
            copy_x(0, 0)
            copy_x(0, 1)
            bodies(act, step)
            copy_hidden(BODIES - 1, RING - 1)

        @block.vector
        def _(dve):
            nc.vector.memset(hid[:, :, :], 0.0).then_inc(w.zeroed, 1)
            nc.vector.memset(carry[:, :], 0.0).then_inc(w.zeroed, 1)
            nc.vector.memset(sg[:, :, :], 0.0).then_inc(w.zeroed, 1)
            nc.vector.memset(y[:, :, :], 0.0).then_inc(w.zeroed, 1)
            dve.wait_ge(w.zeroed, 4)

            def stage_in(i, u):
                if (at := ahead(i, u, -RING)):
                    dve.wait_ge(k[u % 2].turned, nth(*at) + 1)
                    dve.wait_ge(ring[u].gathered, 16 * i)
                nc.vector.tensor_copy(idx[:, u, 0:1], g.slot_from[:, bass.ds(i * RING + u, 1)]).then_inc(ring[u].staged_in, 1)

            def hidden(i, u):
                par = u % 2
                dve.wait_ge(k[par].sg, nth(i, u) + 1)
                dve.wait_ge(k[par].val, nth(i, u) + 1)
                dve.wait_ge(k[par].h_turned, nth(i, u))
                nc.vector.tensor_tensor(hid[:, par, 0:HID], sg[:, par, :], val_ps[par][:, 0:HID], ALU.mult)\
                    .then_inc(k[par].hid, 1)

            def output(i, u):
                par = u % 2
                dve.wait_ge(ring[u].scattered, 16 * i)
                nc.vector.tensor_copy(idx[:, u, 1:2], g.slot_to[:, bass.ds(i * RING + u, 1)]).then_inc(ring[u].staged_out, 1)
                dve.wait_ge(k[par].down, nth(i, u) + 1)
                nc.vector.tensor_copy(y[:, u, :], h_ps[par][:, P * 128:P * 128 + D]).then_inc(k[par].y, 1)

            def step(i, u):
                hidden(i, u)
                if (at := ahead(i, u, AHEAD + 1)):
                    stage_in(*at)
                if (at := ahead(i, u, -2)):
                    output(*at)
            for u in range(AHEAD + 1):
                stage_in(0, u)
            bodies(dve, step)
            output(BODIES - 1, RING - 2)
            output(BODIES - 1, RING - 1)


def combine_phase(nc, dram, g, out):
    with Scope(nc, "comb") as s:
        rows = s.sb("rows", [128, PAR, K1, TILES, D])
        part = s.sb("part", [128, PAR, K1, TILES, D])
        mixed = s.sb("mixed", [128, PAR, TILES, D])
        y = s.sb("y", [128, PAR, CH])
        done = s.sb("done", [128, PAR, TILES, D])
        by_channel = [s.ps(f"by_channel{par}") for par in range(PAR)]
        by_row = [s.ps(f"by_row{par}") for par in range(PAR)]
        k = [s.sems("in0 in1 part0 part1 mixed turned y back copied out", par) for par in range(PAR)]
        block = s.block()
        out_rows = out.rearrange("b t c -> (b t) c")
        cols = lambda i, par, first=0: bass.ds(i * (PAR * CH) + par * CH + first, CH)
        both = range(PAR)
        by_tile = lambda ap: ap.rearrange("(r p) c -> p r c", p=128)

        @block.sync
        def _(sp):
            with sp.Fori(0, NCH // PAR) as i:
                for par in both:
                    sp.wait_ge(k[par].part0, i)
                    sp.wait_ge(k[par].part1, i)
                    for c, sem in enumerate((k[par].in0, k[par].in1)):
                        sp.dma_start(rows[:, par, c], by_tile(g.choice_rows[cols(i, par, c * N), :])).then_inc(sem, 16)

        @block.tensor
        def _(pe):
            with pe.Fori(0, NCH // PAR) as i:
                for par in both:
                    pe.wait_ge(k[par].mixed, i + 1)
                    pe.wait_ge(k[par].y, i)
                    for r in range(TILES):
                        last = nc.tensor.transpose(by_channel[par][:, 128 * r:128 * r + 128], mixed[:, par, r, :], g.t("ident"))
                    last.then_inc(k[par].turned, 1)
                for par in both:
                    pe.wait_ge(k[par].y, i + 1)
                    pe.wait_ge(k[par].copied, i)
                    for r in range(TILES):
                        last = nc.tensor.transpose(by_row[par][:, 128 * r:128 * r + 128], y[:, par, 128 * r:128 * r + 128],
                                                   g.t("ident"))
                    last.then_inc(k[par].back, 1)

        @block.scalar
        def _(act):
            with act.Fori(0, NCH // PAR) as i:
                for par in both:
                    act.wait_ge(k[par].back, i + 1)
                    act.wait_ge(k[par].out, 16 * i)
                    nc.scalar.activation(done[:, par].rearrange("p r c -> p (r c)"), by_row[par][:, :], ACT.Copy)\
                        .then_inc(k[par].copied, 1)
                for par in both:
                    act.wait_ge(k[par].copied, i + 1)
                    act.dma_start(by_tile(out_rows[cols(i, par), :]), done[:, par]).then_inc(k[par].out, 16)
            for par in both:
                act.wait_ge(k[par].out, 16 * (NCH // PAR))

        @block.vector
        def _(dve):
            with dve.Fori(0, NCH // PAR) as i:
                for c in range(K1):
                    for par in both:
                        dve.wait_ge((k[par].in0, k[par].in1)[c], 16 * (i + 1))
                        share = g.gate1[:, bass.ds(i * (PAR * TILES) + par * TILES, TILES), c:c + 1]
                        nc.vector.tensor_tensor(part[:, par, c], rows[:, par, c], share.to_broadcast([128, TILES, D]), ALU.mult)\
                            .then_inc((k[par].part0, k[par].part1)[c], 1)
                for par in both:
                    dve.wait_ge(k[par].part0, i + 1)
                    dve.wait_ge(k[par].part1, i + 1)
                    dve.wait_ge(k[par].turned, i)
                    nc.vector.tensor_tensor(mixed[:, par], part[:, par, 0], part[:, par, 1], ALU.add).then_inc(k[par].mixed, 1)
                for par in both:
                    dve.wait_ge(k[par].turned, i + 1)
                    dve.wait_ge(k[par].back, i)
                    for j in range(BPC):
                        b = i * (PAR * BPC) + par * BPC + j
                        last = nc.vector.scalar_tensor_tensor(y[:, par, j * T:(j + 1) * T], by_channel[par][:, j * T:(j + 1) * T],
                                                              g.mod[:, 1, 5, bass.ds(b, 1)], g.keptT[:, bass.ds(b * T, T)],
                                                              ALU.mult, ALU.add)
                    last.then_inc(k[par].y, 1)


def launch_arrays(inputs):
    a = {k: np.asarray(v) for k, v in inputs.items()}
    out = {}
    f, bf = constants()
    out["tables"] = np.concatenate(list(f.values()), 1)
    out["tables_bf"] = np.concatenate(list(bf.values()), 1)
    out["x"] = a["L0_attn_x"]
    for layer in range(2):
        out[f"c{layer}"] = a[f"L{layer}_c"].T
        out[f"wmod{layer}"] = a[f"L{layer}_wmod"]
    out["ln"] = np.stack([a["L0_attn_ln_g"], a["L0_attn_ln_b"]], 1)

    def slots(w):
        z = np.zeros((H0, SLOT) + w.shape[1:], w.dtype)
        z[:, :DH0] = w.reshape((H0, DH0) + w.shape[1:])
        return z.reshape((GROUPS, PER * SLOT) + w.shape[1:])
    half = DH0 // 2
    turn = np.concatenate([np.arange(half, DH0), np.arange(half)])
    turned = lambda w: w.reshape(H0, DH0, D)[:, turn].reshape(D, D)
    wq, wk, wv = (a[f"L0_attn_W{n}"] for n in "qkv")
    out["w_attn"] = np.stack([slots(w).transpose(2, 0, 1) for w in (wq, turned(wq), wk, turned(wk), wv)], 1)
    out["wo"] = slots(a["L0_attn_Wo"].T).transpose(1, 0, 2)
    rows = np.zeros((GROUPS, PER, SLOT, PER, SLOT), np.float32)
    wide = np.zeros((GROUPS, PER, SLOT, PER, SLOT), np.float32)
    for gr in range(GROUPS):
        for h in range(PER):
            rows[gr, h, :GEO_D, h, gr] = a["L0_attn_head_dirs"][gr * PER + h]
            wide[gr, h, :GEO_D, h, :] = a["L0_attn_head_dirs"][gr * PER + h][:, None]
    out["dirs"] = np.stack([rows, wide]).reshape(2, GROUPS, 128, 128).transpose(2, 0, 1, 3)
    out["hs"] = np.repeat(a["L0_attn_head_scales"].reshape(GROUPS, PER), SLOT, 1).T
    out["gate_w"] = a["L0_ffn_gate_w"].T
    out["gate_bias"] = a["L0_ffn_bias"][None, :]
    out["sw13"] = np.stack([a["L0_ffn_sw1"].T, a["L0_ffn_sw3"].T], 1)
    out["sw2"] = a["L0_ffn_sw2"].T
    out["w13"] = np.concatenate([a["L0_ffn_W1"], a["L0_ffn_W3"]], 2).transpose(1, 0, 2)
    out["w2"] = a["L0_ffn_W2"].transpose(1, 0, 2)
    out["w1_qkv"] = np.stack([a[f"L1_attn_W{n}"].T for n in "kqv"], 1)
    out["w_beta"] = a["L1_attn_Wbeta"].T
    out["b1"] = np.stack([a[f"L1_attn_b{n}"] for n in "kqv"] + [np.repeat(a["L1_attn_bbeta"], DH1)], 1)
    out["taps"] = np.stack([a[f"L1_attn_conv_{n}"] for n in "kqv"], 1)
    out["w1_out"] = a["L1_attn_Wout"].T
    out["cols1"] = np.stack([np.tile(a["L1_attn_rms_w"], H1), a["L1_attn_bout"], a["L1_ffn_norm_scale"]], 1)
    out["router"] = a["L1_ffn_w_router"].T
    out["w_up"] = a["L1_ffn_w_up"].transpose(2, 0, 1)
    down = np.zeros((E1, len(HC) * 128, D), np.float32)
    down[:, :HID] = a["L1_ffn_w_down"].transpose(0, 2, 1)
    out["w_down"] = down.reshape(E1, len(HC), 128, D).transpose(2, 0, 1, 3)
    return {k: np.ascontiguousarray(v) for k, v in out.items()}


def build(nc, dram, out):
    f, bf = constants()
    cols, nf = table_columns(f)
    cols_bf, nb = table_columns(bf)
    with ExitStack() as ctx:
        g = Shared()
        g.tab = ctx.enter_context(nc.sbuf_tensor("tables_sb", [128, nf], F32))
        g.tab_bf = ctx.enter_context(nc.sbuf_tensor("tables_bf_sb", [128, nb], BF16))

        def t(name):
            if name in cols:
                return g.tab[:, cols[name][0]:cols[name][1]]
            return g.tab_bf[:, cols_bf[name][0]:cols_bf[name][1]]
        g.t = t
        g.mod = ctx.enter_context(nc.sbuf_tensor("mod", [128, 2, 6, B], F32))
        g.xT = ctx.enter_context(nc.sbuf_tensor("xT", [128, N], F32))
        g.xnT = ctx.enter_context(nc.sbuf_tensor("xnT", [128, N], F32))
        g.slot_token = ctx.enter_context(nc.sbuf_tensor("slot_token", [128, E0], U32))
        g.rows = nc.dram_tensor("rows", (N + CAP, ROW), F32, kind="Internal").ap()
        g.acc = nc.dram_tensor("acc", (N + CAP, D), F32, kind="Internal").ap()
        g.x_kept = nc.dram_tensor("x_kept", (128, N), F32, kind="Internal").ap()
        setup_phase(nc, dram, g)
        load_phase(nc, dram, g)
        attention_phase(nc, dram, g)
        route_phase(nc, dram, g)
        experts_phase(nc, dram, g)
        g.kT, g.vT = g.xT, g.xnT
        g.qT = ctx.enter_context(nc.sbuf_tensor("qT", [128, N], F32))
        rates = ctx.enter_context(ExitStack())
        g.bT = rates.enter_context(nc.sbuf_tensor("bT", [128, N], F32))
        project_phase(nc, dram, g)
        delta_phase(nc, dram, g)
        rates.close()
        g.keptT = g.xT
        tiles = (128, N // 128, K1)
        g.chosen1, g.gate1, g.rank1 = (ctx.enter_context(nc.sbuf_tensor(n, tiles, F32)) for n in ("chosen1", "gate1", "rank1"))
        g.count1 = ctx.enter_context(nc.sbuf_tensor("count1", [128, E1], F32))
        g.slot_from = ctx.enter_context(nc.sbuf_tensor("slot_from", [128, TILES1], U32))
        g.slot_to = ctx.enter_context(nc.sbuf_tensor("slot_to", [128, TILES1], U32))
        g.tile_expert = ctx.enter_context(nc.sbuf_tensor("tile_expert", [128, TILES1], mybir.dt.int32))
        g.rows1 = nc.dram_tensor("rows1", (N, D), F32, kind="Internal").ap()
        g.choice_rows = nc.dram_tensor("choice_rows", (K1 * N + 128 * TILES1, D), F32, kind="Internal").ap()
        mix_phase(nc, dram, g)
        dispatch_phase(nc, dram, g)
        ffn_phase(nc, dram, g)
        combine_phase(nc, dram, g, out)


def kernel(**inputs):
    import concourse.bacc as bacc
    from concourse.bass_utils import run_bass_kernel_spmd

    nc = bacc.Bacc("TRN2", target_bir_lowering=False, num_devices=1)
    arrays = {f"in_{name}": a for name, a in launch_arrays(inputs).items()}
    dram = {name[3:]: nc.dram_tensor(name, a.shape, mybir.dt.from_np(a.dtype), kind="ExternalInput").ap()
            for name, a in arrays.items()}
    out = nc.dram_tensor("out", (B, T, D), F32, kind="ExternalOutput").ap()
    build(nc, dram, out)
    return run_bass_kernel_spmd(nc, [arrays], core_ids=[0]).results[0]["out"]
```
